# Optimizing a Trainium2 kernel written in Bass

```python
import numpy as np
import jax
import jax.numpy as jnp

def _softmax(x, axis=-1):
    return jax.nn.softmax(x, axis=axis)

def _gelu(x):
    return jax.nn.gelu(x, approximate=True)

def _silu(x):
    return jax.nn.silu(x)

def _sigmoid(x):
    return jax.nn.sigmoid(x)

def _layernorm(x, axis=-1, eps=1e-05):
    m = jnp.mean(x, axis=axis, keepdims=True)
    v = jnp.var(x, axis=axis, keepdims=True)
    return (x - m) / jnp.sqrt(v + eps)

def _scatter_add(tgt, idx, src, axis=0):
    return tgt.at[idx].add(src)

def _segment_sum(src, seg, n):
    return jax.ops.segment_sum(src, seg, n)
kernel_name = 'mk_flamingo_gated_d4_seqx_r8_e79735'

def setup_inputs(seed: int=0):
    np.random.seed(seed)
    _w = jnp.asarray

    def _rec_inputs():
        import jax
        import jax.numpy as jnp
        _rk = jax.random.key(seed)
        x = 7.22e-05 + 1 * jax.random.normal(jax.random.fold_in(_rk, 1), (4, 256, 128), jnp.float32)
        _lenS = 256 - jax.random.randint(jax.random.fold_in(_rk, 7), (4,), 0, max(1, 256 // 4) + 1, jnp.int32)
        _lenS2 = 256 - jax.random.randint(jax.random.fold_in(_rk, 8), (4,), 0, max(1, 256 // 4) + 1, jnp.int32)
        _ctx_1024P = jax.random.normal(jax.random.fold_in(_rk, 11), (4, 16, 128), jnp.float32)
        _ctx_1024c = jax.random.dirichlet(jax.random.fold_in(_rk, 511), 0.3 * jnp.ones((16,), jnp.float32), (4, 256))
        _ctx_1024t = jnp.einsum('bsk,bkd->bsd', _ctx_1024c, _ctx_1024P)
        _ctx_1024t = _ctx_1024t * jax.lax.rsqrt(jnp.mean(jnp.square(_ctx_1024t)) + 1e-12) * 0.953939
        ctx_1024 = 4.13588e-05 + 0.999923 * (_ctx_1024t + 0.3 * jax.random.normal(jax.random.fold_in(_rk, 611), (4, 256, 128), jnp.float32))
        _g = jax.random.normal(jax.random.fold_in(_rk, 9001), (2, 4), jnp.float32)
        _g = jnp.sign(_g) * jnp.maximum(jnp.abs(_g), 1.0) + (_g == 0) * 1.0
        g_xattn = _g[0]
        g_ffn = _g[1]
        return (x, ctx_1024, g_xattn, g_ffn)
    x, ctx_1024, g_xattn, g_ffn = _rec_inputs()

    def _L0_xattn_setup():
        import jax, jax.numpy as jnp
        import numpy as np
        EMBED = 128
        HEADS = 16
        HEAD_DIM = EMBED // HEADS
        key = jax.random.key(seed)
        ks = jax.random.split(key, 7)
        B, Sd, Se = (4, 256, 256)
        dec = jax.random.normal(ks[0], (B, Sd, EMBED), dtype=jnp.float32)
        enc = jax.random.normal(ks[1], (B, Se, EMBED), dtype=jnp.float32)
        scale = 1.0 / np.sqrt(EMBED)
        W_q = jax.random.normal(ks[2], (EMBED, EMBED), dtype=jnp.float32) * scale
        W_k = jax.random.normal(ks[3], (EMBED, EMBED), dtype=jnp.float32) * scale
        W_v = jax.random.normal(ks[4], (EMBED, EMBED), dtype=jnp.float32) * scale
        W_o = jax.random.normal(ks[5], (EMBED, EMBED), dtype=jnp.float32) * scale
        b_o = jax.random.normal(ks[6], (EMBED,), dtype=jnp.float32) * 0.01
        return {'decoder_input': dec, 'encoder_output': enc, 'W_q': W_q, 'W_k': W_k, 'W_v': W_v, 'W_o': W_o, 'b_o': b_o}
    _L0_xattn_all = _L0_xattn_setup()
    _L0_xattn_in = {k: v for k, v in _L0_xattn_all.items() if k in ('W_q', 'W_k', 'W_v', 'W_o', 'b_o')}
    del _L0_xattn_all

    def _L0_ffn_setup():
        import jax, jax.numpy as jnp
        import numpy as np
        key = jax.random.key(seed)
        k_x, k_W, k_b, k_ids, k_w = jax.random.split(key, 5)
        N_ADAPTERS, D_OUT, D_IN = (32, 128, 128)
        B, S = (2, 256)
        K = 8
        x = jax.random.normal(k_x, (B, S, D_IN), dtype=jnp.float32)
        W = jax.random.normal(k_W, (N_ADAPTERS, D_OUT, D_IN), dtype=jnp.float32)
        b = jax.random.normal(k_b, (N_ADAPTERS, D_OUT), dtype=jnp.float32)
        ids = jax.random.randint(k_ids, (K,), 0, N_ADAPTERS, dtype=jnp.int64)
        weights = jax.random.uniform(k_w, (K,), dtype=jnp.float32)
        return {'x': x, 'W': W, 'b': b, 'ids': ids, 'weights': weights}
    _L0_ffn_all = _L0_ffn_setup()
    _L0_ffn_in = {k: v for k, v in _L0_ffn_all.items() if k in ('W', 'b', 'ids', 'weights')}
    del _L0_ffn_all

    def _L1_xattn_setup():
        import jax, jax.numpy as jnp
        import numpy as np
        from jax import lax
        BIG = jnp.float32(1e+30)

        def _pairwise_euclidean(a, b):
            aa = jnp.sum(a * a, axis=-1)[:, None]
            bb = jnp.sum(b * b, axis=-1)[None, :]
            ab = a @ b.T
            return jnp.sqrt(jnp.maximum(aa + bb - 2.0 * ab, 0.0))

        def _dtw_cost(D):
            row0 = jnp.cumsum(D[0])

            def row_step(prev_row, d_row):
                first = d_row[0] + prev_row[0]

                def col_step(left, inp):
                    d_ij, up, diag = inp
                    r = d_ij + jnp.minimum(jnp.minimum(up, left), diag)
                    return (r, r)
                _, rest = lax.scan(col_step, first, (d_row[1:], prev_row[1:], prev_row[:-1]))
                row = jnp.concatenate([first[None], rest])
                return (row, row)
            _, rows = lax.scan(row_step, row0, D[1:])
            return jnp.concatenate([row0[None], rows], axis=0)

        def _backtrack(R, T1, T2):
            L = T1 + T2 - 1

            def step(carry, _):
                i, j, done = carry
                valid = jnp.logical_not(done)
                cd = jnp.where((i > 0) & (j > 0), R[jnp.maximum(i - 1, 0), jnp.maximum(j - 1, 0)], BIG)
                cu = jnp.where(i > 0, R[jnp.maximum(i - 1, 0), j], BIG)
                cl = jnp.where(j > 0, R[i, jnp.maximum(j - 1, 0)], BIG)
                choice = jnp.argmin(jnp.stack([cd, cu, cl]))
                ni = jnp.where(choice <= 1, i - 1, i)
                nj = jnp.where((choice == 0) | (choice == 2), j - 1, j)
                at_origin = (i == 0) & (j == 0)
                ni = jnp.where(at_origin, 0, ni)
                nj = jnp.where(at_origin, 0, nj)
                return ((ni, nj, done | at_origin), (i, j, valid))
            init = (jnp.int32(T1 - 1), jnp.int32(T2 - 1), jnp.bool_(False))
            _, (i_idx, j_idx, valid) = lax.scan(step, init, None, length=L)
            return (i_idx, j_idx, valid)

        def _align_one(small, large):
            T_small, d = small.shape
            T_large = large.shape[0]
            D = _pairwise_euclidean(small, large)
            R = _dtw_cost(D)
            i_idx, j_idx, valid = _backtrack(R, T_small, T_large)
            contrib = small[i_idx] * valid[:, None].astype(small.dtype)
            expanded = jnp.zeros((T_large, d), dtype=small.dtype).at[j_idx].add(contrib)
            return expanded
        key = jax.random.key(seed)
        k1, k2 = jax.random.split(key)
        teacher = jax.random.normal(k1, (16, 50, 128), dtype=jnp.float32)
        student = jax.random.normal(k2, (16, 75, 128), dtype=jnp.float32)
        return {'teacher_features': teacher, 'student_features': student}
    _L1_xattn_all = _L1_xattn_setup()
    _L1_xattn_in = {k: v for k, v in _L1_xattn_all.items() if k in ()}
    del _L1_xattn_all

    def _L1_ffn_setup():
        import jax, jax.numpy as jnp
        import numpy as np
        HIDDEN = 128
        NUM_EXPERTS = 8
        TOP_K = 2
        B, S = (2, 256)
        key = jax.random.key(seed)
        k1, k2, k3, k4, k5 = jax.random.split(key, 5)
        d, dff, E = (HIDDEN, 4 * HIDDEN, NUM_EXPERTS)
        x = jax.random.normal(k1, (B, S, d), dtype=jnp.float32)
        W1 = jax.random.normal(k2, (E, d, dff), dtype=jnp.float32) * (1.0 / np.sqrt(d))
        b1 = jax.random.normal(k3, (E, dff), dtype=jnp.float32) * 0.01
        W2 = jax.random.normal(k4, (E, dff, d), dtype=jnp.float32) * (1.0 / np.sqrt(dff))
        b2 = jax.random.normal(k5, (E, d), dtype=jnp.float32) * 0.01
        return {'x': x, 'W1': W1, 'b1': b1, 'W2': W2, 'b2': b2}
    _L1_ffn_all = _L1_ffn_setup()
    _L1_ffn_in = {k: v for k, v in _L1_ffn_all.items() if k in ('W1', 'b1', 'W2', 'b2')}
    del _L1_ffn_all

    def _L2_xattn_setup():
        import jax, jax.numpy as jnp
        import numpy as np
        import math
        NHEADS = 16
        CAUSAL = True
        NEG_INF = -1e+18
        key = jax.random.key(seed)
        kq, kk, kv = jax.random.split(key, 3)
        B, S, D = (4, 1024, 128)
        q = jax.random.normal(kq, (B, S, D), dtype=jnp.float32)
        k = jax.random.normal(kk, (B, S, D), dtype=jnp.float32)
        v = jax.random.normal(kv, (B, S, D), dtype=jnp.float32)
        return {'q': q, 'k': k, 'v': v}
    _L2_xattn_all = _L2_xattn_setup()
    _L2_xattn_in = {k: v for k, v in _L2_xattn_all.items() if k in ()}
    del _L2_xattn_all

    def _L2_ffn_setup():
        import jax, jax.numpy as jnp
        import numpy as np
        B, T, C, E = (4, 256, 128, 8)
        key = jax.random.key(seed)
        k_x, k_wr, k_we = jax.random.split(key, 3)
        x = jax.random.normal(k_x, (B, T, C), dtype=jnp.float32)
        Wr = jax.random.normal(k_wr, (E, C), dtype=jnp.float32) * 0.05
        br = jnp.zeros((E,), dtype=jnp.float32)
        We = jax.random.normal(k_we, (E, C, C), dtype=jnp.float32) * (1.0 / np.sqrt(C))
        be = jnp.zeros((E, C), dtype=jnp.float32)
        return {'x': x, 'Wr': Wr, 'br': br, 'We': We, 'be': be}
    _L2_ffn_all = _L2_ffn_setup()
    _L2_ffn_in = {k: v for k, v in _L2_ffn_all.items() if k in ('Wr', 'br', 'We', 'be')}
    del _L2_ffn_all

    def _L3_xattn_setup():
        import jax, jax.numpy as jnp
        import numpy as np
        THETA = 10000.0
        SCALE_BASE = 512.0
        GAMMA = 0.96875

        def _dup_interleave(x):
            return jnp.repeat(x, 2, axis=-1)

        def _xpos(x, offset, inverse_scale):
            L, d = (x.shape[-2], x.shape[-1])
            half = d // 2
            base = (jnp.arange(0, d, 2, dtype=x.dtype) + 0.4 * d) / (1.4 * d)
            pos = jnp.arange(offset, offset + L, dtype=x.dtype)
            scale = base[None, :] ** (pos[:, None] / SCALE_BASE)
            freqs = 1.0 / THETA ** (jnp.arange(half, dtype=x.dtype) / half)
            sin_in = pos[:, None] * freqs[None, :]
            if inverse_scale:
                scale = 1.0 / scale
            sin = _dup_interleave(jnp.sin(sin_in) * scale)
            cos = _dup_interleave(jnp.cos(sin_in) * scale)
            rot = jnp.stack((-x[..., 1::2], x[..., ::2]), axis=-1).reshape(x.shape)
            return x * cos + rot * sin

        def _decay_mask(L, gamma, dtype):
            u = jnp.arange(L, dtype=dtype)[:, None]
            v = jnp.arange(L, dtype=dtype)[None, :]
            return jnp.where(u >= v, gamma ** (u - v), jnp.zeros((), dtype))
        key = jax.random.key(seed)
        ks = jax.random.split(key, 6)
        B, L, E = (2, 512, 128)
        query = jax.random.normal(ks[0], (B, L, E), jnp.float32)
        k_in = jax.random.normal(ks[1], (B, L, E), jnp.float32)
        value = jax.random.normal(ks[2], (B, L, E), jnp.float32)
        s = 1.0 / np.sqrt(E)
        Wq = jax.random.normal(ks[3], (E, E), jnp.float32) * s
        Wk = jax.random.normal(ks[4], (E, E), jnp.float32) * s
        Wv = jax.random.normal(ks[5], (E, E), jnp.float32) * s
        return {'query': query, 'key': k_in, 'value': value, 'Wq': Wq, 'Wk': Wk, 'Wv': Wv}
    _L3_xattn_all = _L3_xattn_setup()
    _L3_xattn_in = {k: v for k, v in _L3_xattn_all.items() if k in ('Wq', 'Wk', 'Wv')}
    del _L3_xattn_all

    def _L3_ffn_setup():
        import jax, jax.numpy as jnp
        import numpy as np

        def _binarize(w):
            alpha = jax.lax.stop_gradient(jnp.mean(jnp.abs(w), axis=1, keepdims=True))
            bw = alpha * jnp.sign(w)
            return w + jax.lax.stop_gradient(bw - w)
        key = jax.random.key(seed)
        k1, k2, k3, k4, k5 = jax.random.split(key, 5)
        D, H = (128, 512)
        x = jax.random.normal(k1, (64, 196, D), dtype=jnp.float32)
        w1 = jax.random.normal(k2, (H, D), dtype=jnp.float32) * 0.02
        b1 = jax.random.normal(k3, (H,), dtype=jnp.float32) * 0.02
        w2 = jax.random.normal(k4, (D, H), dtype=jnp.float32) * 0.02
        b2 = jax.random.normal(k5, (D,), dtype=jnp.float32) * 0.02
        return {'x': x, 'w1': w1, 'b1': b1, 'w2': w2, 'b2': b2}
    _L3_ffn_all = _L3_ffn_setup()
    _L3_ffn_in = {k: v for k, v in _L3_ffn_all.items() if k in ('w1', 'b1', 'w2', 'b2')}
    del _L3_ffn_all
    return {'x': x, 'ctx_1024': ctx_1024, 'g_xattn': g_xattn, 'g_ffn': g_ffn, 'L0_xattn_W_q': _L0_xattn_in['W_q'], 'L0_xattn_W_k': _L0_xattn_in['W_k'], 'L0_xattn_W_v': _L0_xattn_in['W_v'], 'L0_xattn_W_o': _L0_xattn_in['W_o'], 'L0_xattn_b_o': _L0_xattn_in['b_o'], 'L0_ffn_W': _L0_ffn_in['W'], 'L0_ffn_b': _L0_ffn_in['b'], 'L0_ffn_ids': _L0_ffn_in['ids'], 'L0_ffn_weights': _L0_ffn_in['weights'], 'L1_ffn_W1': _L1_ffn_in['W1'], 'L1_ffn_b1': _L1_ffn_in['b1'], 'L1_ffn_W2': _L1_ffn_in['W2'], 'L1_ffn_b2': _L1_ffn_in['b2'], 'L2_ffn_Wr': _L2_ffn_in['Wr'], 'L2_ffn_br': _L2_ffn_in['br'], 'L2_ffn_We': _L2_ffn_in['We'], 'L2_ffn_be': _L2_ffn_in['be'], 'L3_xattn_Wq': _L3_xattn_in['Wq'], 'L3_xattn_Wk': _L3_xattn_in['Wk'], 'L3_xattn_Wv': _L3_xattn_in['Wv'], 'L3_ffn_w1': _L3_ffn_in['w1'], 'L3_ffn_b1': _L3_ffn_in['b1'], 'L3_ffn_w2': _L3_ffn_in['w2'], 'L3_ffn_b2': _L3_ffn_in['b2']}

def reference(x, ctx_1024, g_xattn, g_ffn, L0_xattn_W_q, L0_xattn_W_k, L0_xattn_W_v, L0_xattn_W_o, L0_xattn_b_o, L0_ffn_W, L0_ffn_b, L0_ffn_ids, L0_ffn_weights, L1_ffn_W1, L1_ffn_b1, L1_ffn_W2, L1_ffn_b2, L2_ffn_Wr, L2_ffn_br, L2_ffn_We, L2_ffn_be, L3_xattn_Wq, L3_xattn_Wk, L3_xattn_Wv, L3_ffn_w1, L3_ffn_b1, L3_ffn_w2, L3_ffn_b2):
    import jax
    import jax.numpy as jnp

    def _L0_xattn_ref(decoder_input, encoder_output, W_q, W_k, W_v, W_o, b_o):
        import jax, jax.numpy as jnp
        import numpy as np
        EMBED = 128
        HEADS = 16
        HEAD_DIM = EMBED // HEADS
        B, Sd, E = decoder_input.shape
        Se = encoder_output.shape[1]
        Q = (decoder_input @ W_q).reshape(B, Sd, HEADS, HEAD_DIM)
        K = (encoder_output @ W_k).reshape(B, Se, HEADS, HEAD_DIM)
        V = (encoder_output @ W_v).reshape(B, Se, HEADS, HEAD_DIM)
        scores = jnp.einsum('bqhd,bkhd->bhqk', Q, K) / jnp.sqrt(jnp.float32(HEAD_DIM))
        attn = jax.nn.softmax(scores, axis=-1)
        out = jnp.einsum('bhqk,bkhd->bqhd', attn, V).reshape(B, Sd, E)
        return out @ W_o + b_o

    def _L0_ffn_ref(x, W, b, ids, weights):
        import jax, jax.numpy as jnp
        import numpy as np
        Wsel = W[ids]
        bsel = b[ids]
        out = jnp.einsum('k,kod,bsd->bso', weights, Wsel, x)
        out = out + jnp.einsum('k,ko->o', weights, bsel)
        return out

    def _L1_xattn_ref(teacher_features, student_features):
        import jax, jax.numpy as jnp
        import numpy as np
        from jax import lax
        BIG = jnp.float32(1e+30)

        def _pairwise_euclidean(a, b):
            aa = jnp.sum(a * a, axis=-1)[:, None]
            bb = jnp.sum(b * b, axis=-1)[None, :]
            ab = a @ b.T
            return jnp.sqrt(jnp.maximum(aa + bb - 2.0 * ab, 0.0))

        def _dtw_cost(D):
            row0 = jnp.cumsum(D[0])

            def row_step(prev_row, d_row):
                first = d_row[0] + prev_row[0]

                def col_step(left, inp):
                    d_ij, up, diag = inp
                    r = d_ij + jnp.minimum(jnp.minimum(up, left), diag)
                    return (r, r)
                _, rest = lax.scan(col_step, first, (d_row[1:], prev_row[1:], prev_row[:-1]))
                row = jnp.concatenate([first[None], rest])
                return (row, row)
            _, rows = lax.scan(row_step, row0, D[1:])
            return jnp.concatenate([row0[None], rows], axis=0)

        def _backtrack(R, T1, T2):
            L = T1 + T2 - 1

            def step(carry, _):
                i, j, done = carry
                valid = jnp.logical_not(done)
                cd = jnp.where((i > 0) & (j > 0), R[jnp.maximum(i - 1, 0), jnp.maximum(j - 1, 0)], BIG)
                cu = jnp.where(i > 0, R[jnp.maximum(i - 1, 0), j], BIG)
                cl = jnp.where(j > 0, R[i, jnp.maximum(j - 1, 0)], BIG)
                choice = jnp.argmin(jnp.stack([cd, cu, cl]))
                ni = jnp.where(choice <= 1, i - 1, i)
                nj = jnp.where((choice == 0) | (choice == 2), j - 1, j)
                at_origin = (i == 0) & (j == 0)
                ni = jnp.where(at_origin, 0, ni)
                nj = jnp.where(at_origin, 0, nj)
                return ((ni, nj, done | at_origin), (i, j, valid))
            init = (jnp.int32(T1 - 1), jnp.int32(T2 - 1), jnp.bool_(False))
            _, (i_idx, j_idx, valid) = lax.scan(step, init, None, length=L)
            return (i_idx, j_idx, valid)

        def _align_one(small, large):
            T_small, d = small.shape
            T_large = large.shape[0]
            D = _pairwise_euclidean(small, large)
            R = _dtw_cost(D)
            i_idx, j_idx, valid = _backtrack(R, T_small, T_large)
            contrib = small[i_idx] * valid[:, None].astype(small.dtype)
            expanded = jnp.zeros((T_large, d), dtype=small.dtype).at[j_idx].add(contrib)
            return expanded
        return jax.vmap(_align_one)(teacher_features, student_features)

    def _L1_ffn_ref(x, W1, b1, W2, b2):
        import jax, jax.numpy as jnp
        import numpy as np
        HIDDEN = 128
        NUM_EXPERTS = 8
        TOP_K = 2
        B, S = (2, 256)
        Bm, Sm, d = x.shape
        E = W1.shape[0]
        x_flat = x.reshape(-1, d)
        h = jnp.mod(x_flat[:, :TOP_K].sum(axis=1).astype(jnp.int32), E)
        sel = jnp.stack([h, jnp.mod(h + 1, E)], axis=1)

        def step(acc, params):
            e, W1e, b1e, W2e, b2e = params
            w = jnp.any(sel == e, axis=1).astype(x.dtype) / TOP_K
            y = jnp.maximum(x_flat @ W1e + b1e, 0.0) @ W2e + b2e
            return (acc + w[:, None] * y, None)
        init = jnp.zeros_like(x_flat)
        out_flat, _ = jax.lax.scan(step, init, (jnp.arange(E), W1, b1, W2, b2))
        return out_flat.reshape(Bm, Sm, d)

    def _L2_xattn_ref(q, k, v):
        import jax, jax.numpy as jnp
        import numpy as np
        import math
        NHEADS = 16
        CAUSAL = True
        NEG_INF = -1e+18
        B, S, D = q.shape
        hd = D // NHEADS
        qh = q.reshape(B, S, NHEADS, hd)
        kh = k.reshape(B, S, NHEADS, hd)
        vh = v.reshape(B, S, NHEADS, hd)
        scores = jnp.einsum('bsqd,bskd->bsqk', qh, kh) / math.sqrt(hd)
        if CAUSAL:
            mask = jnp.tril(jnp.ones((NHEADS, NHEADS), dtype=bool))
            scores = jnp.where(mask, scores, jnp.asarray(NEG_INF, scores.dtype))
        attn = jax.nn.softmax(scores, axis=-1)
        out = jnp.einsum('bsqk,bskd->bsqd', attn, vh)
        return out.reshape(B, S, D)

    def _L2_ffn_ref(x, Wr, br, We, be):
        import jax, jax.numpy as jnp
        import numpy as np
        B, T, C, E = (4, 256, 128, 8)
        logits = jnp.einsum('btc,ec->bte', x, Wr) + br
        gates = jax.nn.softmax(logits, axis=-1)
        mask = (gates > 0.5).astype(x.dtype)
        h = jnp.einsum('btc,edc->bted', x, We) + be
        return jnp.einsum('bted,bte->btd', h, mask)

    def _L3_xattn_ref(query, key, value, Wq, Wk, Wv):
        import jax, jax.numpy as jnp
        import numpy as np
        THETA = 10000.0
        SCALE_BASE = 512.0
        GAMMA = 0.96875

        def _dup_interleave(x):
            return jnp.repeat(x, 2, axis=-1)

        def _xpos(x, offset, inverse_scale):
            L, d = (x.shape[-2], x.shape[-1])
            half = d // 2
            base = (jnp.arange(0, d, 2, dtype=x.dtype) + 0.4 * d) / (1.4 * d)
            pos = jnp.arange(offset, offset + L, dtype=x.dtype)
            scale = base[None, :] ** (pos[:, None] / SCALE_BASE)
            freqs = 1.0 / THETA ** (jnp.arange(half, dtype=x.dtype) / half)
            sin_in = pos[:, None] * freqs[None, :]
            if inverse_scale:
                scale = 1.0 / scale
            sin = _dup_interleave(jnp.sin(sin_in) * scale)
            cos = _dup_interleave(jnp.cos(sin_in) * scale)
            rot = jnp.stack((-x[..., 1::2], x[..., ::2]), axis=-1).reshape(x.shape)
            return x * cos + rot * sin

        def _decay_mask(L, gamma, dtype):
            u = jnp.arange(L, dtype=dtype)[:, None]
            v = jnp.arange(L, dtype=dtype)[None, :]
            return jnp.where(u >= v, gamma ** (u - v), jnp.zeros((), dtype))
        q = jnp.einsum('ble,de->bld', query, Wq)
        k = jnp.einsum('ble,de->bld', key, Wk)
        v = jnp.einsum('ble,de->bld', value, Wv)
        q = _xpos(q, 0, False)
        k = _xpos(k, 0, True)
        L = q.shape[-2]
        mask = _decay_mask(L, jnp.asarray(GAMMA, q.dtype), q.dtype)
        retention = jnp.einsum('bqd,bkd->bqk', q, k) * mask[None, :, :]
        out = jnp.einsum('bqk,bkv->bqv', retention, v)
        return out

    def _L3_ffn_ref(x, w1, b1, w2, b2):
        import jax, jax.numpy as jnp
        import numpy as np

        def _binarize(w):
            alpha = jax.lax.stop_gradient(jnp.mean(jnp.abs(w), axis=1, keepdims=True))
            bw = alpha * jnp.sign(w)
            return w + jax.lax.stop_gradient(bw - w)
        bw1 = _binarize(w1)
        h = jnp.einsum('bsd,hd->bsh', x, bw1) + b1
        h = jax.nn.gelu(h, approximate=False)
        bw2 = _binarize(w2)
        out = jnp.einsum('bsh,dh->bsd', h, bw2) + b2
        return out
    x = x + jnp.tanh(g_xattn[0]) * _L0_xattn_ref(_layernorm(x, axis=-1), ctx_1024, L0_xattn_W_q, L0_xattn_W_k, L0_xattn_W_v, L0_xattn_W_o, L0_xattn_b_o)
    x = x + jnp.tanh(g_ffn[0]) * _L0_ffn_ref(_layernorm(x, axis=-1), L0_ffn_W, L0_ffn_b, L0_ffn_ids, L0_ffn_weights)
    x = x + jnp.tanh(g_xattn[1]) * _L1_xattn_ref(ctx_1024, _layernorm(x, axis=-1))
    x = x + jnp.tanh(g_ffn[1]) * _L1_ffn_ref(_layernorm(x, axis=-1), L1_ffn_W1, L1_ffn_b1, L1_ffn_W2, L1_ffn_b2)
    x = x + jnp.tanh(g_xattn[2]) * _L2_xattn_ref(_layernorm(x, axis=-1), ctx_1024, ctx_1024)
    x = x + jnp.tanh(g_ffn[2]) * _L2_ffn_ref(_layernorm(x, axis=-1), L2_ffn_Wr, L2_ffn_br, L2_ffn_We, L2_ffn_be)
    x = x + jnp.tanh(g_xattn[3]) * _L3_xattn_ref(_layernorm(x, axis=-1), ctx_1024, ctx_1024, L3_xattn_Wq, L3_xattn_Wk, L3_xattn_Wv)
    x = x + jnp.tanh(g_ffn[3]) * _L3_ffn_ref(_layernorm(x, axis=-1), L3_ffn_w1, L3_ffn_b1, L3_ffn_w2, L3_ffn_b2)
    return x

_drawn_inputs = setup_inputs


def setup_inputs(seed=0):
    import zlib

    import numpy as np

    out = dict(_drawn_inputs(seed))
    spreads = {'L2_ffn_br': (0.0, 0.1), 'L2_ffn_be': (0.0, 0.8)}
    factors = {'g_ffn': 8.0,
     'L0_xattn_b_o': 7.675,
     'L1_ffn_b1': 8.0,
     'L1_ffn_b2': 26.737,
     'L2_ffn_Wr': 8.0,
     'L2_ffn_We': 8.0,
     'L3_ffn_w1': 8.0,
     'L3_ffn_b1': 64.0,
     'L3_ffn_w2': 8.0,
     'L3_ffn_b2': 200.0}
    for name, (base, spread) in spreads.items():
        noise = np.random.default_rng([zlib.crc32(name.encode()), seed]).standard_normal(out[name].shape)
        drawn = base * np.exp(spread * noise) if base else spread * noise
        out[name] = jnp.asarray(drawn.astype(out[name].dtype))
    for name, factor in factors.items():
        out[name] = (out[name] * factor).astype(out[name].dtype)
    return out
```

```python
from contextlib import ExitStack

import numpy as np
import concourse.bass as bass
from concourse import mybir

F32 = mybir.dt.float32
F32R = mybir.dt.float32r
BF16 = mybir.dt.bfloat16
I32 = mybir.dt.int32
ALU = mybir.AluOpType
ACT = mybir.ActivationFunctionType
AX = mybir.AxisListType.X

B, S, D = 4, 256, 128
P = 128
T = S // P
NT = B * T
HEADS, HD = 16, 8
NJ, NI = 4, 4
E1, FF = 8, 512
CH = FF // P
E2 = 8
NA, KA = 32, 8
EPS = 1e-5
BIG = 1e30
NEG = -1e18

LANES = 32
W = S // LANES
G = 2
W1C = W + 1
LAGMAX = G * (LANES - 1)
HALF = 16
HS = HALF * G
SLOTS = -(-(S + LAGMAX) // (2 * HS)) * 2 * HS
ITERS = SLOTS // (2 * HS)
ROWS = LAGMAX + SLOTS
R = 8
STRIPS = S // R
FAR = 1e4


class Steps:

    def __init__(self, eng, sem):
        self.eng, self.sem, self.n = eng, sem, 0

    def __call__(self, ins):
        self.n += 1
        ins.then_inc(self.sem, 1)

    def settle(self):
        self.eng.wait_ge(self.sem, self.n)


def build(nc, a, out):
    with ExitStack() as ctx:
        def sb(name, shape, dt=F32):
            return ctx.enter_context(nc.sbuf_tensor(name, shape, dt))

        def sem(name):
            return ctx.enter_context(nc.semaphore(name))

        with ExitStack() as l0:
            def early(name, shape):
                return l0.enter_context(nc.sbuf_tensor(name, shape, F32R))

            qk = early("qk", [P, NJ, 2, S]); mT = early("mT", [P, S]); sel = early("sel", [P, NJ, P])
        cd = sb("cd", [P, 6, HS, W])
        Cw = sb("Cw", [P, SLOTS * W], BF16)
        x = sb("x", [P, NT, D])
        cx = sb("cx", [P, NT, D])
        cxT = sb("cxT", [P, B, S])
        y = sb("y", [P, NT, D])
        yT = sb("yT", [P, B, S])
        st6 = sb("st6", [P, NT, 6])
        mv = sb("mv", [P, NT, 2])
        veps = sb("veps", [P, NT])
        rstd = sb("rstd", [P, NT])
        halfc = sb("halfc", [P, NT])
        gate = sb("gate", [P, 8])
        ident = sb("ident", [P, P])
        identb = sb("identb", [P, P], BF16)
        ones = sb("ones", [P, P])
        wq = sb("wq", [P, D]); wk = sb("wk", [P, D]); wv = sb("wv", [P, D]); wo = sb("wo", [P, D])
        wqp = sb("wqp", [P, NJ, P]); wkp = sb("wkp", [P, NJ, P])
        spl = sb("spl", [P, 3]); selc = sb("selc", [P, NJ])
        rows = sb("rows", [1, 2, D])
        Z = sb("Z", [P, 4 * R * S])

        def part(at, *shape):
            n = int(np.prod(shape))
            names = "abc"[:len(shape)]
            v = Z[:, at:at + n]
            if len(shape) == 1:
                return v
            return v.rearrange(f"p ({' '.join(names)}) -> p {' '.join(names)}", **dict(zip(names, shape)))

        qkh = part(0, NJ, 2, S).bitcast(F32R)
        mneg = part(2 * NJ * S, T, P)
        mTh = part(2 * NJ * S + T * P, S).bitcast(F32R)
        Ge = Z[0:B, 0:STRIPS * S // 2].bitcast(BF16).rearrange("p (n s) -> p n s", n=STRIPS)
        rqk, ret = part(0, 2, S), part(2 * S, T, S)
        rtmp = part(4 * S, S)
        hg = part(5 * S, CH, S)
        pen, msk, xn, Nc = (part(n * R * S, R, S) for n in range(4))
        hT = part(0, 2 * CH, S)
        vaug = sb("vaug", [P, T, HEADS, HD + 1])
        big = sb("big", [P, T * HEADS * S])
        pT = big[:].rearrange("p (t h s) -> p t h s", t=T, h=HEADS)
        w1 = big[:, 0:E1 * FF].rearrange("p (e f) -> p e f", e=E1)
        w2 = big[:, E1 * FF:2 * E1 * FF].rearrange("p (e c d) -> p e c d", e=E1, c=CH)
        rden = sb("rden", [P, T * HEADS])
        o = sb("o", [P, T, D])
        oT = sb("oT", [P, S])
        ads = sb("ads", [P, KA, D])
        adb = sb("adb", [KA, D])
        wB = sb("wB", [P, KA]); wc = sb("wc", [KA, 1]); wrow = sb("wrow", [KA, P])
        weff = sb("weff", [P, D]); weffT = sb("weffT", [P, D])
        idsb = sb("idsb", [1, KA], I32)
        sq = sb("sq", [P, S])
        Y = sb("Y", [P, R * S])
        sqc = Y[:, 0:B * S].rearrange("p (b s) -> p b s", b=B)
        crem = Y[:, B * S:2 * B * S]
        dsum = Y[:].rearrange("p (c s) -> p c s", c=W)
        Ac = Y[:].rearrange("p (r s) -> p r s", r=R)
        aab = sb("aab", [P, S]); bbk = sb("bbk", [P, W])
        Dun = sb("Dun", [P, ROWS, W1C])
        Dw = sb("Dw", [P, 2, HS, W1C])
        Rw = sb("Rw", [P, 2, HS + 1, W1C])
        mb = sb("mb", [P, G, W1C])
        late = [Dun[:].rearrange("p r c -> p (r c)")[:, n * R * S // 2:(n + 1) * R * S // 2].bitcast(BF16)
                for n in range(3)]
        Cl = late[0].rearrange("p (s w) -> p s w", w=W)
        CT = late[1].rearrange("p (b t s) -> p b t s", t=T, b=B)
        Cs = late[2].rearrange("p (r s) -> p r s", r=R)
        Pi = late[0].rearrange("p (b t s) -> p b t s", t=T, b=B)
        Pm = late[1].rearrange("p (r s) -> p r s", r=R)
        iot = sb("iot", [P, S + 1]); ioti = sb("ioti", [P, S + 1], I32)
        iotr = sb("iotr", [P, R, S])
        Gp = sb("Gp", [P, 2, S + 1])
        Gx = sb("Gx", [P, S])
        ech = sb("ech", [B, STRIPS])
        el = sb("el", [P, R + 1]); al = sb("al", [P, R])
        junk = sb("junk", [P, S])
        Gb = sb("Gb", [P, S], BF16)
        c3 = sb("c3", [P, 3, NT * D], BF16)
        b1r = sb("b1r", [E1 * CH, P]); b1c = sb("b1c", [P, E1 * CH])
        b2r = sb("b2r", [E1, D])
        thr = sb("thr", [P, 17]); modt = sb("modt", [P, 9, 7]); modi = sb("modi", [P, 63], I32)
        thri = sb("thri", [P, 17], I32)
        ssum = sb("ssum", [P, 2, T]); cmp = sb("cmp", [P, 2 * T, 17]); cnt = sb("cnt", [P, 2, T])
        cnts = sb("cnts", [P, T]); hit = sb("hit", [P, T, 9, 7]); oh = sb("oh", [P, T, 9])
        wts = sb("wts", [P, T, E1]); wtsT = sb("wtsT", [E1, S])
        acc = sb("acc", [P, 2, T, D])
        prod = sb("prod", [P, 4 * HEADS * HD])
        sc = sb("sc", [P, T, HEADS, HEADS]); sc2 = sb("sc2", [P, T, HEADS, HEADS])
        cmask = sb("cmask", [P, HEADS, HEADS])
        mx = sb("mx", [P, T * HEADS]); sm = sb("sm", [P, T * HEADS])
        wrT = sb("wrT", [P, E2]); wrr = sb("wrr", [E2, D]); brr = sb("brr", [1, E2])
        We = sb("We", [P, E2, D]); WeT = sb("WeT", [P, E2, D]); ber = sb("ber", [E2, D])
        lg = sb("lg", [P, T, E2]); lmx = sb("lmx", [P, T]); lsm = sb("lsm", [P, T])
        gm = sb("gm", [P, T, E2]); gmT = sb("gmT", [E2, S])
        w3 = sb("w3", [P, 3, D]); w3T = sb("w3T", [P, 5, D])
        xcos = sb("xcos", [P, 2, S]); xsin = sb("xsin", [P, 2, S]); decay = sb("decay", [P, T, S])
        v3 = sb("v3", [P, T, D])
        f1 = sb("f1", [P, CH, D]); f2 = sb("f2", [P, FF]); fs = prod[:].rearrange("p (c d) -> p c d", c=CH); ft = sb("ft", [P, CH, D])
        fal = sb("fal", [P, CH + 1])
        neg = acc[:].rearrange("p a t d -> p (a t) d")
        f1T = sb("f1T", [P, CH, P]); f2T = sb("f2T", [P, CH, D])
        f1br = sb("f1br", [CH, P]); f1bc = sb("f1bc", [P, CH])
        PS = ctx.enter_context(nc.psum_tensor("PS", [P, 8, 512], F32))

        dD = nc.dram_tensor("dD", (P, ROWS * W1C), F32, kind="Internal").ap()
        dC = nc.dram_tensor("dC", (P, SLOTS * W), BF16, kind="Internal").ap()
        dCr = nc.dram_tensor("dCr", (B, S, S), BF16, kind="Internal").ap()
        dG = nc.dram_tensor("dG", (B, STRIPS * S), BF16, kind="Internal").ap()
        dE = nc.dram_tensor("dE", (B, STRIPS), F32, kind="Internal").ap()
        dP = nc.dram_tensor("dP", (B, S, S), BF16, kind="Internal").ap()

        names = """ln_mv ln_rstd ln_y ln_T ln_yT ld_x ld_cx ld_w0 ld_gate ld_ids ld_ads ld_mix ld_moe ld_l2 ld_l3 ld_tab cst cst_v
            own_dve own_dp own_pool turns init_r lg_s gates padded padq
            cxT_p cxT_s q0_p q0_h q0_s v_p v_s s_p s_m mn_s qm_p qm_h qm_s st_p st_e pv_p o_n oT_p oT_s at_p x0
            weff_s weffT_p weffT_s f0_p x1
            sq_s sqc_s aabb_p aabb_s ab_p dsq d_s d_w d_r0 d_r1 rows_g codes codes_w cl_r clT_p ct_s ct_w cs_r
            g_s g_w g_r e_s e_w e_r p_s p_w p_r ex_p x2 c3_s
            b1_p b1_s wt_s wtT_p wtT_s b2_p b2_s mm1_p mm1_s mm2_p mm2_s x3
            sc_s sc_e x4 weT_p weT_s lg_p lg_e gm_s gmT_p gmT_s eb_p eb_s e2_p e2_s x5
            w3T_p w3T_s k3_p q3_s k3_s v3_p v3_s rt_p rt_s ro_p x6
            fb_s fT_p fT_s h3_p h3_s f3_p x7 st_out""".split()
        s = {n: sem(n) for n in names}

        block = ctx.enter_context(nc.Block())

        def nth(L, b):
            return B * L + b + 1

        def nth_T(L, b):
            return nth(L - (L > 4), b)

        def lnbank(L, b):
            return 7 if L == 0 else b % 2 if L in (1, 2) else 0

        def tiles(b):
            return slice(b * T, (b + 1) * T)

        @block.sync
        def _(sp):
            xin = a["x"].rearrange("b (t p) d -> p (b t) d", p=P)
            cin = a["ctx_1024"].rearrange("b (t p) d -> p (b t) d", p=P)
            sp.dma_start(x[:], xin).then_inc(s["ld_x"], 16)
            sp.dma_start(cx[:], cin).then_inc(s["ld_cx"], 16)
            for dst, nm in ((wq, "W_q"), (wk, "W_k"), (wv, "W_v"), (wo, "W_o")):
                sp.dma_start(dst[:], a["L0_xattn_" + nm]).then_inc(s["ld_w0"], 16)
            sp.dma_start(spl[:], a["t_split"]).then_inc(s["ld_w0"], 16)
            sp.dma_start(selc[:], a["t_sel"]).then_inc(s["ld_w0"], 16)
            sp.dma_start(rows[0:1, 0, :], a["L0_xattn_b_o"][None, :]).then_inc(s["ld_w0"], 16)
            for n, nm in enumerate(("g_xattn", "g_ffn")):
                sp.dma_start(gate[:, 4 * n:4 * n + 4],
                             a[nm][None, :].partition_broadcast(P)).then_inc(s["ld_gate"], 16)
            sp.dma_start(idsb[:], a["L0_ffn_ids"][None, :]).then_inc(s["ld_ids"], 16)
            sp.dma_start(wB[:], a["L0_ffn_weights"][None, :].partition_broadcast(P)).then_inc(s["ld_mix"], 16)
            sp.dma_start(wc[:], a["L0_ffn_weights"][:, None]).then_inc(s["ld_mix"], 16)
            sp.wait_ge(s["ld_ids"], 16)
            for k in range(KA):
                i = sp.value_load(idsb[0:1, k:k + 1], min_val=0, max_val=NA - 1)
                sp.dma_start(ads[:, k, :], a["L0_ffn_W"][bass.ds(i, 1), :, :].rearrange("a o d -> (a o) d")
                             ).then_inc(s["ld_ads"], 16)
                sp.dma_start(adb[k:k + 1, :], a["L0_ffn_b"][bass.ds(i, 1), :]).then_inc(s["ld_ads"], 16)
            sp.dma_start(b1r[:], a["L1_ffn_b1"].rearrange("e (c p) -> (e c) p", p=P)).then_inc(s["ld_moe"], 16)
            sp.dma_start(b2r[:], a["L1_ffn_b2"]).then_inc(s["ld_moe"], 16)
            sp.dma_start(wrr[:], a["L2_ffn_Wr"]).then_inc(s["ld_l2"], 16)
            sp.dma_start(brr[:], a["L2_ffn_br"][None, :]).then_inc(s["ld_l2"], 16)
            sp.dma_start(We[:], a["L2_ffn_We"].rearrange("e d c -> d e c")).then_inc(s["ld_l2"], 16)
            sp.dma_start(ber[:], a["L2_ffn_be"]).then_inc(s["ld_l2"], 16)
            for n, nm in enumerate(("Wq", "Wk", "Wv")):
                sp.dma_start(w3[:, n, :], a["L3_xattn_" + nm]).then_inc(s["ld_l3"], 16)
            sp.dma_start(f1[:], a["L3_ffn_w1"].rearrange("(c p) d -> p c d", p=P)).then_inc(s["ld_l3"], 16)
            sp.dma_start(f2[:], a["L3_ffn_w2"]).then_inc(s["ld_l3"], 16)
            sp.dma_start(f1br[:], a["L3_ffn_b1"].rearrange("(c p) -> c p", p=P)).then_inc(s["ld_l3"], 16)
            sp.dma_start(rows[0:1, 1, :], a["L3_ffn_b2"][None, :]).then_inc(s["ld_l3"], 16)
            sp.dma_start(xcos[:], a["t_cos"]).then_inc(s["ld_tab"], 16)
            sp.dma_start(xsin[:], a["t_sin"]).then_inc(s["ld_tab"], 16)
            sp.dma_start(decay[:], a["t_decay"]).then_inc(s["ld_tab"], 16)
            sp.dma_start(cmask[:], a["t_causal"]).then_inc(s["ld_tab"], 16)
            sp.wait_ge(s["pv_p"], B)
            sp.dma_start(w1, a["L1_ffn_W1"].rearrange("e d f -> d e f")).then_inc(s["ld_moe"], 16)
            sp.dma_start(w2, a["L1_ffn_W2"].rearrange("e (c p) d -> p e c d", p=P)).then_inc(s["ld_moe"], 16)
            sp.wait_ge(s["d_s"], W)
            sp.wait_ge(s["padded"], 3)
            sp.wait_ge(s["padq"], B)
            sp.dma_start(dD, Dun[:].rearrange("p r c -> p (r c)")).then_inc(s["d_w"], 16)
            sp.wait_ge(s["d_w"], 16)

            skew = bass.AP(tensor=dD.tensor, offset=LAGMAX * W1C,
                           ap=[[LANES * ROWS * W1C, B], [ROWS * W1C - G * W1C, LANES], [1, SLOTS * W1C]])
            HW = HS * W1C
            for h in range(2):
                sp.dma_start(Dw[:, h].rearrange("p r c -> p (r c)"), skew[:, :, h * HW:(h + 1) * HW]
                             ).then_inc(s[f"d_r{h}"], 16)
            with sp.Fori(0, ITERS - 1) as it:
                for h in range(2):
                    sp.wait_ge(s["rows_g"], 2 * it + h + 1)
                    sp.dma_start(Dw[:, h].rearrange("p r c -> p (r c)"),
                                 skew[:, :, bass.ds((2 * it + 2 + h) * HW, HW)]).then_inc(s[f"d_r{h}"], 16)
            sp.wait_ge(s["codes"], 2 * ITERS + 2)
            sp.dma_start(dC, Cw[:]).then_inc(s["codes_w"], 16)
            sp.wait_ge(s["codes_w"], 16)
            sp.dma_start(Cl.rearrange("p r c -> p (r c)"),
                         bass.AP(tensor=dC.tensor, offset=0,
                                 ap=[[LANES * SLOTS * W, B], [SLOTS * W + G * W, LANES], [1, S * W]])
                         ).then_inc(s["cl_r"], 16)
            sp.wait_ge(s["ct_s"], T)
            sp.dma_start(dCr.rearrange("b (t p) j -> p (b t) j", p=P), CT.rearrange("p b t s -> p (b t) s")).then_inc(s["ct_w"], 16)
            sp.wait_ge(s["ct_w"], 16)
            sp.dma_start(Cs.rearrange("p r j -> p (r j)"), dCr.rearrange("b (s r) j -> (b s) (r j)", r=R)
                         ).then_inc(s["cs_r"], 16)
            sp.wait_ge(s["g_s"], 1)
            sp.dma_start(dG.rearrange("b (s j) -> (b s) j", j=S), Gb[:]).then_inc(s["g_w"], 16)
            sp.wait_ge(s["g_w"], 16)
            sp.dma_start(Ge.rearrange("b s j -> b (s j)"), dG).then_inc(s["g_r"], 16)
            sp.wait_ge(s["e_s"], 1)
            sp.dma_start(dE, ech[:]).then_inc(s["e_w"], 16)
            sp.wait_ge(s["e_w"], 16)
            sp.dma_start(el[:, R:R + 1], dE.rearrange("b (s o) -> (b s) o", o=1)).then_inc(s["e_r"], 16)
            sp.wait_ge(s["p_s"], 1)
            sp.dma_start(dP.rearrange("b (s r) j -> (b s) (r j)", r=R), Pm.rearrange("p r j -> p (r j)")
                         ).then_inc(s["p_w"], 16)
            sp.wait_ge(s["p_w"], 16)
            sp.dma_start(Pi.rearrange("p b t s -> p (b t) s"), dP.rearrange("b (t p) j -> p (b t) j", p=P)).then_inc(s["p_r"], 16)
            outv = out.rearrange("b (t p) d -> p (b t) d", p=P)
            for b in range(B):
                sp.wait_ge(s["x7"], b + 1)
                sp.dma_start(outv[:, tiles(b), :], x[:, tiles(b), :]).then_inc(s["st_out"], 16)
            sp.wait_ge(s["st_out"], 16 * B)

        @block.gpsimd
        def _(pool):
            own = Steps(pool, s["own_pool"])
            own(pool.memset(ident[:], 0.0))
            own(pool.memset(halfc[:], -0.5))
            pool.memset(ones[:], 1.0).then_inc(s["cst"], 1)
            own.settle()
            pool.affine_select(out=ident[:], in_=ident[:], compare_op=ALU.not_equal, fill=1.0, base=0,
                               pattern=[[-1, P]], channel_multiplier=1).then_inc(s["cst"], 1)
            pool.memset(mneg, 0.0).then_inc(s["cst"], 1)
            pool.memset(vaug[:], 1.0).then_inc(s["cst"], 1)
            pool.iota(ioti[:], pattern=[[1, S + 1]], base=-1, channel_multiplier=0).then_inc(s["cst"], 1)
            pool.iota(thri[:], pattern=[[1, 17]], base=1, channel_multiplier=0).then_inc(s["cst"], 1)
            pool.iota(modi[:], pattern=[[1, 9], [8, 7]], base=-8, channel_multiplier=0).then_inc(s["cst"], 1)

            def rstds(L):
                for b in range(B):
                    pool.wait_ge(s["ln_mv"], nth(L, b))
                    pool.tensor_tensor(rstd[:, tiles(b)], veps[:, tiles(b)], halfc[:, tiles(b)], ALU.pow
                                       ).then_inc(s["ln_rstd"], 1)

            rstds(0)
            pool.memset(Dun[:, 0:LAGMAX, :], BIG).then_inc(s["padded"], 1)
            pool.memset(Dun[:, LAGMAX + S:ROWS, :], 0.0).then_inc(s["padded"], 1)
            own(pool.memset(Dun[:, LAGMAX:LAGMAX + S, 0:1], 0.0))
            own.settle()
            for b in range(B):
                pool.memset(Dun[b * LANES:b * LANES + 1, LAGMAX:LAGMAX + S, 0:1], BIG).then_inc(s["padq"], 1)
                pool.wait_ge(s["padq"], b + 1)
            own(pool.memset(Rw[:, 1, HS - 1:HS + 1, :], BIG))
            own.settle()
            for b in range(B):
                own(pool.memset(Rw[b * LANES:b * LANES + 1, 1, HS:HS + 1, 0:1], 0.0))
                own.settle()
            own.settle()
            pool.sem_inc(s["init_r"], 1)
            pool.memset(sc[:], 0.0).then_inc(s["padded"], 1)
            pool.wait_ge(s["ld_cx"], 16)
            cf = cx[:].rearrange("p t d -> p (t d)")
            own(pool.tensor_copy(c3[:, 0, :], cf))
            own.settle()
            own(pool.tensor_tensor(crem, cf, c3[:, 0, :], ALU.subtract))
            own.settle()
            own(pool.tensor_copy(c3[:, 1, :], crem))
            own.settle()
            own(pool.tensor_tensor(crem, crem, c3[:, 1, :], ALU.subtract))
            own.settle()
            pool.tensor_copy(c3[:, 2, :], crem).then_inc(s["c3_s"], 1)
            rstds(1)
            rstds(2)
            pool.sem_inc(s["codes"], 2)
            n_code = 10
            with pool.Fori(0, ITERS) as it:
                for h in range(2):
                    k = [0]

                    def step(ins):
                        k[0] += 1
                        ins.then_inc(s["own_pool"], 1)

                    def settle():
                        pool.wait_ge(s["own_pool"], own.n + (2 * it + h) * n_code + k[0])
                        pool.sem_inc(s["turns"], 1)

                    pool.wait_ge(s["rows_g"], 2 * it + h + 1)
                    dg = Rw[:, h, 0:HS, 0:W]
                    up = Rw[:, h, 0:HS, 1:W + 1]
                    lf = Rw[:, h, 1:HS + 1, 0:W]
                    step(pool.tensor_tensor(cd[:, 0], dg, up, ALU.subtract))
                    step(pool.tensor_tensor(cd[:, 1], dg, lf, ALU.subtract))
                    step(pool.tensor_tensor(cd[:, 2], up, lf, ALU.subtract))
                    settle()
                    step(pool.tensor_scalar(cd[:, 3], cd[:, 0], 0.0, None, ALU.is_le))
                    step(pool.tensor_scalar(cd[:, 4], cd[:, 1], 0.0, None, ALU.is_le))
                    step(pool.tensor_scalar(cd[:, 5], cd[:, 2], 0.0, None, ALU.is_le))
                    settle()
                    step(pool.tensor_tensor(cd[:, 0], cd[:, 3], cd[:, 4], ALU.mult))
                    step(pool.tensor_scalar(cd[:, 1], cd[:, 5], -1.0, 2.0, ALU.mult, ALU.add))
                    settle()
                    step(pool.tensor_scalar(cd[:, 2], cd[:, 0], -1.0, 1.0, ALU.mult, ALU.add))
                    settle()
                    step(pool.tensor_tensor(cd[:, 3], cd[:, 2], cd[:, 1], ALU.mult))
                    settle()
                    assert k[0] == n_code
                    pool.tensor_copy(Cw[:, bass.ds((2 * it + h) * HS * W, HS * W)],
                                     cd[:, 3].rearrange("p r c -> p (r c)")).then_inc(s["codes"], 1)
                    pool.wait_ge(s["codes"], 2 * it + h + 3)
            own.n += 2 * ITERS * n_code
            for L in range(3, 8):
                rstds(L)

        @block.tensor
        def _(pe):
            def ln_T(L, b):
                pe.wait_ge(s["ln_y"], nth(L, b))
                if L in (1, 2) and b >= 2:
                    pe.wait_ge(s["ln_yT"], nth_T(L, b) - 2)
                for t in range(T):
                    mm = pe.transpose(PS[:, lnbank(L, b), t * P:(t + 1) * P], y[:, b * T + t, :], ident[:])
                mm.then_inc(s["ln_T"], 1)

            pe.wait_ge(s["cst"], 2)
            pe.wait_ge(s["ld_cx"], 16)
            for n in range(NT):
                mm = pe.transpose(PS[:, 2 + n // 4, (n % 4) * P:(n % 4 + 1) * P], cx[:, n, :], ident[:])
                if n % 4 == 3:
                    mm.then_inc(s["cxT_p"], 1)
            pe.wait_ge(s["cst_v"], 2)
            pe.wait_ge(s["ld_w0"], 112)
            pe.wait_ge(s["cxT_s"], 2)

            def project(b):
                pe.wait_ge(s["ln_yT"], nth_T(0, b))
                for j in range(NJ):
                    pe.matmul(PS[:, j, 0:S], wqp[:, j, :], yT[:, b, :], start=True, stop=True)
                    pe.matmul(PS[:, j, S:2 * S], wkp[:, j, :], cxT[:, b, :], start=True, stop=True
                              ).then_inc(s["q0_p"], 1)
                for t in range(T):
                    mm = pe.matmul(PS[:, 7, t * P:(t + 1) * P], cxT[:, b, t * P:(t + 1) * P], wv[:],
                                   start=True, stop=True)
                mm.then_inc(s["v_p"], 1)

            def scores(u, at_, lhs, rhs, done, maxima):
                jp, t = divmod(u, T)
                for i in range(NI):
                    r = slice(32 * i, 32 * (i + 1))
                    r8 = slice(32 * i, 32 * i + 2 * NJ)
                    for jj in range(2):
                        j = 2 * jp + jj
                        to = PS[:, at_ + i, jj * S:(jj + 1) * S]
                        if maxima:
                            pe.matmul(to, sel[r8, j, :], mT[r8, :], start=True, stop=False)
                        mm = pe.matmul(to, qk[r, j, lhs, t * P:(t + 1) * P], qk[r, j, rhs, :],
                                       start=not maxima, stop=True)
                mm.then_inc(s[done], 1)

            def weigh(b, jp):
                for t in range(T):
                    for h in range(2 * NI * jp, 2 * NI * (jp + 1)):
                        c = (t * HEADS + h) * (HD + 1)
                        for kt in range(T):
                            mm = pe.matmul(PS[:, 4, c:c + HD + 1], pT[:, kt, h, t * P:(t + 1) * P],
                                           vaug[:, kt, h, :], start=(kt == 0), stop=(kt == T - 1))
                if jp:
                    mm.then_inc(s["pv_p"], 1)

            def finish(b):
                pe.wait_ge(s["o_n"], b + 1)
                for t in range(T):
                    mm = pe.transpose(PS[:, 5, t * P:(t + 1) * P], o[:, t, :], ident[:])
                mm.then_inc(s["oT_p"], 1)
                pe.wait_ge(s["oT_s"], b + 1)
                for t in range(T):
                    c = slice(t * P, (t + 1) * P)
                    pe.matmul(PS[:, 6, c], oT[:, c], wo[:], start=True, stop=False)
                    mm = pe.matmul(PS[:, 6, c], ones[0:1, :], rows[0:1, 0, :], start=False, stop=True)
                mm.then_inc(s["at_p"], 1)

            ln_T(0, 0)
            project(0)
            for b in range(B):
                for u in range(4):
                    if u == 0:
                        pe.wait_ge(s["q0_s"], NJ * (b + 1))
                    elif u == 1:
                        if b:
                            finish(b - 1)
                            pe.wait_ge(s["x0"], b)
                        pe.wait_ge(s["v_s"], b + 1)
                    else:
                        pe.wait_ge(s["s_m"], 4 * b + u - 1)
                    scores(u, 4 * (u % 2), 0, 1, "s_p", False)
                pe.wait_ge(s["mn_s"], b + 1)
                for t in range(T):
                    mm = pe.transpose(PS[:, 0, t * P:(t + 1) * P], mneg[:, t, :], ident[:])
                mm.then_inc(s["qm_p"], 1)
                pe.wait_ge(s["qm_s"], b + 1)
                for u in range(4):
                    if u >= 2:
                        pe.wait_ge(s["st_e"], 4 * b + u - 1)
                    scores(u, 4 * (1 - u % 2), 1, 0, "st_p", True)
                pe.wait_ge(s["st_e"], 4 * b + 3)
                if b + 1 < B:
                    ln_T(0, b + 1)
                weigh(b, 0)
                pe.wait_ge(s["st_e"], 4 * b + 4)
                if b + 1 < B:
                    project(b + 1)
                weigh(b, 1)
            finish(B - 1)
            pe.wait_ge(s["weff_s"], 1)
            pe.transpose(PS[:, 5, 0:P], weff[:], ident[:]).then_inc(s["weffT_p"], 1)
            pe.wait_ge(s["weffT_s"], 1)
            for b in range(B):
                ln_T(1, b)
                pe.wait_ge(s["ln_yT"], nth_T(1, b))
                if b >= 2:
                    pe.wait_ge(s["x1"], b - 1)
                for t in range(T):
                    c = slice(t * P, (t + 1) * P)
                    pe.matmul(PS[:, 2 + b % 2, c], yT[:, b, c], weffT[:], start=True, stop=False)
                    mm = pe.matmul(PS[:, 2 + b % 2, c], wrow[:], adb[:], start=False, stop=True)
                mm.then_inc(s["f0_p"], 1)
            pe.wait_ge(s["x1"], B)
            pe.wait_ge(s["sqc_s"], 1)
            for b in range(B):
                ln_T(2, b)
                pe.wait_ge(s["ln_yT"], nth_T(2, b))
                q = slice(b * LANES, (b + 1) * LANES)
                for c in range(W):
                    mm = pe.matmul(PS[q, 2 + c // 2, (c % 2) * S:(c % 2 + 1) * S], yT[:, b, c:S:W], cxT[:, b, :],
                                   start=True, stop=True)
                mm.then_inc(s["ab_p"], 1)
                pe.matmul(PS[q, 6, 0:S], ones[:, 0:LANES], sqc[:, b, :], start=True, stop=True)
                pe.wait_ge(s["sq_s"], b + 1)
                for c in range(W):
                    mm = pe.matmul(PS[q, 6, S + c:S + c + 1], sq[:, c:S:W], ones[:, 0:1], start=True, stop=True)
                mm.then_inc(s["aabb_p"], 1)
            pe.wait_ge(s["ld_moe"], 64)
            pe.transpose(PS[:, 0, 0:E1 * CH], b1r[:], ident[0:E1 * CH, 0:E1 * CH]).then_inc(s["b1_p"], 1)
            pe.wait_ge(s["ld_l2"], 64)
            pe.wait_ge(s["aabb_s"], 1)
            pe.wait_ge(s["dsq"], 1)
            for e in range(E2):
                mm = pe.transpose(PS[:, 2 + e // 4, (e % 4) * D:(e % 4 + 1) * D], We[:, e, :], ident[:])
            pe.transpose(PS[:, 4, 0:E2], wrr[:], ident[0:E2, 0:E2]).then_inc(s["weT_p"], 1)
            pe.wait_ge(s["ld_l3"], 112)
            for n in range(3):
                pe.transpose(PS[:, 5, n * D:(n + 1) * D], w3[:, n, :], ident[:])
            pe.transpose(PS[:, 5, 3 * D:3 * D + CH], f1br[:], ident[0:CH, 0:CH]).then_inc(s["w3T_p"], 1)
            pe.wait_ge(s["fb_s"], 1)
            for c in range(CH):
                pe.transpose(PS[:, 6, c * P:(c + 1) * P], fs[:, c, :], ident[:])
            for c in range(CH):
                mm = pe.transpose(PS[:, 7, c * P:(c + 1) * P], ft[:, c, :], ident[:])
            mm.then_inc(s["fT_p"], 1)
            pe.wait_ge(s["weT_s"], 1)
            pe.wait_ge(s["cl_r"], 16)
            pe.wait_ge(s["cst_v"], 2)
            for t in range(T):
                bank = PS[:, 2 + t, :].bitcast(BF16)
                for c in range(W):
                    mm = pe.transpose(bank[:, c * P:(c + 1) * P], Cl[:, t * P:(t + 1) * P, c], identb[:])
                mm.then_inc(s["clT_p"], 1)
            pe.wait_ge(s["p_r"], 16)
            pe.wait_ge(s["c3_s"], 1)
            pe.wait_ge(s["w3T_s"], 1)
            pe.wait_ge(s["ct_s"], T)
            for b in range(B):
                for jt in range(T):
                    for n in range(3 * T):
                        t, part = divmod(n, 3)
                        mm = pe.matmul(PS[:, 2 + b, jt * P:(jt + 1) * P], Pi[:, b, t, jt * P:(jt + 1) * P],
                                       c3[:, part, (b * T + t) * D:(b * T + t + 1) * D],
                                       start=(n == 0), stop=(n == 3 * T - 1))
                mm.then_inc(s["ex_p"], 1)
            pe.wait_ge(s["x2"], B)
            pe.wait_ge(s["b1_s"], 1)
            for b in range(B):
                if b:
                    pe.wait_ge(s["b2_s"], b)
                ln_T(3, b)
                pe.wait_ge(s["wt_s"], b + 1)
                for t in range(T):
                    mm = pe.transpose(PS[0:E1, 1, t * P:(t + 1) * P], wts[:, t, :], ident[:])
                mm.then_inc(s["wtT_p"], 1)
                pe.wait_ge(s["ln_yT"], nth_T(3, b))

                def up(e):
                    n = E1 * b + e
                    if n >= 2:
                        pe.wait_ge(s["mm1_s"], 2 * (n - 1))
                    for c in range(CH):
                        mm = pe.matmul(PS[:, 2 + 2 * (n % 2) + c // 2, (c % 2) * S:(c % 2 + 1) * S],
                                       w1[:, e, c * P:(c + 1) * P], yT[:, b, :], start=True, stop=True)
                        if c % 2:
                            mm.then_inc(s["mm1_p"], 1)

                def down(e):
                    n = E1 * b + e
                    pe.wait_ge(s["mm1_s"], 2 * (n + 1))
                    if n >= 2:
                        pe.wait_ge(s["mm2_s"], n - 1)
                    for t in range(T):
                        for c in range(CH):
                            mm = pe.matmul(PS[:, 6 + n % 2, t * D:(t + 1) * D], hT[:, CH * (n % 2) + c, t * P:(t + 1) * P],
                                           w2[:, e, c, :], start=(c == 0), stop=(c == CH - 1))
                    mm.then_inc(s["mm2_p"], 1)

                up(0)
                pe.wait_ge(s["wtT_s"], b + 1)
                for t in range(T):
                    mm = pe.matmul(PS[:, 0, t * D:(t + 1) * D], wtsT[:, t * P:(t + 1) * P], b2r[:],
                                   start=True, stop=True)
                mm.then_inc(s["b2_p"], 1)
                for e in range(1, E1):
                    up(e)
                    down(e - 1)
                down(E1 - 1)
            pe.wait_ge(s["weT_s"], 1)
            for b in range(B):
                ln_T(5, b)
                pe.wait_ge(s["ln_yT"], nth_T(5, b))
                if b:
                    pe.wait_ge(s["x5"], b)
                for t in range(T):
                    c = slice(t * E2, (t + 1) * E2)
                    pe.matmul(PS[:, 1, c], yT[:, b, t * P:(t + 1) * P], wrT[:], start=True, stop=False)
                    mm = pe.matmul(PS[:, 1, c], ones[0:1, :], brr[:], start=False, stop=True)
                mm.then_inc(s["lg_p"], 1)
                for t in range(T):
                    for h in range(2):
                        mm = pe.matmul(PS[:, 2 + 2 * t + h, :], yT[:, b, t * P:(t + 1) * P],
                                       WeT[:, 4 * h:4 * h + 4, :].rearrange("p e d -> p (e d)"),
                                       start=True, stop=True)
                mm.then_inc(s["e2_p"], 1)
                pe.wait_ge(s["gm_s"], b + 1)
                for t in range(T):
                    mm = pe.transpose(PS[0:E2, 6, t * P:(t + 1) * P], gm[:, t, :], ident[:])
                mm.then_inc(s["gmT_p"], 1)
                pe.wait_ge(s["gmT_s"], b + 1)
                for t in range(T):
                    mm = pe.matmul(PS[:, 7, t * D:(t + 1) * D], gmT[:, t * P:(t + 1) * P], ber[:],
                                   start=True, stop=True)
                mm.then_inc(s["eb_p"], 1)
            pe.wait_ge(s["w3T_s"], 1)
            for b in range(B):
                ln_T(6, b)
                pe.wait_ge(s["ln_yT"], nth_T(6, b))
                if b:
                    pe.wait_ge(s["x6"], b)
                pe.matmul(PS[:, 2, 0:S], w3T[:, 0, :], yT[:, b, :], start=True, stop=True)
                pe.matmul(PS[:, 2, S:2 * S], w3T[:, 3, :], yT[:, b, :], start=True, stop=True)
                pe.matmul(PS[:, 3, 0:S], w3T[:, 1, :], cxT[:, b, :], start=True, stop=True)
                pe.matmul(PS[:, 3, S:2 * S], w3T[:, 4, :], cxT[:, b, :], start=True, stop=True
                          ).then_inc(s["k3_p"], 1)
                for t in range(T):
                    mm = pe.matmul(PS[:, 4, t * D:(t + 1) * D], cxT[:, b, t * P:(t + 1) * P], w3T[:, 2, :],
                                   start=True, stop=True)
                mm.then_inc(s["v3_p"], 1)
                pe.wait_ge(s["k3_s"], b + 1)
                for t in range(T):
                    mm = pe.matmul(PS[:, 5, t * S:(t + 1) * S], rqk[:, 1, t * P:(t + 1) * P], rqk[:, 0, :],
                                   start=True, stop=True)
                mm.then_inc(s["rt_p"], 1)
                pe.wait_ge(s["rt_s"], b + 1)
                pe.wait_ge(s["v3_s"], b + 1)
                for t in range(T):
                    for kt in range(t + 1):
                        mm = pe.matmul(PS[:, 6, t * D:(t + 1) * D], ret[:, kt, t * P:(t + 1) * P], v3[:, kt, :],
                                       start=(kt == 0), stop=(kt == t))
                mm.then_inc(s["ro_p"], 1)
            pe.wait_ge(s["fT_s"], 1)
            for b in range(B):
                ln_T(7, b)
                pe.wait_ge(s["ln_yT"], nth_T(7, b))
                if b:
                    pe.wait_ge(s["h3_s"], 2 * b)
                for c in range(CH):
                    mm = pe.matmul(PS[:, 2 + c // 2, (c % 2) * S:(c % 2 + 1) * S], f1T[:, c, :], yT[:, b, :],
                                   start=True, stop=True)
                    if c % 2:
                        mm.then_inc(s["h3_p"], 1)
                pe.wait_ge(s["h3_s"], 2 * (b + 1))
                if b:
                    pe.wait_ge(s["x7"], b)
                for t in range(T):
                    c_ = slice(t * D, (t + 1) * D)
                    for c in range(CH):
                        pe.matmul(PS[:, 7, c_], hg[:, c, t * P:(t + 1) * P], f2T[:, c, :],
                                  start=(c == 0), stop=False)
                    mm = pe.matmul(PS[:, 7, c_], ones[0:1, :], rows[0:1, 1, :], start=False, stop=True)
                mm.then_inc(s["f3_p"], 1)

        @block.scalar
        def _(act):
            def copy(out_, in_):
                return act.activation(out_, in_, ACT.Copy)

            def ln_yT(L, b):
                act.wait_ge(s["ln_T"], nth_T(L, b))
                copy(yT[:, b, :], PS[:, lnbank(L, b), 0:S]).then_inc(s["ln_yT"], 1)

            for n in range(2):
                act.wait_ge(s["cxT_p"], n + 1)
                copy(cxT[:, 2 * n:2 * n + 2, :].rearrange("p b s -> p (b s)"), PS[:, 2 + n, :]
                     ).then_inc(s["cxT_s"], 1)
            act.wait_ge(s["ld_gate"], 32)
            act.activation(gate[:], gate[:], ACT.Tanh).then_inc(s["gates"], 1)
            act.wait_ge(s["cst"], 4)

            def projected(b):
                for j in range(NJ):
                    act.wait_ge(s["q0_p"], NJ * b + j + 1)
                    if b:
                        act.wait_ge(s["q0_s"], NJ * (b - 1) + j + 1)
                    copy(qkh[:, j].rearrange("p n s -> p (n s)"), PS[:, j, :]).then_inc(s["q0_h"], 1)
                act.wait_ge(s["v_p"], b + 1)
                if b:
                    act.wait_ge(s["pv_p"], b)
                copy(vaug[:, :, :, 0:HD].rearrange("p t h d -> p (t h) d"),
                     PS[:, 7, 0:S].rearrange("p (n d) -> p n d", d=HD)).then_inc(s["v_s"], 1)

            def o_T(b):
                act.wait_ge(s["oT_p"], b + 1)
                if b:
                    act.wait_ge(s["at_p"], b)
                copy(oT[:], PS[:, 5, 0:S]).then_inc(s["oT_s"], 1)

            ln_yT(0, 0)
            projected(0)
            for b in range(B):
                act.wait_ge(s["qm_p"], b + 1)
                copy(mTh, PS[:, 0, 0:S]).then_inc(s["qm_h"], 1)
                for u in range(4):
                    jp, t = divmod(u, T)
                    at_ = 4 * (1 - u % 2)
                    act.wait_ge(s["st_p"], 4 * b + u + 1)
                    act.activation(pT[:, t, 2 * NI * jp:2 * NI * (jp + 1), :].rearrange("p (j i) q -> p i j q", j=2),
                                   PS[:, at_:at_ + 4, :].rearrange("p i (j q) -> p i j q", j=2),
                                   ACT.Exp, scale=HD ** -0.5).then_inc(s["st_e"], 1)
                if b + 1 < B:
                    ln_yT(0, b + 1)
                    projected(b + 1)
                o_T(b)
            act.wait_ge(s["weffT_p"], 1)
            copy(weffT[:], PS[:, 5, 0:P]).then_inc(s["weffT_s"], 1)
            for b in range(B):
                ln_yT(1, b)
            for b in range(B):
                ln_yT(2, b)
            for c in range(W):
                act.wait_ge(s["dsq"], 1)
                act.activation(Dun[:, LAGMAX:LAGMAX + S, c + 1], dsum[:, c, :], ACT.Sqrt).then_inc(s["d_s"], 1)
            act.wait_ge(s["b1_p"], 1)
            copy(b1c[:], PS[:, 0, 0:E1 * CH]).then_inc(s["b1_s"], 1)
            act.wait_ge(s["weT_p"], 1)
            copy(WeT[:].rearrange("p e d -> p (e d)"), PS[:, 2:4, :].rearrange("p a n -> p (a n)"))
            copy(wrT[:], PS[:, 4, 0:E2]).then_inc(s["weT_s"], 1)
            act.wait_ge(s["w3T_p"], 1)
            copy(w3T[:, 0:3, :].rearrange("p a n -> p (a n)"), PS[:, 5, 0:3 * D])
            copy(f1bc[:], PS[:, 5, 3 * D:3 * D + CH])
            for n in range(2):
                pv = PS[:, 5, n * D:(n + 1) * D].rearrange("p (m two) -> p m two", two=2)
                wv_ = w3T[:, 3 + n, :].rearrange("p (m two) -> p m two", two=2)
                act.activation(wv_[:, :, 0], pv[:, :, 1], ACT.Copy, scale=-1.0)
                last = copy(wv_[:, :, 1], pv[:, :, 0])
            last.then_inc(s["w3T_s"], 1)
            act.wait_ge(s["fT_p"], 1)
            copy(f1T[:].rearrange("p c n -> p (c n)"), PS[:, 6, :])
            copy(f2T[:].rearrange("p c n -> p (c n)"), PS[:, 7, :]).then_inc(s["fT_s"], 1)
            for t in range(T):
                act.wait_ge(s["clT_p"], t + 1)
                copy(CT[:, :, t, :].rearrange("p b (k c) -> p b k c", c=W),
                     PS[:, 2 + t, :].bitcast(BF16).rearrange("p (c b k) -> p b k c", c=W, b=B)
                     ).then_inc(s["ct_s"], 1)
            for b in range(B):
                ln_yT(3, b)
                act.wait_ge(s["wtT_p"], b + 1)
                if b:
                    act.wait_ge(s["b2_p"], b)
                copy(wtsT[:], PS[0:E1, 1, 0:S]).then_inc(s["wtT_s"], 1)
                for e in range(E1):
                    n = E1 * b + e
                    for c in range(CH):
                        act.wait_ge(s["mm1_p"], 2 * n + c // 2 + 1)
                        if n >= 2 and c == 0:
                            act.wait_ge(s["mm2_p"], n - 1)
                        last = act.activation(hT[:, CH * (n % 2) + c, :],
                                              PS[:, 2 + 2 * (n % 2) + c // 2, (c % 2) * S:(c % 2 + 1) * S],
                                              ACT.Relu, bias=b1c[:, e * CH + c:e * CH + c + 1])
                        if c % 2:
                            last.then_inc(s["mm1_s"], 1)
            for b in range(B):
                act.wait_ge(s["sc_s"], b + 1)
                act.activation(sc2[:], sc2[:], ACT.Exp).then_inc(s["sc_e"], 1)
            for b in range(B):
                ln_yT(5, b)
                act.wait_ge(s["lg_s"], b + 1)
                act.activation(lg[:], lg[:], ACT.Exp).then_inc(s["lg_e"], 1)
                act.wait_ge(s["gmT_p"], b + 1)
                copy(gmT[:], PS[0:E2, 6, 0:S]).then_inc(s["gmT_s"], 1)
            for b in range(B):
                ln_yT(6, b)
                act.wait_ge(s["v3_p"], b + 1)
                if b:
                    act.wait_ge(s["ro_p"], b)
                copy(v3[:].rearrange("p t d -> p (t d)"), PS[:, 4, 0:S]).then_inc(s["v3_s"], 1)
            for b in range(B):
                ln_yT(7, b)
                if b:
                    act.wait_ge(s["f3_p"], b)
                for c in range(CH):
                    act.wait_ge(s["h3_p"], 2 * b + c // 2 + 1)
                    last = act.activation(hg[:, c, :], PS[:, 2 + c // 2, (c % 2) * S:(c % 2 + 1) * S], ACT.Gelu,
                                          bias=f1bc[:, c:c + 1])
                    if c % 2:
                        last.then_inc(s["h3_s"], 1)

        @block.vector
        def _(v):
            own = Steps(v, s["own_dve"])

            def stats(L, b):
                if L:
                    v.wait_ge(s[f"x{L - 1}"], b + 1)
                for t in range(T):
                    own(v.bn_stats(st6[:, b * T + t, :], x[:, b * T + t, :]))
                own.settle()
                for t in range(T):
                    own(v.bn_aggr(mv[:, b * T + t, :], st6[:, b * T + t, :]))
                own.settle()
                v.tensor_scalar(veps[:, tiles(b)], mv[:, tiles(b), 1], EPS, None, ALU.add
                                ).then_inc(s["ln_mv"], 1)

            def norm(L, b):
                v.wait_ge(s["ln_rstd"], nth(L, b))
                for t in range(T):
                    n = b * T + t
                    ins = v.tensor_scalar(y[:, n, :], x[:, n, :], mv[:, n, 0:1], rstd[:, n:n + 1],
                                          ALU.subtract, ALU.mult)
                ins.then_inc(s["ln_y"], 1)

            def add(L, b, src, g):
                v.scalar_tensor_tensor(out=x[:, tiles(b), :].rearrange("p t d -> p (t d)"), in0=src,
                                       scalar=gate[:, g:g + 1],
                                       in1=x[:, tiles(b), :].rearrange("p t d -> p (t d)"),
                                       op0=ALU.mult, op1=ALU.add).then_inc(s[f"x{L}"], 1)

            v.wait_ge(s["ld_x"], 16)
            for b in range(B):
                stats(0, b)
            own.settle()
            v.wait_ge(s["ld_w0"], 112)
            for dst, src in ((wqp, wq), (wkp, wk)):
                for j in range(NJ):
                    own(v.tensor_copy(dst[:, j, :].rearrange("p (i n d) -> p i n d", i=NI, n=4),
                                      src[:, j * NI * HD:(j + 1) * NI * HD].rearrange("p (i d) -> p i d", i=NI)
                                      .unsqueeze(2).broadcast_to([P, NI, 4, HD])))
            own(v.tensor_copy(sel[:], selc[:].unsqueeze(2).broadcast_to([P, NJ, P])))
            own.settle()
            v.sem_inc(s["cst_v"], 1)
            v.wait_ge(s["cst"], 7)
            v.tensor_copy(identb[:], ident[:]).then_inc(s["cst_v"], 1)
            v.tensor_copy(iot[:], ioti[:]).then_inc(s["cst_v"], 1)
            v.tensor_copy(thr[:], thri[:]).then_inc(s["cst_v"], 1)
            v.tensor_copy(modt[:].rearrange("p a b -> p (a b)"), modi[:]).then_inc(s["cst_v"], 1)
            v.wait_ge(s["cst_v"], 5)
            own(v.tensor_copy(iotr[:], iot[:, 1:S + 1].unsqueeze(1).broadcast_to([P, R, S])))
            for b in range(B):
                norm(0, b)

            def attended(b):
                v.wait_ge(s["pv_p"], b + 1)
                pv = PS[:, 4, 0:T * HEADS * (HD + 1)].rearrange("p (n c) -> p n c", c=HD + 1)
                own(v.reciprocal(rden[:], pv[:, :, HD]))
                own.settle()
                if b:
                    v.wait_ge(s["oT_p"], b)
                v.tensor_tensor(o[:].rearrange("p t (h d) -> p (t h) d", d=HD), pv[:, :, 0:HD],
                                rden[:].unsqueeze(2).broadcast_to([P, T * HEADS, HD]), ALU.mult
                                ).then_inc(s["o_n"], 1)

            def projected_out(b):
                v.wait_ge(s["at_p"], b + 1)
                v.wait_ge(s["gates"], 1)
                add(0, b, PS[:, 6, 0:S], 0)

            def maxima(b, u):
                jp, t = divmod(u, T)
                at_ = 4 * (u % 2)
                v.wait_ge(s["s_p"], 4 * b + u + 1)
                if b and u == 0:
                    v.wait_ge(s["qm_p"], b)
                v.tensor_reduce(mneg[:, t, :].rearrange("p (i c) -> p i c", i=NI)[:, :, 4 * jp:4 * jp + 4:2],
                                PS[:, at_:at_ + 4, :].rearrange("p i (j k) -> p i j k", j=2), AX, ALU.max,
                                negate=True).then_inc(s["s_m"], 1)

            for b in range(B):
                for j in range(NJ):
                    v.wait_ge(s["q0_h"], NJ * b + j + 1)
                    if b:
                        v.wait_ge(s["st_p"], 4 * b)
                    for n in range(2):
                        ins = v.scalar_tensor_tensor(out=qk[:, j, n, :], in0=qkh[:, j, n, :].bitcast(F32),
                                                     scalar=spl[:, n:n + 1], in1=PS[:, j, n * S:(n + 1) * S],
                                                     op0=ALU.mult, op1=ALU.add)
                    ins.then_inc(s["q0_s"], 1)
                if b:
                    attended(b - 1)
                maxima(b, 0)
                if b:
                    projected_out(b - 1)
                for u in range(1, 4):
                    maxima(b, u)
                v.wait_ge(s["s_m"], 4 * (b + 1))
                mp = mneg.rearrange("p t (i c) -> p (t i) c", i=NI)
                v.tensor_copy(mp[:, :, 1:2 * NJ:2], mp[:, :, 0:2 * NJ:2]).then_inc(s["mn_s"], 1)
                v.wait_ge(s["qm_h"], b + 1)
                v.scalar_tensor_tensor(out=mT[:], in0=mTh.bitcast(F32), scalar=spl[:, 2:3], in1=PS[:, 0, 0:S],
                                       op0=ALU.mult, op1=ALU.add).then_inc(s["qm_s"], 1)
                if b:
                    stats(1, b - 1)
                    norm(1, b - 1)
                else:
                    v.wait_ge(s["ld_ads"], 32 * KA)
                    v.wait_ge(s["ld_mix"], 32)
                    own(v.tensor_scalar(weff[:], ads[:, 0, :], wB[:, 0:1], None, ALU.mult))
                    own(v.tensor_scalar(wrow[:], ones[0:KA, :], wc[:, 0:1], None, ALU.mult))
                    for k in range(1, KA):
                        own.settle()
                        own(v.scalar_tensor_tensor(out=weff[:], in0=ads[:, k, :], scalar=wB[:, k:k + 1],
                                                   in1=weff[:], op0=ALU.mult, op1=ALU.add))
                    own.settle()
                    v.sem_inc(s["weff_s"], 1)
            attended(B - 1)
            projected_out(B - 1)
            stats(1, B - 1)
            norm(1, B - 1)
            for b in range(B):
                v.wait_ge(s["f0_p"], b + 1)
                add(1, b, PS[:, 2 + b % 2, 0:S], 4)
                stats(2, b)
                norm(2, b)
            v.wait_ge(s["cxT_s"], 2)
            v.wait_ge(s["c3_s"], 1)
            cf = cxT[:].rearrange("p b s -> p (b s)")
            v.tensor_tensor(sqc.rearrange("p b s -> p (b s)"), cf, cf, ALU.mult).then_inc(s["sqc_s"], 1)
            for b in range(B):
                v.wait_ge(s["ln_yT"], nth_T(2, b))
                if b:
                    v.wait_ge(s["aabb_p"], b)
                v.tensor_tensor(sq[:], yT[:, b, :], yT[:, b, :], ALU.mult).then_inc(s["sq_s"], 1)
            v.wait_ge(s["aabb_p"], B)
            own(v.tensor_copy(aab[:], PS[:, 6, 0:S]))
            own(v.tensor_copy(bbk[:], PS[:, 6, S:S + W]))
            own.settle()
            v.sem_inc(s["aabb_s"], 1)
            for c in range(W):
                own(v.tensor_scalar(dsum[:, c, :], aab[:], bbk[:, c:c + 1], None, ALU.add))
            own.settle()
            for c in range(0, W, 2):
                d2 = dsum[:, c:c + 2, :].rearrange("p c s -> p (c s)")
                own(v.scalar_tensor_tensor(out=d2, in0=PS[:, 2 + c // 2, :], scalar=-2.0, in1=d2,
                                           op0=ALU.mult, op1=ALU.add))
            own.settle()
            df = dsum.rearrange("p c s -> p (c s)")
            v.tensor_scalar(df, df, 0.0, None, ALU.max).then_inc(s["dsq"], 1)
            v.wait_ge(s["ld_l3"], 112)
            own(v.tensor_reduce(fal[:, 0:CH], f1[:], AX, ALU.add, apply_absolute_value=True))
            own(v.tensor_reduce(fal[:, CH:CH + 1], f2[:], AX, ALU.add, apply_absolute_value=True))
            own.settle()
            own(v.tensor_scalar(fal[:, 0:CH], fal[:, 0:CH], 1.0 / D, None, ALU.mult))
            own(v.tensor_scalar(fal[:, CH:CH + 1], fal[:, CH:CH + 1], 1.0 / FF, None, ALU.mult))
            w2v = f2[:].rearrange("p (c n) -> p c n", c=CH)
            for dst, src in ((fs, f1[:]), (ft, w2v)):
                own(v.tensor_scalar(dst[:], src, 0.0, None, ALU.is_gt))
                own(v.tensor_scalar(neg, src, 0.0, None, ALU.is_lt))
                own.settle()
                own(v.tensor_tensor(dst[:], dst[:], neg, ALU.subtract))
                own.settle()
            for c in range(CH):
                own(v.scalar_tensor_tensor(out=fs[:, c, :], in0=fs[:, c, :], scalar=fal[:, c:c + 1], in1=f1[:, c, :],
                                           op0=ALU.mult, op1=ALU.subtract))
            own(v.scalar_tensor_tensor(out=ft[:].rearrange("p c n -> p (c n)"),
                                       in0=ft[:].rearrange("p c n -> p (c n)"), scalar=fal[:, CH:CH + 1],
                                       in1=f2[:], op0=ALU.mult, op1=ALU.subtract))
            own.settle()
            own(v.tensor_tensor(fs, fs, f1[:], ALU.add))
            own(v.tensor_tensor(ft[:], ft[:], w2v, ALU.add))
            own.settle()
            v.sem_inc(s["fb_s"], 1)
            v.wait_ge(s["init_r"], 1)
            n_dp = HALF * 2 * G + HALF
            shift = [0] + list(range(LANES - 1))
            with v.Fori(0, ITERS) as it:
                for h in range(2):
                    k = [0]

                    def step(ins):
                        k[0] += 1
                        ins.then_inc(s["own_dp"], 1)

                    def settle():
                        v.wait_ge(s["own_dp"], (2 * it + h) * n_dp + k[0])

                    v.wait_ge(s[f"d_r{h}"], (it + 1) * 16)
                    v.wait_ge(s["codes"], 2 * it + h + 1)
                    for st in range(HALF):
                        r0 = st * G
                        prev = Rw[:, 1 - h, HS, :] if st == 0 else Rw[:, h, r0, :]
                        edge = Rw[:, 1 - h, HS - 1:HS + 1, W] if st == 0 else Rw[:, h, r0 - 1:r0 + 1, W]
                        for g in range(G):
                            if g:
                                prev = Rw[:, h, r0 + g, :]
                            step(v.tensor_tensor(mb[:, g, 1:W1C], prev[:, 0:W], prev[:, 1:W1C], ALU.min))
                            if not g:
                                step(v.stream_shuffle(mb[:, :, 0], edge, shift))
                            settle()
                            ins = v.tensor_tensor_scan(Rw[:, h, r0 + g + 1, :], mb[:, g, :], Dw[:, h, r0 + g, :],
                                                       BIG, ALU.min, ALU.add)
                            if st == HALF - 1 and g == G - 1:
                                ins.then_inc(s["rows_g"], 1)
                                v.wait_ge(s["rows_g"], 2 * it + h + 1)
                            else:
                                step(ins)
                                settle()
                        if st == 0:
                            step(v.tensor_copy(Rw[:, h, 0, :], Rw[:, 1 - h, HS, :]))
                    assert k[0] == n_dp, k[0]
            v.wait_ge(s["cs_r"], 16)
            own(v.tensor_scalar(pen, Cs, 1.0, FAR, ALU.min, ALU.mult))
            own(v.tensor_scalar(msk, Cs, -FAR, 1.5 * FAR, ALU.mult, ALU.add))
            own.settle()
            own(v.tensor_tensor(xn, pen, iot[:, 0:S].unsqueeze(1).broadcast_to([P, R, S]), ALU.add))
            own.settle()
            own(v.tensor_tensor(xn, xn, iotr[:], ALU.min))
            own(v.tensor_tensor_scan(Ac.rearrange("p r j -> p (r j)"), msk.rearrange("p r j -> p (r j)"),
                                     iotr[:].rearrange("p r j -> p (r j)"), 0.0, ALU.max, ALU.min))
            own.settle()
            own(v.tensor_tensor_scan(Nc.rearrange("p r j -> p (r j)"), msk.rearrange("p r j -> p (r j)"),
                                     xn.rearrange("p r j -> p (r j)"), 0.0, ALU.max, ALU.min))
            own(v.memset(Gp[:, :, 0:1], 0.0))
            own.settle()
            own(v.tensor_copy(Gp[:, 0, 1:S + 1], Nc[:, 0, :]))
            own.settle()
            for r in range(1, R):
                g0, g1 = (r - 1) % 2, r % 2
                own(v.tensor_tensor(Gx[:], Gp[:, g0, 0:S], pen[:, r, :], ALU.add))
                own.settle()
                own(v.tensor_tensor(Gx[:], Gx[:], Gp[:, g0, 1:S + 1], ALU.min))
                own.settle()
                to = Gb[:] if r == R - 1 else Gp[:, g1, 1:S + 1]
                ins = v.tensor_tensor_scan(to, msk[:, r, :], Gx[:], 0.0, ALU.max, ALU.min)
                if r == R - 1:
                    ins.then_inc(s["g_s"], 1)
                else:
                    own(ins)
                    own.settle()

            def lookup(lanes, at_, table, col, to):
                own(v.scalar_tensor_tensor(out=junk[0:lanes, :], in0=iot[0:lanes, 1:S + 1], scalar=at_[:, col],
                                           in1=table, op0=ALU.is_equal, op1=ALU.mult, accum_out=to))

            v.memset(ech[:, STRIPS - 1:STRIPS], float(S - 1)).then_inc(s["own_dve"], 1)
            own.n += 1
            own.settle()
            v.wait_ge(s["g_r"], 16)
            for st in range(STRIPS - 1, 0, -1):
                lookup(B, ech, Ge[:, st, :], slice(st, st + 1), ech[:, st - 1:st])
                own.settle()
            v.sem_inc(s["e_s"], 1)
            v.wait_ge(s["e_r"], 16)
            for r in range(R - 1, -1, -1):
                lookup(P, el, Nc[:, r, :], slice(r + 1, r + 2), el[:, r:r + 1])
                own.settle()
            for r in range(R):
                lookup(P, el, Ac[:, r, :], slice(r + 1, r + 2), al[:, r:r + 1])
                own.settle()
            for r in range(R):
                own(v.tensor_scalar(xn[:, r, :], iot[:, 1:S + 1], el[:, r + 1:r + 2], None, ALU.is_le))
            own.settle()
            for r in range(R):
                own(v.scalar_tensor_tensor(out=Pm[:, r, :], in0=iot[:, 1:S + 1], scalar=al[:, r:r + 1],
                                           in1=xn[:, r, :], op0=ALU.is_ge, op1=ALU.mult))
            own.settle()
            v.sem_inc(s["p_s"], 1)
            for b in range(B):
                v.wait_ge(s["ex_p"], b + 1)
                add(2, b, PS[:, 2 + b, 0:S], 1)
                stats(3, b)
                norm(3, b)
            for b in range(B):
                v.wait_ge(s["ln_y"], nth(3, b))
                own(v.tensor_tensor(ssum[:, 0, :], y[:, tiles(b), 0], y[:, tiles(b), 1], ALU.add))
                own.settle()
                own(v.tensor_scalar(ssum[:, 1, :], ssum[:, 0, :], -1.0, None, ALU.mult))
                own.settle()
                thb = thr[:].unsqueeze(1).broadcast_to([P, T, 17])
                own(v.tensor_tensor(cmp[:, 0:T, :], thb, ssum[:, 0, :].unsqueeze(2).broadcast_to([P, T, 17]),
                                    ALU.is_le))
                own(v.tensor_tensor(cmp[:, T:2 * T, :], thb, ssum[:, 1, :].unsqueeze(2).broadcast_to([P, T, 17]),
                                    ALU.is_gt))
                own.settle()
                own(v.tensor_reduce(cnt[:].rearrange("p a t -> p (a t)"), cmp[:], AX, ALU.add))
                own.settle()
                own(v.tensor_tensor(cnts[:], cnt[:, 0, :], cnt[:, 1, :], ALU.add))
                own.settle()
                for t in range(T):
                    own(v.tensor_scalar(hit[:, t], modt[:], cnts[:, t:t + 1], None, ALU.is_equal))
                own.settle()
                own(v.tensor_reduce(oh[:].rearrange("p t e -> p (t e)"),
                                    hit[:].rearrange("p t e m -> p (t e) m"), AX, ALU.add))
                own.settle()
                if b:
                    v.wait_ge(s["wtT_p"], b)
                own(v.tensor_tensor(wts[:], oh[:, :, 0:E1], oh[:, :, 1:E1 + 1], ALU.add))
                own.settle()
                v.tensor_scalar(wts[:], wts[:], 0.5, None, ALU.mult).then_inc(s["wt_s"], 1)
                v.wait_ge(s["wt_s"], b + 1)
                v.wait_ge(s["b2_p"], b + 1)
                ab = acc[:, b % 2]
                v.tensor_copy(ab.rearrange("p t d -> p (t d)"), PS[:, 0, 0:S]).then_inc(s["b2_s"], 1)
                v.wait_ge(s["b2_s"], b + 1)
                for e in range(E1):
                    n = E1 * b + e
                    v.wait_ge(s["mm2_p"], n + 1)
                    if n:
                        v.wait_ge(s["mm2_s"], n)
                    for t in range(T):
                        ins = v.scalar_tensor_tensor(out=ab[:, t, :], in0=PS[:, 6 + n % 2, t * D:(t + 1) * D],
                                                     scalar=wts[:, t, e:e + 1], in1=ab[:, t, :],
                                                     op0=ALU.mult, op1=ALU.add)
                    ins.then_inc(s["mm2_s"], 1)
                v.wait_ge(s["mm2_s"], E1 * (b + 1))
                add(3, b, ab.rearrange("p t d -> p (t d)"), 5)
            v.wait_ge(s["padded"], 3)
            v.wait_ge(s["ld_tab"], 64)
            for b in range(B):
                stats(4, b)
                norm(4, b)
                v.wait_ge(s["ln_y"], nth(4, b))
                for t in range(T):
                    n = b * T + t
                    for qb in range(4):
                        kk = 4 * (qb + 1)
                        q4 = y[:, n, 32 * qb:32 * (qb + 1)].rearrange("p (q d) -> p q d", d=HD)
                        kv = cx[:, n, 0:kk * HD].rearrange("p (k d) -> p k d", d=HD)
                        pr = prod[:, 0:4 * kk * HD].rearrange("p (q k d) -> p q k d", q=4, d=HD)
                        own(v.tensor_tensor(pr, q4.unsqueeze(2).broadcast_to([P, 4, kk, HD]),
                                            kv.unsqueeze(1).broadcast_to([P, 4, kk, HD]), ALU.mult))
                        own.settle()
                        own(v.tensor_reduce(sc[:, t, 4 * qb:4 * qb + 4, 0:kk], pr, AX, ALU.add))
                        own.settle()
                for t in range(T):
                    own(v.scalar_tensor_tensor(out=sc2[:, t].rearrange("p q k -> p (q k)"),
                                               in0=sc[:, t].rearrange("p q k -> p (q k)"), scalar=HD ** -0.5,
                                               in1=cmask[:].rearrange("p q k -> p (q k)"),
                                               op0=ALU.mult, op1=ALU.add))
                own.settle()
                s2f = sc2[:].rearrange("p t q k -> p (t q) k")
                own(v.tensor_reduce(mx[:], s2f, AX, ALU.max))
                own.settle()
                bc = [P, T * HEADS, HEADS]
                v.tensor_tensor(s2f, s2f, mx[:].unsqueeze(2).broadcast_to(bc), ALU.subtract
                                ).then_inc(s["sc_s"], 1)
                v.wait_ge(s["sc_e"], b + 1)
                own(v.tensor_reduce(sm[:], s2f, AX, ALU.add))
                own.settle()
                own(v.reciprocal(sm[:], sm[:]))
                own.settle()
                own(v.tensor_tensor(s2f, s2f, sm[:].unsqueeze(2).broadcast_to(bc), ALU.mult))
                own.settle()
                ab = acc[:, b % 2]
                for t in range(T):
                    n = b * T + t
                    for qb in range(4):
                        kk = 4 * (qb + 1)
                        pr = prod[:, 0:4 * kk * HD].rearrange("p (q d k) -> p q d k", q=4, d=HD)
                        kv = cx[:, n, 0:kk * HD].rearrange("p (k d) -> p d k", d=HD)
                        at_ = sc2[:, t, 4 * qb:4 * qb + 4, 0:kk]
                        own(v.tensor_tensor(pr, at_.unsqueeze(2).broadcast_to([P, 4, HD, kk]),
                                            kv.unsqueeze(1).broadcast_to([P, 4, HD, kk]), ALU.mult))
                        own.settle()
                        own(v.tensor_reduce(ab[:, t, 32 * qb:32 * (qb + 1)].rearrange("p (q d) -> p q d", d=HD),
                                            pr, AX, ALU.add))
                        own.settle()
                add(4, b, ab.rearrange("p t d -> p (t d)"), 2)
            for b in range(B):
                stats(5, b)
                norm(5, b)
                v.wait_ge(s["lg_p"], b + 1)
                lp = PS[:, 1, 0:T * E2].rearrange("p (t e) -> p t e", e=E2)
                own(v.tensor_reduce(lmx[:], lp, AX, ALU.max))
                own.settle()
                v.tensor_tensor(lg[:], lp, lmx[:].unsqueeze(2).broadcast_to([P, T, E2]), ALU.subtract
                                ).then_inc(s["lg_s"], 1)
                v.wait_ge(s["lg_e"], b + 1)
                own(v.tensor_reduce(lsm[:], lg[:], AX, ALU.add))
                own.settle()
                own(v.reciprocal(lsm[:], lsm[:]))
                own.settle()
                own(v.tensor_tensor(lg[:], lg[:], lsm[:].unsqueeze(2).broadcast_to([P, T, E2]), ALU.mult))
                own.settle()
                v.tensor_scalar(gm[:], lg[:], 0.5, None, ALU.is_gt).then_inc(s["gm_s"], 1)
                v.wait_ge(s["gm_s"], b + 1)
                v.wait_ge(s["eb_p"], b + 1)
                ab = acc[:, b % 2]
                own(v.tensor_copy(ab.rearrange("p t d -> p (t d)"), PS[:, 7, 0:S]))
                own.settle()
                for e in range(E2):
                    for t in range(T):
                        own(v.scalar_tensor_tensor(out=ab[:, t, :],
                                                   in0=PS[:, 2 + 2 * t + e // 4, (e % 4) * D:(e % 4 + 1) * D],
                                                   scalar=gm[:, t, e:e + 1], in1=ab[:, t, :],
                                                   op0=ALU.mult, op1=ALU.add))
                    own.settle()
                add(5, b, ab.rearrange("p t d -> p (t d)"), 6)
            for b in range(B):
                stats(6, b)
                norm(6, b)
                v.wait_ge(s["k3_p"], b + 1)
                for n in range(2):
                    own(v.tensor_tensor(rqk[:, n, :], PS[:, 2 + n, 0:S], xcos[:, n, :], ALU.mult))
                    own(v.tensor_tensor(rtmp, PS[:, 2 + n, S:2 * S], xsin[:, n, :], ALU.mult))
                    own.settle()
                    ins = v.tensor_tensor(rqk[:, n, :], rqk[:, n, :], rtmp, ALU.add)
                    if n:
                        ins.then_inc(s["k3_s"], 1)
                    else:
                        own(ins)
                        own.settle()
                v.wait_ge(s["rt_p"], b + 1)
                for t in range(T):
                    ins = v.tensor_tensor(ret[:, t, :], PS[:, 5, t * S:(t + 1) * S], decay[:, t, :], ALU.mult)
                ins.then_inc(s["rt_s"], 1)
                v.wait_ge(s["ro_p"], b + 1)
                add(6, b, PS[:, 6, 0:S], 3)
            for b in range(B):
                stats(7, b)
                norm(7, b)
            for b in range(B):
                v.wait_ge(s["f3_p"], b + 1)
                add(7, b, PS[:, 7, 0:S], 7)


_INS = ["x", "ctx_1024", "g_xattn", "g_ffn", "L0_xattn_W_q", "L0_xattn_W_k", "L0_xattn_W_v", "L0_xattn_W_o",
        "L0_xattn_b_o", "L0_ffn_W", "L0_ffn_b", "L0_ffn_ids", "L0_ffn_weights", "L1_ffn_W1", "L1_ffn_b1",
        "L1_ffn_W2", "L1_ffn_b2", "L2_ffn_Wr", "L2_ffn_br", "L2_ffn_We", "L2_ffn_be", "L3_xattn_Wq",
        "L3_xattn_Wk", "L3_xattn_Wv", "L3_ffn_w1", "L3_ffn_b1", "L3_ffn_w2", "L3_ffn_b2"]


def tables():
    f = np.float32
    base = (np.arange(0, D, 2, dtype=f) + f(0.4 * D)) / f(1.4 * D)
    pos = np.arange(0, S, dtype=f)
    scale = (base[None, :] ** (pos[:, None] / f(512.0))).astype(f)
    freqs = (f(1.0) / f(10000.0) ** (np.arange(D // 2, dtype=f) / f(D // 2))).astype(f)
    arg = (pos[:, None] * freqs[None, :]).astype(f)
    sin, cos = np.sin(arg), np.cos(arg)
    both = lambda m: np.repeat(m, 2, axis=-1).T
    inv = f(1.0) / scale
    t_cos = np.stack([both(cos * scale), both(cos * inv)], 1).astype(f)
    t_sin = np.stack([both(sin * scale), both(sin * inv)], 1).astype(f)
    q, k = np.arange(S)[None, :], np.arange(S)[:, None]
    decay = np.where(q >= k, np.float64(0.96875) ** np.maximum(q - k, 0), 0.0).astype(f)
    decay = decay.reshape(T, P, S).transpose(1, 0, 2)
    causal = np.where(np.tril(np.ones((HEADS, HEADS), bool)), 0.0, NEG).astype(f)
    causal = np.broadcast_to(causal, (P, HEADS, HEADS))
    p = np.arange(P)
    split = -np.stack([p // HD % 2, p // (2 * HD) % 2, p % 2], 1).astype(f)
    sel = (p[:, None] % 32 // 2 == np.arange(NJ)[None, :]).astype(f)
    return {"t_split": split, "t_sel": sel, "t_cos": t_cos, "t_sin": t_sin, "t_decay": decay, "t_causal": causal}


def kernel(**inputs):
    import numpy as _np
    import concourse.bacc as _bacc
    from concourse import mybir as _mybir
    from concourse.bass_utils import run_bass_kernel_spmd as _run

    nc = _bacc.Bacc("TRN2", target_bir_lowering=False, num_devices=1)
    arrays, args = {}, {}
    data = {n: inputs[n] for n in _INS}
    data.update(tables())
    for name, val in data.items():
        arr = _np.ascontiguousarray(val)
        arrays[f"in_{name}"] = arr
        args[name] = nc.dram_tensor(f"in_{name}", arr.shape, _mybir.dt.from_np(arr.dtype), kind="ExternalInput").ap()
    out = nc.dram_tensor("out_0", (B, S, D), _mybir.dt.float32, kind="ExternalOutput").ap()
    build(nc, args, out)
    r = _run(nc, [arrays], core_ids=[0])
    return r.results[0]["out_0"]
```

```python
from contextlib import ExitStack

import numpy as np
import concourse.bass as bass
from concourse import mybir

F32 = mybir.dt.float32
F32R = mybir.dt.float32r
BF16 = mybir.dt.bfloat16
I32 = mybir.dt.int32
ALU = mybir.AluOpType
ACT = mybir.ActivationFunctionType
AX = mybir.AxisListType.X

B, S, D = 4, 256, 128
P = 128
T = S // P
NT = B * T
HEADS, HD = 16, 8
NJ, NI = 4, 4
E1, FF = 8, 512
CH = FF // P
E2 = 8
NA, KA = 32, 8
EPS = 1e-5
BIG = 1e30
NEG = -1e18

LANES = 32
W = S // LANES
G = 2
W1C = W + 1
LAGMAX = G * (LANES - 1)
HALF = 16
HS = HALF * G
SLOTS = -(-(S + LAGMAX) // (2 * HS)) * 2 * HS
ITERS = SLOTS // (2 * HS)
ROWS = LAGMAX + SLOTS
R = 8
STRIPS = S // R
FAR = 1e4


PIPE = [(L, n - (L - 5)) for n in range(B + 2) for L in (5, 6, 7) if 0 <= n - (L - 5) < B]


class Steps:

    def __init__(self, eng, sem):
        self.eng, self.sem, self.n = eng, sem, 0

    def __call__(self, ins):
        self.n += 1
        ins.then_inc(self.sem, 1)

    def settle(self, but=0):
        self.eng.wait_ge(self.sem, self.n - but)


def build(nc, a, out):
    with ExitStack() as ctx:
        def sb(name, shape, dt=F32):
            return ctx.enter_context(nc.sbuf_tensor(name, shape, dt))

        def sem(name):
            return ctx.enter_context(nc.semaphore(name))

        with ExitStack() as l0:
            def early(name, shape):
                return l0.enter_context(nc.sbuf_tensor(name, shape, F32R))

            qk = early("qk", [P, NJ, 2, S]); mT = early("mT", [P, S]); sel = early("sel", [P, NJ, P])
        cd = sb("cd", [P, 6, HS, W])
        Cw = sb("Cw", [P, SLOTS * W], BF16)
        x = sb("x", [P, NT, D])
        cx = sb("cx", [P, NT, D])
        cxT = sb("cxT", [P, B, S])
        y = sb("y", [P, NT, D])
        yT = sb("yT", [P, B, S])
        st6 = sb("st6", [P, NT, 6])
        mv = sb("mv", [P, NT, 2])
        veps = sb("veps", [P, NT])
        rstd = sb("rstd", [P, NT])
        halfc = sb("halfc", [P, NT])
        gate = sb("gate", [P, 8])
        ident = sb("ident", [P, P])
        identb = sb("identb", [P, P], BF16)
        ones = sb("ones", [P, P])
        wq = sb("wq", [P, D]); wk = sb("wk", [P, D]); wv = sb("wv", [P, D]); wo = sb("wo", [P, D])
        wqp = sb("wqp", [P, NJ, P]); wkp = sb("wkp", [P, NJ, P])
        spl = sb("spl", [P, 3]); selc = sb("selc", [P, NJ])
        rows = sb("rows", [1, 2, D])
        Z = sb("Z", [P, 4 * R * S])

        def part(at, *shape):
            n = int(np.prod(shape))
            names = "abcd"[:len(shape)]
            v = Z[:, at:at + n]
            if len(shape) == 1:
                return v
            return v.rearrange(f"p ({' '.join(names)}) -> p {' '.join(names)}", **dict(zip(names, shape)))

        qkh = part(0, NJ, 2, S).bitcast(F32R)
        mneg = part(2 * NJ * S, T, P)
        mTh = part(2 * NJ * S + T * P, S).bitcast(F32R)
        Ge = Z[0:B, 0:STRIPS * S // 2].bitcast(BF16).rearrange("p (n s) -> p n s", n=STRIPS)
        rq, ret = part(0, S), part(2 * S, T, S)
        rtmp = part(S, S)
        hg = part(6 * S, CH, S)
        pen, xn, msk, Nc = (part(n * R * S, R, S) for n in range(4))
        hT = part(0, 2 * CH, S)
        uT = part(4 * NJ * S, NJ, S)
        vaug = part(5 * NJ * S, T, HEADS, 32)
        big = sb("big", [P, T * HEADS * S])
        pT = big[:].rearrange("p (t h s) -> p t h s", t=T, h=HEADS)
        w1 = big[:, 0:E1 * FF].rearrange("p (e f) -> p e f", e=E1)
        w2 = big[:, E1 * FF:2 * E1 * FF].rearrange("p (e c d) -> p e c d", e=E1, c=CH)
        rden = sb("rden", [P, T * HEADS])
        o = sb("o", [P, T, D])
        oT = sb("oT", [P, S])
        ads = sb("ads", [P, KA, D])
        adb = sb("adb", [KA, D])
        wB = sb("wB", [P, KA]); wc = sb("wc", [KA, 1]); wrow = sb("wrow", [KA, P])
        v3 = ads[:].rearrange("p (b t) d -> p b t d", t=T)
        kturn = [w[:].rearrange("p (b t) n -> p b (t n)", t=T) for w in (wqp, wkp)]
        rk = [kturn[b // 2][:, b % 2, :] for b in range(B)]
        weff = sb("weff", [P, D]); weffT = sb("weffT", [P, D])
        idsb = sb("idsb", [1, KA], I32)
        sq = sb("sq", [P, S])
        Y = sb("Y", [P, R * S])
        sqc = Y[:, 0:B * S].rearrange("p (b s) -> p b s", b=B)
        crem = Y[:, B * S:2 * B * S]
        dsum = Y[:].rearrange("p (c s) -> p c s", c=W)
        Ac = Y[:].rearrange("p (r s) -> p r s", r=R)
        aab = sb("aab", [P, S]); bbk = sb("bbk", [P, W])
        Dun = sb("Dun", [P, ROWS, W1C])
        Dw = sb("Dw", [P, 2, HS, W1C])
        Rw = sb("Rw", [P, 2, HS + 1, W1C])
        mb = sb("mb", [P, G, W1C])
        late = [Dun[:].rearrange("p r c -> p (r c)")[:, n * R * S // 2:(n + 1) * R * S // 2].bitcast(BF16)
                for n in range(3)]
        Cl = late[0].rearrange("p (s w) -> p s w", w=W)
        CT = late[1].rearrange("p (b t s) -> p b t s", t=T, b=B)
        Cs = late[2].rearrange("p (r s) -> p r s", r=R)
        Pi = late[0].rearrange("p (b t s) -> p b t s", t=T, b=B)
        Pm = late[1].rearrange("p (r s) -> p r s", r=R)
        prod2 = Dun[:].rearrange("p r c -> p (r c)")[:, R * S:R * S + 4 * HEADS * HD]
        iot = sb("iot", [P, S + 1]); ioti = sb("ioti", [P, S + 1], I32)
        iotr = sb("iotr", [P, R, S])
        Gp = sb("Gp", [P, 2, S + 1])
        Gx = sb("Gx", [P, S])
        ech = sb("ech", [B, STRIPS])
        el = sb("el", [P, R + 1]); al = sb("al", [P, R])
        junk = sb("junk", [P, 2, S])
        Gb = sb("Gb", [P, S], BF16)
        c3 = sb("c3", [P, 3, NT * D], BF16)
        b1r = sb("b1r", [E1 * CH, P]); b1c = sb("b1c", [P, E1 * CH])
        b2r = sb("b2r", [E1, D])
        thr = sb("thr", [P, 17]); modt = sb("modt", [P, 9, 7]); modi = sb("modi", [P, 63], I32)
        thri = sb("thri", [P, 17], I32)
        ssum = sb("ssum", [P, 2, T]); cmp = sb("cmp", [P, 2 * T, 17]); cnt = sb("cnt", [P, 2, T])
        cnts = sb("cnts", [P, T]); hit = sb("hit", [P, T, 9, 7]); oh = sb("oh", [P, T, 9])
        wts = sb("wts", [P, 2, T, E1]); wtsT = sb("wtsT", [E1, S])
        acc = sb("acc", [P, 2, T, D])
        prod = sb("prod", [P, 4 * HEADS * HD])
        sc = sb("sc", [P, T, HEADS, HEADS]); sc2 = sb("sc2", [P, T, HEADS, HEADS])
        cmask = sb("cmask", [P, HEADS, HEADS])
        mx = sb("mx", [P, T * HEADS]); sm = sb("sm", [P, T * HEADS])
        wrT = sb("wrT", [P, E2]); wrr = sb("wrr", [E2, D]); brr = sb("brr", [1, E2])
        We = sb("We", [P, E2, D]); WeT = sb("WeT", [P, E2, D]); ber = sb("ber", [E2, D])
        lg = sb("lg", [P, T, E2]); lmx = sb("lmx", [P, T]); lsm = sb("lsm", [P, T])
        gm = sb("gm", [P, T, E2]); gmT = sb("gmT", [E2, S])
        w3 = sb("w3", [P, 3, D]); w3T = sb("w3T", [P, 5, D])
        xcos = sb("xcos", [P, 2, S]); xsin = sb("xsin", [P, 2, S]); decay = sb("decay", [P, T, S])
        f1 = sb("f1", [P, CH, D]); f2 = sb("f2", [P, FF]); fs = prod[:].rearrange("p (c d) -> p c d", c=CH); ft = sb("ft", [P, CH, D])
        fal = sb("fal", [P, CH + 1])
        neg = acc[:].rearrange("p a t d -> p (a t) d")
        f1T = sb("f1T", [P, CH, P]); f2T = sb("f2T", [P, CH, D])
        f1br = sb("f1br", [CH, P]); f1bc = sb("f1bc", [P, CH])
        PS = ctx.enter_context(nc.psum_tensor("PS", [P, 8, 512], F32))

        dD = nc.dram_tensor("dD", (P, ROWS * W1C), F32, kind="Internal").ap()
        dC = nc.dram_tensor("dC", (P, SLOTS * W), BF16, kind="Internal").ap()
        dCr = nc.dram_tensor("dCr", (B, S, S), BF16, kind="Internal").ap()
        dP = nc.dram_tensor("dP", (B, S, S), BF16, kind="Internal").ap()

        names = """ln_mv ln_rstd ln_y ln_T ln_yT ld_x ld_cx ld_w0 ld_gate ld_ids ld_ads ld_mix ld_moe ld_l2 ld_l3 ld_tab cst cst_v
            own_dve own_dp own_pool turns init_r lg_s gates padded padq
            cxT_p cxT_s q0_p q0_h q0_s v_p v_s s_p s_m mn_s qm_p qm_h qm_s st_p st_e pv_p uT_s un_p o_n oT_p oT_s at_p x0
            weff_s weffT_p weffT_s f0_p x1
            sq_s sqc_s aabb_p aabb_s ab_p dsq d_s d_w d_r0 d_r1 rows_g codes codes_w cl_r clT_p ct_s ct_w cs_r
            g_s g_r e_s e_r p_s p_w p_r ex_p x2 c3_s
            b1_p b1_s wt_s wtT_p wtT_s b2_p b2_s mm1_p mm1_s mm2_p mm2_s x3
            sc_s sc_e x4 weT_p weT_s lg_p lg_e gm_s gmT_p gmT_s eb_p eb_s e2_p e2_s x5
            w3T_p w3T_s kc_p kc_s rk_s k3_p k3_s v3_p v3_s rt_p rt_s ro_p x6
            fb_s fT_p fT_s h3_p h3_s f3_p x7 st_out""".split()
        s = {n: sem(n) for n in names}

        block = ctx.enter_context(nc.Block())

        def nth(L, b):
            return B * L + b + 1 if L < 5 else 5 * B + PIPE.index((L, b)) + 1

        def nth_T(L, b):
            return nth(L, b) - B * (L > 4)

        def lnbank(L, b):
            return {0: 7, 1: b % 2, 2: b % 2, 3: 0, 5: 1, 6: 4, 7: 6}[L]

        def tiles(b):
            return slice(b * T, (b + 1) * T)

        def together(n):
            return slice(max(n - 2, 0) * T, min(n + 1, B) * T)

        @block.sync
        def _(sp):
            xin = a["x"].rearrange("b (t p) d -> p (b t) d", p=P)
            cin = a["ctx_1024"].rearrange("b (t p) d -> p (b t) d", p=P)
            sp.dma_start(x[:], xin).then_inc(s["ld_x"], 16)
            sp.dma_start(cx[:], cin).then_inc(s["ld_cx"], 16)
            for dst, nm in ((wq, "W_q"), (wk, "W_k"), (wv, "W_v"), (wo, "W_o")):
                sp.dma_start(dst[:], a["L0_xattn_" + nm]).then_inc(s["ld_w0"], 16)
            sp.dma_start(spl[:], a["t_split"]).then_inc(s["ld_w0"], 16)
            sp.dma_start(selc[:], a["t_sel"]).then_inc(s["ld_w0"], 16)
            sp.dma_start(rows[0:1, 0, :], a["L0_xattn_b_o"][None, :]).then_inc(s["ld_w0"], 16)
            for n, nm in enumerate(("g_xattn", "g_ffn")):
                sp.dma_start(gate[:, 4 * n:4 * n + 4],
                             a[nm][None, :].partition_broadcast(P)).then_inc(s["ld_gate"], 16)
            sp.dma_start(idsb[:], a["L0_ffn_ids"][None, :]).then_inc(s["ld_ids"], 16)
            sp.dma_start(wB[:], a["L0_ffn_weights"][None, :].partition_broadcast(P)).then_inc(s["ld_mix"], 16)
            sp.dma_start(wc[:], a["L0_ffn_weights"][:, None]).then_inc(s["ld_mix"], 16)
            sp.wait_ge(s["ld_ids"], 16)
            for k in range(KA):
                i = sp.value_load(idsb[0:1, k:k + 1], min_val=0, max_val=NA - 1)
                sp.dma_start(ads[:, k, :], a["L0_ffn_W"][bass.ds(i, 1), :, :].rearrange("a o d -> (a o) d")
                             ).then_inc(s["ld_ads"], 16)
                sp.dma_start(adb[k:k + 1, :], a["L0_ffn_b"][bass.ds(i, 1), :]).then_inc(s["ld_ads"], 16)
            sp.dma_start(b1r[:], a["L1_ffn_b1"].rearrange("e (c p) -> (e c) p", p=P)).then_inc(s["ld_moe"], 16)
            sp.dma_start(b2r[:], a["L1_ffn_b2"]).then_inc(s["ld_moe"], 16)
            sp.dma_start(wrr[:], a["L2_ffn_Wr"]).then_inc(s["ld_l2"], 16)
            sp.dma_start(brr[:], a["L2_ffn_br"][None, :]).then_inc(s["ld_l2"], 16)
            sp.dma_start(We[:], a["L2_ffn_We"].rearrange("e d c -> d e c")).then_inc(s["ld_l2"], 16)
            sp.dma_start(ber[:], a["L2_ffn_be"]).then_inc(s["ld_l2"], 16)
            for n, nm in enumerate(("Wq", "Wk", "Wv")):
                sp.dma_start(w3[:, n, :], a["L3_xattn_" + nm]).then_inc(s["ld_l3"], 16)
            sp.dma_start(f1[:], a["L3_ffn_w1"].rearrange("(c p) d -> p c d", p=P)).then_inc(s["ld_l3"], 16)
            sp.dma_start(f2[:], a["L3_ffn_w2"]).then_inc(s["ld_l3"], 16)
            sp.dma_start(f1br[:], a["L3_ffn_b1"].rearrange("(c p) -> c p", p=P)).then_inc(s["ld_l3"], 16)
            sp.dma_start(rows[0:1, 1, :], a["L3_ffn_b2"][None, :]).then_inc(s["ld_l3"], 16)
            sp.dma_start(xcos[:], a["t_cos"]).then_inc(s["ld_tab"], 16)
            sp.dma_start(xsin[:], a["t_sin"]).then_inc(s["ld_tab"], 16)
            sp.dma_start(decay[:], a["t_decay"]).then_inc(s["ld_tab"], 16)
            sp.dma_start(cmask[:], a["t_causal"]).then_inc(s["ld_tab"], 16)
            sp.wait_ge(s["pv_p"], 2 * B)
            sp.dma_start(w1, a["L1_ffn_W1"].rearrange("e d f -> d e f")).then_inc(s["ld_moe"], 16)
            sp.dma_start(w2, a["L1_ffn_W2"].rearrange("e (c p) d -> p e c d", p=P)).then_inc(s["ld_moe"], 16)
            sp.wait_ge(s["d_s"], W)
            sp.wait_ge(s["padded"], 3)
            sp.wait_ge(s["padq"], B)
            sp.dma_start(dD, Dun[:].rearrange("p r c -> p (r c)")).then_inc(s["d_w"], 16)
            sp.wait_ge(s["d_w"], 16)

            skew = bass.AP(tensor=dD.tensor, offset=LAGMAX * W1C,
                           ap=[[LANES * ROWS * W1C, B], [ROWS * W1C - G * W1C, LANES], [1, SLOTS * W1C]])
            HW = HS * W1C
            for h in range(2):
                sp.dma_start(Dw[:, h].rearrange("p r c -> p (r c)"), skew[:, :, h * HW:(h + 1) * HW]
                             ).then_inc(s[f"d_r{h}"], 16)
            with sp.Fori(0, ITERS - 1) as it:
                for h in range(2):
                    sp.wait_ge(s["rows_g"], 2 * it + h + 1)
                    sp.dma_start(Dw[:, h].rearrange("p r c -> p (r c)"),
                                 skew[:, :, bass.ds((2 * it + 2 + h) * HW, HW)]).then_inc(s[f"d_r{h}"], 16)
            sp.wait_ge(s["codes"], 2 * ITERS + 2)
            sp.dma_start(dC, Cw[:]).then_inc(s["codes_w"], 16)
            sp.wait_ge(s["codes_w"], 16)
            sp.dma_start(Cl.rearrange("p r c -> p (r c)"),
                         bass.AP(tensor=dC.tensor, offset=0,
                                 ap=[[LANES * SLOTS * W, B], [SLOTS * W + G * W, LANES], [1, S * W]])
                         ).then_inc(s["cl_r"], 16)
            sp.wait_ge(s["ct_s"], T)
            sp.dma_start(dCr.rearrange("b (t p) j -> p (b t) j", p=P), CT.rearrange("p b t s -> p (b t) s")).then_inc(s["ct_w"], 16)
            sp.wait_ge(s["ct_w"], 16)
            sp.dma_start(Cs.rearrange("p r j -> p (r j)"), dCr.rearrange("b (s r) j -> (b s) (r j)", r=R)
                         ).then_inc(s["cs_r"], 16)
            sp.wait_ge(s["g_s"], 1)
            sp.dma_start(Ge.rearrange("b s j -> b (s j)"), Gb[:]).then_inc(s["g_r"], 16)
            sp.wait_ge(s["e_s"], 1)
            sp.dma_start(el[:, R:R + 1], ech[:]).then_inc(s["e_r"], 16)
            sp.wait_ge(s["p_s"], 1)
            sp.dma_start(dP.rearrange("b (s r) j -> (b s) (r j)", r=R), Pm.rearrange("p r j -> p (r j)")
                         ).then_inc(s["p_w"], 16)
            sp.wait_ge(s["p_w"], 16)
            sp.dma_start(Pi.rearrange("p b t s -> p (b t) s"), dP.rearrange("b (t p) j -> p (b t) j", p=P)).then_inc(s["p_r"], 16)
            outv = out.rearrange("b (t p) d -> p (b t) d", p=P)
            for b in range(B):
                sp.wait_ge(s["x7"], b + 1)
                sp.dma_start(outv[:, tiles(b), :], x[:, tiles(b), :]).then_inc(s["st_out"], 16)
            sp.wait_ge(s["st_out"], 16 * B)

        @block.gpsimd
        def _(pool):
            own = Steps(pool, s["own_pool"])
            own(pool.memset(ident[:], 0.0))
            own(pool.memset(halfc[:], -0.5))
            pool.memset(ones[:], 1.0).then_inc(s["cst"], 1)
            own.settle()
            pool.affine_select(out=ident[:], in_=ident[:], compare_op=ALU.not_equal, fill=1.0, base=0,
                               pattern=[[-1, P]], channel_multiplier=1).then_inc(s["cst"], 1)
            pool.memset(mneg, 0.0).then_inc(s["cst"], 1)
            own(pool.memset(vaug, 0.0))
            own.settle()
            pool.memset(vaug[:, :, :, HD:HD + 1], 1.0).then_inc(s["cst"], 1)
            pool.iota(ioti[:], pattern=[[1, S + 1]], base=-1, channel_multiplier=0).then_inc(s["cst"], 1)
            pool.iota(thri[:], pattern=[[1, 17]], base=1, channel_multiplier=0).then_inc(s["cst"], 1)
            pool.iota(modi[:], pattern=[[1, 9], [8, 7]], base=-8, channel_multiplier=0).then_inc(s["cst"], 1)

            def inv_std(L, b):
                pool.wait_ge(s["ln_mv"], nth(L, b))
                pool.tensor_tensor(rstd[:, tiles(b)], veps[:, tiles(b)], halfc[:, tiles(b)], ALU.pow
                                   ).then_inc(s["ln_rstd"], 1)

            def rstds(L):
                for b in range(B):
                    inv_std(L, b)

            rstds(0)
            pool.memset(Dun[:, 0:LAGMAX, :], BIG).then_inc(s["padded"], 1)
            pool.memset(Dun[:, LAGMAX + S:ROWS, :], 0.0).then_inc(s["padded"], 1)
            own(pool.memset(Dun[:, LAGMAX:LAGMAX + S, 0:1], 0.0))
            own.settle()
            for b in range(B):
                pool.memset(Dun[b * LANES:b * LANES + 1, LAGMAX:LAGMAX + S, 0:1], BIG).then_inc(s["padq"], 1)
                pool.wait_ge(s["padq"], b + 1)
            own(pool.memset(Rw[:, 1, HS - 1:HS + 1, :], BIG))
            own.settle()
            for b in range(B):
                own(pool.memset(Rw[b * LANES:b * LANES + 1, 1, HS:HS + 1, 0:1], 0.0))
                own.settle()
            own.settle()
            pool.sem_inc(s["init_r"], 1)
            pool.memset(sc[:], 0.0).then_inc(s["padded"], 1)
            pool.wait_ge(s["ld_cx"], 16)
            cf = cx[:].rearrange("p t d -> p (t d)")
            own(pool.tensor_copy(c3[:, 0, :], cf))
            own.settle()
            own(pool.tensor_tensor(crem, cf, c3[:, 0, :], ALU.subtract))
            own.settle()
            own(pool.tensor_copy(c3[:, 1, :], crem))
            own.settle()
            own(pool.tensor_tensor(crem, crem, c3[:, 1, :], ALU.subtract))
            own.settle()
            pool.tensor_copy(c3[:, 2, :], crem).then_inc(s["c3_s"], 1)
            rstds(1)
            rstds(2)
            pool.sem_inc(s["codes"], 2)
            n_code = 7
            with pool.Fori(0, ITERS) as it:
                for h in range(2):
                    k = [0]

                    def step(ins):
                        k[0] += 1
                        ins.then_inc(s["own_pool"], 1)

                    def settle():
                        pool.wait_ge(s["own_pool"], own.n + (2 * it + h) * n_code + k[0])
                        pool.sem_inc(s["turns"], 1)

                    pool.wait_ge(s["rows_g"], 2 * it + h + 1)
                    dg = Rw[:, h, 0:HS, 0:W]
                    up = Rw[:, h, 0:HS, 1:W + 1]
                    lf = Rw[:, h, 1:HS + 1, 0:W]
                    step(pool.tensor_tensor(cd[:, 0], dg, up, ALU.subtract))
                    step(pool.tensor_tensor(cd[:, 1], dg, lf, ALU.subtract))
                    step(pool.tensor_tensor(cd[:, 2], up, lf, ALU.subtract))
                    settle()
                    step(pool.tensor_scalar(cd[:, 3], cd[:, 0], 0.0, None, ALU.is_gt))
                    step(pool.tensor_scalar(cd[:, 4], cd[:, 1], 0.0, None, ALU.is_gt))
                    step(pool.tensor_scalar(cd[:, 5], cd[:, 2], 0.0, 0.5, ALU.is_gt, ALU.add))
                    settle()
                    step(pool.tensor_tensor(cd[:, 0], cd[:, 3], cd[:, 4], ALU.add))
                    settle()
                    assert k[0] == n_code
                    pool.tensor_tensor(Cw[:, bass.ds((2 * it + h) * HS * W, HS * W)],
                                       cd[:, 0].rearrange("p r c -> p (r c)"),
                                       cd[:, 5].rearrange("p r c -> p (r c)"), ALU.mult).then_inc(s["codes"], 1)
                    pool.wait_ge(s["codes"], 2 * it + h + 3)
            own.n += 2 * ITERS * n_code
            pool.wait_ge(s["ld_tab"], 64)
            kc = ft[:].rearrange("p (n c) d -> p n (c d)", n=2)
            for b in range(B):
                pool.wait_ge(s["kc_s"], b + 1)
                own(pool.tensor_tensor(rk[b], kc[:, 0, :], xcos[:, 1, :], ALU.mult))
                own(pool.tensor_tensor(kc[:, 1, :], kc[:, 1, :], xsin[:, 1, :], ALU.mult))
                own.settle()
                pool.tensor_tensor(rk[b], rk[b], kc[:, 1, :], ALU.add).then_inc(s["rk_s"], 1)
            for L in (3, 4):
                rstds(L)
            for n in range(B + 2):
                pool.wait_ge(s["ln_mv"], 5 * B + n + 1)
                pool.tensor_tensor(rstd[:, together(n)], veps[:, together(n)], halfc[:, together(n)], ALU.pow
                                   ).then_inc(s["ln_rstd"], 1)

        @block.tensor
        def _(pe):
            def ln_T(L, b):
                pe.wait_ge(s["ln_y"], nth(L, b))
                if L in (1, 2) and b >= 2:
                    pe.wait_ge(s["ln_yT"], nth_T(L, b) - 2)
                for t in range(T):
                    mm = pe.transpose(PS[:, lnbank(L, b), t * P:(t + 1) * P], y[:, b * T + t, :], ident[:])
                mm.then_inc(s["ln_T"], 1)

            pe.wait_ge(s["cst"], 2)
            pe.wait_ge(s["ld_cx"], 16)
            for n in range(NT):
                mm = pe.transpose(PS[:, 2 + n // 4, (n % 4) * P:(n % 4 + 1) * P], cx[:, n, :], ident[:])
                if n % 4 == 3:
                    mm.then_inc(s["cxT_p"], 1)
            pe.wait_ge(s["cst_v"], 2)
            pe.wait_ge(s["ld_w0"], 112)
            pe.wait_ge(s["cxT_s"], 2)

            def project(b):
                pe.wait_ge(s["ln_yT"], nth_T(0, b))
                for j in range(NJ):
                    pe.matmul(PS[:, j, 0:S], wqp[:, j, :], yT[:, b, :], start=True, stop=True)
                    pe.matmul(PS[:, j, S:2 * S], wkp[:, j, :], cxT[:, b, :], start=True, stop=True
                              ).then_inc(s["q0_p"], 1)
                for t in range(T):
                    mm = pe.matmul(PS[:, 7, t * P:(t + 1) * P], cxT[:, b, t * P:(t + 1) * P], wv[:],
                                   start=True, stop=True)
                mm.then_inc(s["v_p"], 1)

            def scores(u, at_, lhs, rhs, done, maxima):
                jp, t = divmod(u, T)
                for i in range(NI):
                    r = slice(32 * i, 32 * (i + 1))
                    r8 = slice(32 * i, 32 * i + 2 * NJ)
                    for jj in range(2):
                        j = 2 * jp + jj
                        to = PS[:, at_ + i, jj * S:(jj + 1) * S]
                        if maxima:
                            pe.matmul(to, sel[r8, j, :], mT[r8, :], start=True, stop=False)
                        mm = pe.matmul(to, qk[r, j, lhs, t * P:(t + 1) * P], qk[r, j, rhs, :],
                                       start=not maxima, stop=True)
                mm.then_inc(s[done], 1)

            def weigh(b, jp):
                for jj in range(2):
                    for i in range(NI):
                        h = (2 * jp + jj) * NI + i
                        for kt in range(T):
                            mm = pe.matmul(PS[32 * i:32 * (i + 1), 4 + jp, jj * S:(jj + 1) * S], vaug[:, kt, h, :],
                                           pT[:, kt, h, :], start=(kt == 0), stop=(kt == T - 1))
                mm.then_inc(s["pv_p"], 1)

            def back(b):
                pe.wait_ge(s["uT_s"], 2 * (b + 1))
                for t in range(T):
                    for j in range(NJ):
                        mm = pe.transpose(PS[:, 4 + t, j * P:(j + 1) * P], uT[:, j, t * P:(t + 1) * P], ident[:])
                mm.then_inc(s["un_p"], 1)

            def turn(b):
                pe.wait_ge(s["o_n"], b + 1)
                for t in range(T):
                    mm = pe.transpose(PS[:, 5, t * P:(t + 1) * P], o[:, t, :], ident[:])
                mm.then_inc(s["oT_p"], 1)

            def finish(b):
                pe.wait_ge(s["oT_s"], b + 1)
                for t in range(T):
                    c = slice(t * P, (t + 1) * P)
                    pe.matmul(PS[:, 6, c], oT[:, c], wo[:], start=True, stop=False)
                    mm = pe.matmul(PS[:, 6, c], ones[0:1, :], rows[0:1, 0, :], start=False, stop=True)
                mm.then_inc(s["at_p"], 1)

            ln_T(0, 0)
            project(0)
            for b in range(B):
                for u in range(4):
                    if u == 0:
                        pe.wait_ge(s["q0_s"], NJ * (b + 1))
                    elif u == 1:
                        if b:
                            turn(b - 1)
                            finish(b - 1)
                            pe.wait_ge(s["x0"], b)
                        pe.wait_ge(s["v_s"], b + 1)
                    else:
                        pe.wait_ge(s["s_m"], 4 * b + u - 1)
                    scores(u, 4 * (u % 2), 0, 1, "s_p", False)
                pe.wait_ge(s["mn_s"], b + 1)
                for t in range(T):
                    mm = pe.transpose(PS[:, 0, t * P:(t + 1) * P], mneg[:, t, :], ident[:])
                mm.then_inc(s["qm_p"], 1)
                pe.wait_ge(s["qm_s"], b + 1)
                for u in range(4):
                    if u >= 2:
                        pe.wait_ge(s["st_e"], 4 * b + u - 1)
                    scores(u, 4 * (1 - u % 2), 1, 0, "st_p", True)
                pe.wait_ge(s["st_e"], 4 * b + 3)
                if b + 1 < B:
                    ln_T(0, b + 1)
                weigh(b, 0)
                pe.wait_ge(s["st_e"], 4 * b + 4)
                weigh(b, 1)
                if b + 1 < B:
                    project(b + 1)
                back(b)
            turn(B - 1)
            finish(B - 1)
            pe.wait_ge(s["weff_s"], 1)
            pe.transpose(PS[:, 5, 0:P], weff[:], ident[:]).then_inc(s["weffT_p"], 1)
            pe.wait_ge(s["weffT_s"], 1)
            for b in range(B):
                ln_T(1, b)
                pe.wait_ge(s["ln_yT"], nth_T(1, b))
                if b >= 2:
                    pe.wait_ge(s["x1"], b - 1)
                for t in range(T):
                    c = slice(t * P, (t + 1) * P)
                    pe.matmul(PS[:, 2 + b % 2, c], yT[:, b, c], weffT[:], start=True, stop=False)
                    mm = pe.matmul(PS[:, 2 + b % 2, c], wrow[:], adb[:], start=False, stop=True)
                mm.then_inc(s["f0_p"], 1)
            pe.wait_ge(s["x1"], B)
            pe.wait_ge(s["sqc_s"], 1)
            for b in range(B):
                ln_T(2, b)
                pe.wait_ge(s["ln_yT"], nth_T(2, b))
                q = slice(b * LANES, (b + 1) * LANES)
                for c in range(W):
                    mm = pe.matmul(PS[q, 2 + c // 2, (c % 2) * S:(c % 2 + 1) * S], yT[:, b, c:S:W], cxT[:, b, :],
                                   start=True, stop=True)
                mm.then_inc(s["ab_p"], 1)
                pe.matmul(PS[q, 6, 0:S], ones[:, 0:LANES], sqc[:, b, :], start=True, stop=True)
                pe.wait_ge(s["sq_s"], b + 1)
                for c in range(W):
                    mm = pe.matmul(PS[q, 6, S + c:S + c + 1], sq[:, c:S:W], ones[:, 0:1], start=True, stop=True)
                mm.then_inc(s["aabb_p"], 1)
            pe.wait_ge(s["ld_moe"], 64)
            pe.transpose(PS[:, 0, 0:E1 * CH], b1r[:], ident[0:E1 * CH, 0:E1 * CH]).then_inc(s["b1_p"], 1)
            pe.wait_ge(s["ld_l2"], 64)
            pe.wait_ge(s["aabb_s"], 1)
            pe.wait_ge(s["dsq"], 1)
            for e in range(E2):
                mm = pe.transpose(PS[:, 2 + e // 4, (e % 4) * D:(e % 4 + 1) * D], We[:, e, :], ident[:])
            pe.transpose(PS[:, 4, 0:E2], wrr[:], ident[0:E2, 0:E2]).then_inc(s["weT_p"], 1)
            pe.wait_ge(s["ld_l3"], 112)
            for n in range(3):
                pe.transpose(PS[:, 5, n * D:(n + 1) * D], w3[:, n, :], ident[:])
            pe.transpose(PS[:, 5, 3 * D:3 * D + CH], f1br[:], ident[0:CH, 0:CH]).then_inc(s["w3T_p"], 1)
            pe.wait_ge(s["fb_s"], 1)
            for c in range(CH):
                pe.transpose(PS[:, 6, c * P:(c + 1) * P], fs[:, c, :], ident[:])
            for c in range(CH):
                mm = pe.transpose(PS[:, 7, c * P:(c + 1) * P], ft[:, c, :], ident[:])
            mm.then_inc(s["fT_p"], 1)
            pe.wait_ge(s["weT_s"], 1)
            pe.wait_ge(s["cl_r"], 16)
            pe.wait_ge(s["cst_v"], 2)
            for t in range(T):
                bank = PS[:, 2 + t, :].bitcast(BF16)
                for c in range(W):
                    mm = pe.transpose(bank[:, c * P:(c + 1) * P], Cl[:, t * P:(t + 1) * P, c], identb[:])
                mm.then_inc(s["clT_p"], 1)
            pe.wait_ge(s["w3T_s"], 1)
            pe.wait_ge(s["fT_s"], 1)
            pe.wait_ge(s["b1_s"], 1)
            for b in range(B):
                if b >= 2:
                    pe.wait_ge(s["kc_s"], b - 1)
                pe.matmul(PS[:, 6 + b % 2, 0:S], w3T[:, 1, :], cxT[:, b, :], start=True, stop=True)
                pe.matmul(PS[:, 6 + b % 2, S:2 * S], w3T[:, 4, :], cxT[:, b, :], start=True, stop=True
                          ).then_inc(s["kc_p"], 1)
                for t in range(T):
                    c = (b % 2 * T + t) * D
                    mm = pe.matmul(PS[:, b // 2, c:c + D], cxT[:, b, t * P:(t + 1) * P], w3T[:, 2, :],
                                   start=True, stop=True)
                mm.then_inc(s["v3_p"], 1)
            pe.wait_ge(s["p_r"], 16)
            pe.wait_ge(s["c3_s"], 1)
            pe.wait_ge(s["w3T_s"], 1)
            pe.wait_ge(s["ct_s"], T)
            for b in range(B):
                for jt in range(T):
                    for n in range(3 * T):
                        t, part = divmod(n, 3)
                        mm = pe.matmul(PS[:, 2 + b, jt * P:(jt + 1) * P], Pi[:, b, t, jt * P:(jt + 1) * P],
                                       c3[:, part, (b * T + t) * D:(b * T + t + 1) * D],
                                       start=(n == 0), stop=(n == 3 * T - 1))
                mm.then_inc(s["ex_p"], 1)
            pe.wait_ge(s["x2"], B)
            pe.wait_ge(s["v3_s"], 2)
            pe.wait_ge(s["kc_s"], B)
            for b in range(B):
                if b:
                    pe.wait_ge(s["b2_s"], b)
                ln_T(3, b)
                pe.wait_ge(s["wt_s"], b + 1)
                for t in range(T):
                    mm = pe.transpose(PS[0:E1, 1, t * P:(t + 1) * P], wts[:, b % 2, t, :], ident[:])
                mm.then_inc(s["wtT_p"], 1)
                pe.wait_ge(s["ln_yT"], nth_T(3, b))

                def up(e):
                    n = E1 * b + e
                    if n >= 2:
                        pe.wait_ge(s["mm1_s"], 2 * (n - 1))
                    for c in range(CH):
                        mm = pe.matmul(PS[:, 2 + 2 * (n % 2) + c // 2, (c % 2) * S:(c % 2 + 1) * S],
                                       w1[:, e, c * P:(c + 1) * P], yT[:, b, :], start=True, stop=True)
                        if c % 2:
                            mm.then_inc(s["mm1_p"], 1)

                def down(e):
                    n = E1 * b + e
                    pe.wait_ge(s["mm1_s"], 2 * (n + 1))
                    if n >= 2:
                        pe.wait_ge(s["mm2_s"], n - 1)
                    for t in range(T):
                        for c in range(CH):
                            mm = pe.matmul(PS[:, 6 + n % 2, t * D:(t + 1) * D], hT[:, CH * (n % 2) + c, t * P:(t + 1) * P],
                                           w2[:, e, c, :], start=(c == 0), stop=(c == CH - 1))
                    mm.then_inc(s["mm2_p"], 1)

                up(0)
                pe.wait_ge(s["wtT_s"], b + 1)
                for t in range(T):
                    mm = pe.matmul(PS[:, 0, t * D:(t + 1) * D], wtsT[:, t * P:(t + 1) * P], b2r[:],
                                   start=True, stop=True)
                mm.then_inc(s["b2_p"], 1)
                for e in range(1, E1):
                    up(e)
                    down(e - 1)
                down(E1 - 1)
            pe.wait_ge(s["weT_s"], 1)
            pe.wait_ge(s["rk_s"], B)
            pe.wait_ge(s["v3_s"], 2)

            def expert(b, k, bank):
                h, t = divmod(k, 2)
                return pe.matmul(PS[:, bank, :], yT[:, b, t * P:(t + 1) * P],
                                 WeT[:, 4 * h:4 * h + 4, :].rearrange("p e d -> p (e d)"), start=True, stop=True)

            for n in range(B + 2):
                ba, br, bf = n, n - 1, n - 2
                do_a, do_r, do_f = ba < B, 0 <= br < B, 0 <= bf
                if do_a:
                    if ba:
                        pe.wait_ge(s["x5"], ba)
                    ln_T(5, ba)
                if do_r:
                    if br:
                        pe.wait_ge(s["x6"], br)
                    ln_T(6, br)
                if do_a:
                    pe.wait_ge(s["ln_yT"], nth_T(5, ba))
                    for t in range(T):
                        c = slice(t * E2, (t + 1) * E2)
                        pe.matmul(PS[:, 1, c], yT[:, ba, t * P:(t + 1) * P], wrT[:], start=True, stop=False)
                        mm = pe.matmul(PS[:, 1, c], ones[0:1, :], brr[:], start=False, stop=True)
                    mm.then_inc(s["lg_p"], 1)
                if do_f:
                    if bf:
                        pe.wait_ge(s["x7"], bf)
                    ln_T(7, bf)
                if do_r:
                    pe.wait_ge(s["ln_yT"], nth_T(6, br))
                    pe.matmul(PS[:, 4, 0:S], w3T[:, 0, :], yT[:, br, :], start=True, stop=True)
                    pe.matmul(PS[:, 4, S:2 * S], w3T[:, 3, :], yT[:, br, :], start=True, stop=True
                              ).then_inc(s["k3_p"], 1)
                if do_a:
                    pe.wait_ge(s["gm_s"], ba + 1)
                    for t in range(T):
                        mm = pe.transpose(PS[0:E2, 1, t * P:(t + 1) * P], gm[:, t, :], ident[:])
                    mm.then_inc(s["gmT_p"], 1)
                if do_a:
                    for k, bank in enumerate((0, 2, 3)):
                        mm = expert(ba, k, bank)
                    mm.then_inc(s["e2_p"], 1)
                if do_a:
                    pe.wait_ge(s["gmT_s"], ba + 1)
                    for t in range(T):
                        mm = pe.matmul(PS[:, 1, t * D:(t + 1) * D], gmT[:, t * P:(t + 1) * P], ber[:],
                                       start=True, stop=True)
                    mm.then_inc(s["eb_p"], 1)
                if do_r:
                    pe.wait_ge(s["k3_s"], br + 1)
                    for t in range(T):
                        mm = pe.matmul(PS[:, 4, t * S:(t + 1) * S], rk[br][:, t * P:(t + 1) * P], rq,
                                       start=True, stop=True)
                    mm.then_inc(s["rt_p"], 1)
                if do_f:
                    pe.wait_ge(s["ln_yT"], nth_T(7, bf))
                    for c in range(CH):
                        mm = pe.matmul(PS[:, 6 + c // 2, (c % 2) * S:(c % 2 + 1) * S], f1T[:, c, :], yT[:, bf, :],
                                       start=True, stop=True)
                        if c % 2:
                            mm.then_inc(s["h3_p"], 1)
                if do_a:
                    pe.wait_ge(s["e2_s"], ba + 1)
                    expert(ba, 3, 0).then_inc(s["e2_p"], 1)
                if do_r:
                    pe.wait_ge(s["rt_s"], br + 1)
                    for t in range(T):
                        for kt in range(t + 1):
                            mm = pe.matmul(PS[:, 5, t * D:(t + 1) * D], ret[:, kt, t * P:(t + 1) * P],
                                           v3[:, br, kt, :], start=(kt == 0), stop=(kt == t))
                    mm.then_inc(s["ro_p"], 1)
                if do_f:
                    pe.wait_ge(s["h3_s"], 2 * (bf + 1))
                    for t in range(T):
                        c_ = slice(t * D, (t + 1) * D)
                        for c in range(CH):
                            pe.matmul(PS[:, 6, c_], hg[:, c, t * P:(t + 1) * P], f2T[:, c, :],
                                      start=(c == 0), stop=False)
                        mm = pe.matmul(PS[:, 6, c_], ones[0:1, :], rows[0:1, 1, :], start=False, stop=True)
                    mm.then_inc(s["f3_p"], 1)

        @block.scalar
        def _(act):
            def copy(out_, in_):
                return act.activation(out_, in_, ACT.Copy)

            def ln_yT(L, b):
                act.wait_ge(s["ln_T"], nth_T(L, b))
                copy(yT[:, b, :], PS[:, lnbank(L, b), 0:S]).then_inc(s["ln_yT"], 1)

            for n in range(2):
                act.wait_ge(s["cxT_p"], n + 1)
                copy(cxT[:, 2 * n:2 * n + 2, :].rearrange("p b s -> p (b s)"), PS[:, 2 + n, :]
                     ).then_inc(s["cxT_s"], 1)
            act.wait_ge(s["ld_gate"], 32)
            act.activation(gate[:], gate[:], ACT.Tanh).then_inc(s["gates"], 1)
            act.wait_ge(s["cst"], 4)

            def projected(b):
                for j in range(NJ):
                    act.wait_ge(s["q0_p"], NJ * b + j + 1)
                    if b:
                        act.wait_ge(s["q0_s"], NJ * (b - 1) + j + 1)
                    copy(qkh[:, j].rearrange("p n s -> p (n s)"), PS[:, j, :]).then_inc(s["q0_h"], 1)
                act.wait_ge(s["v_p"], b + 1)
                if b:
                    act.wait_ge(s["pv_p"], 2 * b)
                copy(vaug[:, :, :, 0:HD].rearrange("p t h d -> p (t h) d"),
                     PS[:, 7, 0:S].rearrange("p (n d) -> p n d", d=HD)).then_inc(s["v_s"], 1)

            def o_T(b):
                act.wait_ge(s["oT_p"], b + 1)
                if b:
                    act.wait_ge(s["at_p"], b)
                copy(oT[:], PS[:, 5, 0:S]).then_inc(s["oT_s"], 1)

            ln_yT(0, 0)
            projected(0)
            for b in range(B):
                act.wait_ge(s["qm_p"], b + 1)
                copy(mTh, PS[:, 0, 0:S]).then_inc(s["qm_h"], 1)
                for u in range(4):
                    jp, t = divmod(u, T)
                    at_ = 4 * (1 - u % 2)
                    act.wait_ge(s["st_p"], 4 * b + u + 1)
                    act.activation(pT[:, t, 2 * NI * jp:2 * NI * (jp + 1), :].rearrange("p (j i) q -> p i j q", j=2),
                                   PS[:, at_:at_ + 4, :].rearrange("p i (j q) -> p i j q", j=2),
                                   ACT.Exp, scale=HD ** -0.5).then_inc(s["st_e"], 1)
                if b + 1 < B:
                    ln_yT(0, b + 1)
                for jp in range(2):
                    act.wait_ge(s["pv_p"], 2 * b + jp + 1)
                    if b:
                        act.wait_ge(s["un_p"], b)
                    copy(uT[:, 2 * jp:2 * jp + 2, :].rearrange("p j s -> p (j s)"), PS[:, 4 + jp, :]
                         ).then_inc(s["uT_s"], 1)
                if b + 1 < B:
                    projected(b + 1)
                o_T(b)
            act.wait_ge(s["weffT_p"], 1)
            copy(weffT[:], PS[:, 5, 0:P]).then_inc(s["weffT_s"], 1)
            for b in range(B):
                ln_yT(1, b)
            for b in range(B):
                ln_yT(2, b)
            for c in range(W):
                act.wait_ge(s["dsq"], 1)
                act.activation(Dun[:, LAGMAX:LAGMAX + S, c + 1], dsum[:, c, :], ACT.Sqrt).then_inc(s["d_s"], 1)
            act.wait_ge(s["b1_p"], 1)
            copy(b1c[:], PS[:, 0, 0:E1 * CH]).then_inc(s["b1_s"], 1)
            act.wait_ge(s["weT_p"], 1)
            copy(WeT[:].rearrange("p e d -> p (e d)"), PS[:, 2:4, :].rearrange("p a n -> p (a n)"))
            copy(wrT[:], PS[:, 4, 0:E2]).then_inc(s["weT_s"], 1)
            act.wait_ge(s["w3T_p"], 1)
            copy(w3T[:, 0:3, :].rearrange("p a n -> p (a n)"), PS[:, 5, 0:3 * D])
            copy(f1bc[:], PS[:, 5, 3 * D:3 * D + CH])
            for n in range(2):
                pv = PS[:, 5, n * D:(n + 1) * D].rearrange("p (m two) -> p m two", two=2)
                wv_ = w3T[:, 3 + n, :].rearrange("p (m two) -> p m two", two=2)
                act.activation(wv_[:, :, 0], pv[:, :, 1], ACT.Copy, scale=-1.0)
                last = copy(wv_[:, :, 1], pv[:, :, 0])
            last.then_inc(s["w3T_s"], 1)
            act.wait_ge(s["fT_p"], 1)
            copy(f1T[:].rearrange("p c n -> p (c n)"), PS[:, 6, :])
            copy(f2T[:].rearrange("p c n -> p (c n)"), PS[:, 7, :]).then_inc(s["fT_s"], 1)
            for t in range(T):
                act.wait_ge(s["clT_p"], t + 1)
                copy(CT[:, :, t, :].rearrange("p b (k c) -> p b k c", c=W),
                     PS[:, 2 + t, :].bitcast(BF16).rearrange("p (c b k) -> p b k c", c=W, b=B)
                     ).then_inc(s["ct_s"], 1)
            for b in range(B):
                act.wait_ge(s["kc_p"], b + 1)
                if b:
                    act.wait_ge(s["rk_s"], b)
                copy(ft[:].rearrange("p c d -> p (c d)"), PS[:, 6 + b % 2, :]).then_inc(s["kc_s"], 1)
                if b % 2:
                    act.wait_ge(s["v3_p"], b + 1)
                    copy(v3[:, b - 1:b + 1].rearrange("p b t d -> p (b t d)"), PS[:, b // 2, :]
                         ).then_inc(s["v3_s"], 1)

            def head_exp(b):
                act.wait_ge(s["sc_s"], b + 1)
                act.activation(sc2[:], sc2[:], ACT.Exp).then_inc(s["sc_e"], 1)

            for b in range(B):
                ln_yT(3, b)
                act.wait_ge(s["wtT_p"], b + 1)
                if b:
                    act.wait_ge(s["b2_p"], b)
                copy(wtsT[:], PS[0:E1, 1, 0:S]).then_inc(s["wtT_s"], 1)
                for e in range(E1):
                    n = E1 * b + e
                    for c in range(CH):
                        act.wait_ge(s["mm1_p"], 2 * n + c // 2 + 1)
                        if n >= 2 and c == 0:
                            act.wait_ge(s["mm2_p"], n - 1)
                        last = act.activation(hT[:, CH * (n % 2) + c, :],
                                              PS[:, 2 + 2 * (n % 2) + c // 2, (c % 2) * S:(c % 2 + 1) * S],
                                              ACT.Relu, bias=b1c[:, e * CH + c:e * CH + c + 1])
                        if c % 2:
                            last.then_inc(s["mm1_s"], 1)
                    if b and e == 5:
                        head_exp(b - 1)
            for n in range(B + 2):
                ba, br, bf = n, n - 1, n - 2
                do_a, do_r, do_f = ba < B, 0 <= br < B, 0 <= bf
                if do_a:
                    ln_yT(5, ba)
                if do_r:
                    ln_yT(6, br)
                if do_f:
                    ln_yT(7, bf)
                if do_a:
                    act.wait_ge(s["lg_s"], ba + 1)
                    act.activation(lg[:], lg[:], ACT.Exp).then_inc(s["lg_e"], 1)
                    act.wait_ge(s["gmT_p"], ba + 1)
                    copy(gmT[:], PS[0:E2, 1, 0:S]).then_inc(s["gmT_s"], 1)
                if n == 1:
                    head_exp(B - 1)
                if do_f:
                    if bf:
                        act.wait_ge(s["f3_p"], bf)
                    for c in range(CH):
                        act.wait_ge(s["h3_p"], 2 * bf + c // 2 + 1)
                        last = act.activation(hg[:, c, :], PS[:, 6 + c // 2, (c % 2) * S:(c % 2 + 1) * S], ACT.Gelu,
                                              bias=f1bc[:, c:c + 1])
                        if c % 2:
                            last.then_inc(s["h3_s"], 1)

        @block.vector
        def _(v):
            own = Steps(v, s["own_dve"])

            def stats(L, b):
                if L:
                    v.wait_ge(s[f"x{L - 1}"], b + 1)
                for t in range(T):
                    own(v.bn_stats(st6[:, b * T + t, :], x[:, b * T + t, :]))
                own.settle()
                for t in range(T):
                    own(v.bn_aggr(mv[:, b * T + t, :], st6[:, b * T + t, :]))
                own.settle()
                v.tensor_scalar(veps[:, tiles(b)], mv[:, tiles(b), 1], EPS, None, ALU.add
                                ).then_inc(s["ln_mv"], 1)

            def norm(L, b):
                v.wait_ge(s["ln_rstd"], nth(L, b) if L < 5 else 5 * B + (b + L - 5) + 1)
                for t in range(T):
                    n = b * T + t
                    ins = v.tensor_scalar(y[:, n, :], x[:, n, :], mv[:, n, 0:1], rstd[:, n:n + 1],
                                          ALU.subtract, ALU.mult)
                ins.then_inc(s["ln_y"], 1)

            def add(L, b, src, g):
                v.scalar_tensor_tensor(out=x[:, tiles(b), :].rearrange("p t d -> p (t d)"), in0=src,
                                       scalar=gate[:, g:g + 1],
                                       in1=x[:, tiles(b), :].rearrange("p t d -> p (t d)"),
                                       op0=ALU.mult, op1=ALU.add).then_inc(s[f"x{L}"], 1)

            v.wait_ge(s["ld_x"], 16)
            for b in range(B):
                stats(0, b)
            own.settle()
            v.wait_ge(s["ld_w0"], 112)
            for dst, src in ((wqp, wq), (wkp, wk)):
                for j in range(NJ):
                    own(v.tensor_copy(dst[:, j, :].rearrange("p (i n d) -> p i n d", i=NI, n=4),
                                      src[:, j * NI * HD:(j + 1) * NI * HD].rearrange("p (i d) -> p i d", i=NI)
                                      .unsqueeze(2).broadcast_to([P, NI, 4, HD])))
            own(v.tensor_copy(sel[:], selc[:].unsqueeze(2).broadcast_to([P, NJ, P])))
            own.settle()
            v.sem_inc(s["cst_v"], 1)
            v.wait_ge(s["cst"], 7)
            v.tensor_copy(identb[:], ident[:]).then_inc(s["cst_v"], 1)
            v.tensor_copy(iot[:], ioti[:]).then_inc(s["cst_v"], 1)
            v.tensor_copy(thr[:], thri[:]).then_inc(s["cst_v"], 1)
            v.tensor_copy(modt[:].rearrange("p a b -> p (a b)"), modi[:]).then_inc(s["cst_v"], 1)
            v.wait_ge(s["cst_v"], 5)
            own(v.tensor_copy(iotr[:], iot[:, 1:S + 1].unsqueeze(1).broadcast_to([P, R, S])))
            for b in range(B):
                norm(0, b)

            def attended(b):
                v.wait_ge(s["un_p"], b + 1)
                pv = PS[:, 4:4 + T, :].rearrange("p t (n c) -> p (t n) c", c=32)
                own(v.reciprocal(rden[:], pv[:, :, HD]))
                own.settle()
                if b:
                    v.wait_ge(s["oT_p"], b)
                v.tensor_tensor(o[:].rearrange("p t (h d) -> p (t h) d", d=HD), pv[:, :, 0:HD],
                                rden[:].unsqueeze(2).broadcast_to([P, T * HEADS, HD]), ALU.mult
                                ).then_inc(s["o_n"], 1)

            def projected_out(b):
                v.wait_ge(s["at_p"], b + 1)
                v.wait_ge(s["gates"], 1)
                add(0, b, PS[:, 6, 0:S], 0)

            def maxima(b, u):
                jp, t = divmod(u, T)
                at_ = 4 * (u % 2)
                v.wait_ge(s["s_p"], 4 * b + u + 1)
                if b and u == 0:
                    v.wait_ge(s["qm_p"], b)
                v.tensor_reduce(mneg[:, t, :].rearrange("p (i c) -> p i c", i=NI)[:, :, 4 * jp:4 * jp + 4:2],
                                PS[:, at_:at_ + 4, :].rearrange("p i (j k) -> p i j k", j=2), AX, ALU.max,
                                negate=True).then_inc(s["s_m"], 1)

            for b in range(B):
                for j in range(NJ):
                    v.wait_ge(s["q0_h"], NJ * b + j + 1)
                    if b:
                        v.wait_ge(s["st_p"], 4 * b)
                    for n in range(2):
                        ins = v.scalar_tensor_tensor(out=qk[:, j, n, :], in0=qkh[:, j, n, :].bitcast(F32),
                                                     scalar=spl[:, n:n + 1], in1=PS[:, j, n * S:(n + 1) * S],
                                                     op0=ALU.mult, op1=ALU.add)
                    ins.then_inc(s["q0_s"], 1)
                if b:
                    attended(b - 1)
                maxima(b, 0)
                if b:
                    projected_out(b - 1)
                for u in range(1, 4):
                    maxima(b, u)
                v.wait_ge(s["s_m"], 4 * (b + 1))
                mp = mneg.rearrange("p t (i c) -> p (t i) c", i=NI)
                v.tensor_copy(mp[:, :, 1:2 * NJ:2], mp[:, :, 0:2 * NJ:2]).then_inc(s["mn_s"], 1)
                v.wait_ge(s["qm_h"], b + 1)
                v.scalar_tensor_tensor(out=mT[:], in0=mTh.bitcast(F32), scalar=spl[:, 2:3], in1=PS[:, 0, 0:S],
                                       op0=ALU.mult, op1=ALU.add).then_inc(s["qm_s"], 1)
                if b:
                    stats(1, b - 1)
                    norm(1, b - 1)
                else:
                    v.wait_ge(s["ld_ads"], 32 * KA)
                    v.wait_ge(s["ld_mix"], 32)
                    own(v.tensor_scalar(weff[:], ads[:, 0, :], wB[:, 0:1], None, ALU.mult))
                    own(v.tensor_scalar(wrow[:], ones[0:KA, :], wc[:, 0:1], None, ALU.mult))
                    for k in range(1, KA):
                        own.settle()
                        own(v.scalar_tensor_tensor(out=weff[:], in0=ads[:, k, :], scalar=wB[:, k:k + 1],
                                                   in1=weff[:], op0=ALU.mult, op1=ALU.add))
                    own.settle()
                    v.sem_inc(s["weff_s"], 1)
            attended(B - 1)
            projected_out(B - 1)
            stats(1, B - 1)
            norm(1, B - 1)
            for b in range(B):
                v.wait_ge(s["f0_p"], b + 1)
                add(1, b, PS[:, 2 + b % 2, 0:S], 4)
                stats(2, b)
                norm(2, b)
            v.wait_ge(s["cxT_s"], 2)
            v.wait_ge(s["c3_s"], 1)
            cf = cxT[:].rearrange("p b s -> p (b s)")
            v.tensor_tensor(sqc.rearrange("p b s -> p (b s)"), cf, cf, ALU.mult).then_inc(s["sqc_s"], 1)
            for b in range(B):
                v.wait_ge(s["ln_yT"], nth_T(2, b))
                if b:
                    v.wait_ge(s["aabb_p"], b)
                v.tensor_tensor(sq[:], yT[:, b, :], yT[:, b, :], ALU.mult).then_inc(s["sq_s"], 1)
            v.wait_ge(s["aabb_p"], B)
            own(v.tensor_copy(aab[:], PS[:, 6, 0:S]))
            own(v.tensor_copy(bbk[:], PS[:, 6, S:S + W]))
            own.settle()
            v.sem_inc(s["aabb_s"], 1)
            for c in range(W):
                own(v.tensor_scalar(dsum[:, c, :], aab[:], bbk[:, c:c + 1], None, ALU.add))
            own.settle()
            for c in range(0, W, 2):
                d2 = dsum[:, c:c + 2, :].rearrange("p c s -> p (c s)")
                own(v.scalar_tensor_tensor(out=d2, in0=PS[:, 2 + c // 2, :], scalar=-2.0, in1=d2,
                                           op0=ALU.mult, op1=ALU.add))
            own.settle()
            df = dsum.rearrange("p c s -> p (c s)")
            v.tensor_scalar(df, df, 0.0, None, ALU.max).then_inc(s["dsq"], 1)
            v.wait_ge(s["ld_l3"], 112)
            own(v.tensor_reduce(fal[:, 0:CH], f1[:], AX, ALU.add, apply_absolute_value=True))
            own(v.tensor_reduce(fal[:, CH:CH + 1], f2[:], AX, ALU.add, apply_absolute_value=True))
            own.settle()
            own(v.tensor_scalar(fal[:, 0:CH], fal[:, 0:CH], 1.0 / D, None, ALU.mult))
            own(v.tensor_scalar(fal[:, CH:CH + 1], fal[:, CH:CH + 1], 1.0 / FF, None, ALU.mult))
            w2v = f2[:].rearrange("p (c n) -> p c n", c=CH)
            for dst, src in ((fs, f1[:]), (ft, w2v)):
                own(v.tensor_scalar(dst[:], src, 0.0, None, ALU.is_gt))
                own(v.tensor_scalar(neg, src, 0.0, None, ALU.is_lt))
                own.settle()
                own(v.tensor_tensor(dst[:], dst[:], neg, ALU.subtract))
                own.settle()
            for c in range(CH):
                own(v.scalar_tensor_tensor(out=fs[:, c, :], in0=fs[:, c, :], scalar=fal[:, c:c + 1], in1=f1[:, c, :],
                                           op0=ALU.mult, op1=ALU.subtract))
            own(v.scalar_tensor_tensor(out=ft[:].rearrange("p c n -> p (c n)"),
                                       in0=ft[:].rearrange("p c n -> p (c n)"), scalar=fal[:, CH:CH + 1],
                                       in1=f2[:], op0=ALU.mult, op1=ALU.subtract))
            own.settle()
            own(v.tensor_tensor(fs, fs, f1[:], ALU.add))
            own(v.tensor_tensor(ft[:], ft[:], w2v, ALU.add))
            own.settle()
            v.sem_inc(s["fb_s"], 1)
            v.wait_ge(s["init_r"], 1)
            n_dp = HALF * 2 * G + HALF
            shift = [0] + list(range(LANES - 1))
            with v.Fori(0, ITERS) as it:
                for h in range(2):
                    k = [0]

                    def step(ins):
                        k[0] += 1
                        ins.then_inc(s["own_dp"], 1)

                    def settle():
                        v.wait_ge(s["own_dp"], (2 * it + h) * n_dp + k[0])

                    v.wait_ge(s[f"d_r{h}"], (it + 1) * 16)
                    v.wait_ge(s["codes"], 2 * it + h + 1)
                    for st in range(HALF):
                        r0 = st * G
                        prev = Rw[:, 1 - h, HS, :] if st == 0 else Rw[:, h, r0, :]
                        edge = Rw[:, 1 - h, HS - 1:HS + 1, W] if st == 0 else Rw[:, h, r0 - 1:r0 + 1, W]
                        for g in range(G):
                            if g:
                                prev = Rw[:, h, r0 + g, :]
                            step(v.tensor_tensor(mb[:, g, 1:W1C], prev[:, 0:W], prev[:, 1:W1C], ALU.min))
                            if not g:
                                step(v.stream_shuffle(mb[:, :, 0], edge, shift))
                            settle()
                            ins = v.tensor_tensor_scan(Rw[:, h, r0 + g + 1, :], mb[:, g, :], Dw[:, h, r0 + g, :],
                                                       BIG, ALU.min, ALU.add)
                            if st == HALF - 1 and g == G - 1:
                                ins.then_inc(s["rows_g"], 1)
                                v.wait_ge(s["rows_g"], 2 * it + h + 1)
                            else:
                                step(ins)
                                settle()
                        if st == 0:
                            step(v.tensor_copy(Rw[:, h, 0, :], Rw[:, 1 - h, HS, :]))
                    assert k[0] == n_dp, k[0]
            v.wait_ge(s["cs_r"], 16)
            own(v.tensor_scalar(pen, Cs, 0.5, 2 * FAR, ALU.min, ALU.mult))
            own(v.tensor_scalar(msk, Cs, -FAR, 1.25 * FAR, ALU.mult, ALU.add))
            own.settle()
            own(v.tensor_tensor(xn, pen, iot[:, 0:S].unsqueeze(1).broadcast_to([P, R, S]), ALU.add))
            own.settle()
            own(v.tensor_tensor(xn, xn, iotr[:], ALU.min))
            own.settle()
            own(v.tensor_tensor_scan(Nc.rearrange("p r j -> p (r j)"), msk.rearrange("p r j -> p (r j)"),
                                     xn.rearrange("p r j -> p (r j)"), 0.0, ALU.max, ALU.min))
            own(v.memset(Gp[:, :, 0:1], 0.0))
            own.settle()
            own(v.tensor_copy(Gp[:, 0, 1:S + 1], Nc[:, 0, :]))
            own.settle()
            for r in range(1, R):
                g0, g1 = (r - 1) % 2, r % 2
                own(v.tensor_tensor(Gx[:], Gp[:, g0, 0:S], pen[:, r, :], ALU.add))
                own.settle()
                own(v.tensor_tensor(Gx[:], Gx[:], Gp[:, g0, 1:S + 1], ALU.min))
                own.settle()
                to = Gb[:] if r == R - 1 else Gp[:, g1, 1:S + 1]
                ins = v.tensor_tensor_scan(to, msk[:, r, :], Gx[:], 0.0, ALU.max, ALU.min)
                if r == R - 1:
                    ins.then_inc(s["g_s"], 1)
                else:
                    own(ins)
                    own.settle()

            def lookup(lanes, at_, table, col, to, n=0):
                own(v.scalar_tensor_tensor(out=junk[0:lanes, n, :], in0=iot[0:lanes, 1:S + 1], scalar=at_[:, col],
                                           in1=table, op0=ALU.is_equal, op1=ALU.mult, accum_out=to))

            v.memset(ech[:, STRIPS - 1:STRIPS], float(S - 1)).then_inc(s["own_dve"], 1)
            own.n += 1
            own.settle()
            own(v.tensor_tensor_scan(Ac.rearrange("p r j -> p (r j)"), msk.rearrange("p r j -> p (r j)"),
                                     iotr[:].rearrange("p r j -> p (r j)"), 0.0, ALU.max, ALU.min))
            own.settle()
            v.wait_ge(s["g_r"], 16)
            for st in range(STRIPS - 1, 0, -1):
                lookup(B, ech, Ge[:, st, :], slice(st, st + 1), ech[:, st - 1:st])
                own.settle()
            v.sem_inc(s["e_s"], 1)
            v.wait_ge(s["e_r"], 16)
            for r in range(R - 1, -1, -1):
                lookup(P, el, Nc[:, r, :], slice(r + 1, r + 2), el[:, r:r + 1], 0)
                own.settle(1)
                lookup(P, el, Ac[:, r, :], slice(r + 1, r + 2), al[:, r:r + 1], 1)
                own(v.tensor_scalar(xn[:, r, :], iot[:, 1:S + 1], el[:, r + 1:r + 2], None, ALU.is_le))
                own.settle(2)
            own.settle()
            for r in range(R):
                own(v.scalar_tensor_tensor(out=Pm[:, r, :], in0=iot[:, 1:S + 1], scalar=al[:, r:r + 1],
                                           in1=xn[:, r, :], op0=ALU.is_ge, op1=ALU.mult))
            own.settle()
            v.sem_inc(s["p_s"], 1)
            for b in range(B):
                v.wait_ge(s["ex_p"], b + 1)
                add(2, b, PS[:, 2 + b, 0:S], 1)
                stats(3, b)
                norm(3, b)
            def routes(b):
                v.wait_ge(s["ln_y"], nth(3, b))
                own(v.tensor_tensor(ssum[:, 0, :], y[:, tiles(b), 0], y[:, tiles(b), 1], ALU.add))
                own.settle()
                own(v.tensor_scalar(ssum[:, 1, :], ssum[:, 0, :], -1.0, None, ALU.mult))
                own.settle()
                thb = thr[:].unsqueeze(1).broadcast_to([P, T, 17])
                own(v.tensor_tensor(cmp[:, 0:T, :], thb, ssum[:, 0, :].unsqueeze(2).broadcast_to([P, T, 17]),
                                    ALU.is_le))
                own(v.tensor_tensor(cmp[:, T:2 * T, :], thb, ssum[:, 1, :].unsqueeze(2).broadcast_to([P, T, 17]),
                                    ALU.is_gt))
                own.settle()
                own(v.tensor_reduce(cnt[:].rearrange("p a t -> p (a t)"), cmp[:], AX, ALU.add))
                own.settle()
                own(v.tensor_tensor(cnts[:], cnt[:, 0, :], cnt[:, 1, :], ALU.add))
                own.settle()
                for t in range(T):
                    own(v.tensor_scalar(hit[:, t], modt[:], cnts[:, t:t + 1], None, ALU.is_equal))
                own.settle()
                own(v.tensor_reduce(oh[:].rearrange("p t e -> p (t e)"),
                                    hit[:].rearrange("p t e m -> p (t e) m"), AX, ALU.add))
                own.settle()
                wb = wts[:, b % 2]
                own(v.tensor_tensor(wb, oh[:, :, 0:E1], oh[:, :, 1:E1 + 1], ALU.add))
                own.settle()
                v.tensor_scalar(wb, wb, 0.5, None, ALU.mult).then_inc(s["wt_s"], 1)

            def head_scores(b, qb):
                kk = 4 * (qb + 1)
                prs = [p_[:, 0:4 * kk * HD].rearrange("p (q k d) -> p q k d", q=4, d=HD) for p_ in (prod, prod2)]
                for t in range(T):
                    q4 = y[:, b * T + t, 32 * qb:32 * (qb + 1)].rearrange("p (q d) -> p q d", d=HD)
                    kv = cx[:, b * T + t, 0:kk * HD].rearrange("p (k d) -> p k d", d=HD)
                    own.settle(1)
                    own(v.tensor_tensor(prs[t], q4.unsqueeze(2).broadcast_to([P, 4, kk, HD]),
                                        kv.unsqueeze(1).broadcast_to([P, 4, kk, HD]), ALU.mult))
                for t in range(T):
                    own.settle(1)
                    own(v.tensor_reduce(sc[:, t, 4 * qb:4 * qb + 4, 0:kk], prs[t], AX, ALU.add))

            s2f = sc2[:].rearrange("p t q k -> p (t q) k")
            bc = [P, T * HEADS, HEADS]

            def head_shift(b):
                own.settle()
                for t in range(T):
                    own(v.scalar_tensor_tensor(out=sc2[:, t].rearrange("p q k -> p (q k)"),
                                               in0=sc[:, t].rearrange("p q k -> p (q k)"), scalar=HD ** -0.5,
                                               in1=cmask[:].rearrange("p q k -> p (q k)"),
                                               op0=ALU.mult, op1=ALU.add))
                own.settle()
                own(v.tensor_reduce(mx[:], s2f, AX, ALU.max))
                own.settle()
                v.tensor_tensor(s2f, s2f, mx[:].unsqueeze(2).broadcast_to(bc), ALU.subtract
                                ).then_inc(s["sc_s"], 1)

            def head_weights(b):
                v.wait_ge(s["sc_e"], b + 1)
                own(v.tensor_reduce(sm[:], s2f, AX, ALU.add))
                own.settle()
                own(v.reciprocal(sm[:], sm[:]))
                own.settle()
                own(v.tensor_tensor(s2f, s2f, sm[:].unsqueeze(2).broadcast_to(bc), ALU.mult))
                own.settle()

            def head_values(b, qb):
                kk = 4 * (qb + 1)
                prs = [p_[:, 0:4 * kk * HD].rearrange("p (q d k) -> p q d k", q=4, d=HD) for p_ in (prod, prod2)]
                for t in range(T):
                    kv = cx[:, b * T + t, 0:kk * HD].rearrange("p (k d) -> p d k", d=HD)
                    own.settle(1)
                    own(v.tensor_tensor(prs[t], sc2[:, t, 4 * qb:4 * qb + 4, 0:kk].unsqueeze(2)
                                        .broadcast_to([P, 4, HD, kk]),
                                        kv.unsqueeze(1).broadcast_to([P, 4, HD, kk]), ALU.mult))
                for t in range(T):
                    own.settle(1)
                    own(v.tensor_reduce(acc[:, b % 2, t, 32 * qb:32 * (qb + 1)]
                                        .rearrange("p (q d) -> p q d", d=HD), prs[t], AX, ALU.add))

            def head_add(b):
                own.settle()
                add(4, b, acc[:, b % 2].rearrange("p t d -> p (t d)"), 2)

            v.wait_ge(s["padded"], 3)
            v.wait_ge(s["ld_tab"], 64)
            routes(0)
            v.wait_ge(s["wt_s"], 1)
            for b in range(B):
                v.wait_ge(s["b2_p"], b + 1)
                ab = acc[:, b % 2]
                v.tensor_copy(ab.rearrange("p t d -> p (t d)"), PS[:, 0, 0:S]).then_inc(s["b2_s"], 1)
                if b:
                    norm(4, b - 1)
                    v.wait_ge(s["ln_y"], nth(4, b - 1))
                v.wait_ge(s["b2_s"], b + 1)
                for e in range(E1):
                    if b:
                        for qb in ((0, 1), (2,), (3,))[e] if e < 3 else ():
                            head_scores(b - 1, qb)
                        if e == 3:
                            head_shift(b - 1)
                        if e == 5:
                            head_weights(b - 1)
                        for qb in ((0, 1), (2,), (3,))[e - 5] if e >= 5 else ():
                            head_values(b - 1, qb)
                    if b + 1 < B and e == 4:
                        routes(b + 1)
                    n = E1 * b + e
                    v.wait_ge(s["mm2_p"], n + 1)
                    if n:
                        v.wait_ge(s["mm2_s"], n)
                    for t in range(T):
                        ins = v.scalar_tensor_tensor(out=ab[:, t, :], in0=PS[:, 6 + n % 2, t * D:(t + 1) * D],
                                                     scalar=wts[:, b % 2, t, e:e + 1], in1=ab[:, t, :],
                                                     op0=ALU.mult, op1=ALU.add)
                    ins.then_inc(s["mm2_s"], 1)
                if b:
                    head_add(b - 1)
                v.wait_ge(s["mm2_s"], E1 * (b + 1))
                add(3, b, ab.rearrange("p t d -> p (t d)"), 5)
                stats(4, b)
                if b:
                    v.wait_ge(s["x4"], b)
            norm(4, B - 1)
            v.wait_ge(s["ln_y"], nth(4, B - 1))
            def gate_shift(b):
                v.wait_ge(s["lg_p"], b + 1)
                lp = PS[:, 1, 0:T * E2].rearrange("p (t e) -> p t e", e=E2)
                own(v.tensor_reduce(lmx[:], lp, AX, ALU.max))
                own.settle()
                v.tensor_tensor(lg[:], lp, lmx[:].unsqueeze(2).broadcast_to([P, T, E2]), ALU.subtract
                                ).then_inc(s["lg_s"], 1)

            def gates_open(b):
                v.wait_ge(s["lg_e"], b + 1)
                own(v.tensor_reduce(lsm[:], lg[:], AX, ALU.add))
                own.settle()
                own(v.reciprocal(lsm[:], lsm[:]))
                own.settle()
                own(v.tensor_tensor(lg[:], lg[:], lsm[:].unsqueeze(2).broadcast_to([P, T, E2]), ALU.mult))
                own.settle()
                v.tensor_scalar(gm[:], lg[:], 0.5, None, ALU.is_gt).then_inc(s["gm_s"], 1)

            def mix(b, h):
                ab = acc[:, b % 2]
                if h == 0:
                    v.wait_ge(s["gm_s"], b + 1)
                    v.wait_ge(s["eb_p"], b + 1)
                    own(v.tensor_copy(ab.rearrange("p t d -> p (t d)"), PS[:, 1, 0:S]))
                    own.settle()
                v.wait_ge(s["e2_p"], 2 * b + h + 1)
                for e in range(4):
                    for t in range(T):
                        own.settle(1)
                        own(v.scalar_tensor_tensor(out=ab[:, t, :],
                                                   in0=PS[:, ((0, 2), (3, 0))[h][t], e * D:(e + 1) * D],
                                                   scalar=gm[:, t, 4 * h + e:4 * h + e + 1], in1=ab[:, t, :],
                                                   op0=ALU.mult, op1=ALU.add))
                own.settle()
                if h == 0:
                    v.sem_inc(s["e2_s"], 1)
                else:
                    add(5, b, ab.rearrange("p t d -> p (t d)"), 6)

            def rotate(b):
                v.wait_ge(s["k3_p"], b + 1)
                own(v.tensor_tensor(rq, PS[:, 4, 0:S], xcos[:, 0, :], ALU.mult))
                own(v.tensor_tensor(rtmp, PS[:, 4, S:2 * S], xsin[:, 0, :], ALU.mult))
                own.settle()
                v.tensor_tensor(rq, rq, rtmp, ALU.add).then_inc(s["k3_s"], 1)

            def decayed(b):
                v.wait_ge(s["rt_p"], b + 1)
                for t in range(T):
                    ins = v.tensor_tensor(ret[:, t, :], PS[:, 4, t * S:(t + 1) * S], decay[:, t, :], ALU.mult)
                ins.then_inc(s["rt_s"], 1)

            for n in range(B + 2):
                ba, br, bf = n, n - 1, n - 2
                do_a, do_r, do_f = ba < B, 0 <= br < B, 0 <= bf
                now = [(L, b) for L, b in PIPE if b + L - 5 == n]
                for L, b in now:
                    v.wait_ge(s[f"x{L - 1}"], b + 1)
                    for t in range(T):
                        own(v.bn_stats(st6[:, b * T + t, :], x[:, b * T + t, :]))
                own.settle()
                for L, b in now:
                    for t in range(T):
                        own(v.bn_aggr(mv[:, b * T + t, :], st6[:, b * T + t, :]))
                own.settle()
                v.tensor_scalar(veps[:, together(n)], mv[:, together(n), 1], EPS, None, ALU.add
                                ).then_inc(s["ln_mv"], 1)
                if n < 2:
                    head_scores(B - 1, 2 * n)
                for L, b in now:
                    norm(L, b)
                if n < 2:
                    head_scores(B - 1, 2 * n + 1)
                elif n == 2:
                    head_values(B - 1, 0)
                if do_a:
                    gate_shift(ba)
                if n == 1:
                    head_shift(B - 1)
                if do_a:
                    gates_open(ba)
                if n == 2:
                    head_values(B - 1, 1)
                if do_r:
                    rotate(br)
                if do_a:
                    mix(ba, 0)
                if do_r:
                    decayed(br)
                if n == 2:
                    head_values(B - 1, 2)
                if do_a:
                    mix(ba, 1)
                if n == 1:
                    head_weights(B - 1)
                if n == 2:
                    head_values(B - 1, 3)
                    head_add(B - 1)
                if do_r:
                    v.wait_ge(s["ro_p"], br + 1)
                    add(6, br, PS[:, 5, 0:S], 3)
                if do_f:
                    v.wait_ge(s["f3_p"], bf + 1)
                    add(7, bf, PS[:, 6, 0:S], 7)


_INS = ["x", "ctx_1024", "g_xattn", "g_ffn", "L0_xattn_W_q", "L0_xattn_W_k", "L0_xattn_W_v", "L0_xattn_W_o",
        "L0_xattn_b_o", "L0_ffn_W", "L0_ffn_b", "L0_ffn_ids", "L0_ffn_weights", "L1_ffn_W1", "L1_ffn_b1",
        "L1_ffn_W2", "L1_ffn_b2", "L2_ffn_Wr", "L2_ffn_br", "L2_ffn_We", "L2_ffn_be", "L3_xattn_Wq",
        "L3_xattn_Wk", "L3_xattn_Wv", "L3_ffn_w1", "L3_ffn_b1", "L3_ffn_w2", "L3_ffn_b2"]


def tables():
    f = np.float32
    base = (np.arange(0, D, 2, dtype=f) + f(0.4 * D)) / f(1.4 * D)
    pos = np.arange(0, S, dtype=f)
    scale = (base[None, :] ** (pos[:, None] / f(512.0))).astype(f)
    freqs = (f(1.0) / f(10000.0) ** (np.arange(D // 2, dtype=f) / f(D // 2))).astype(f)
    arg = (pos[:, None] * freqs[None, :]).astype(f)
    sin, cos = np.sin(arg), np.cos(arg)
    both = lambda m: np.repeat(m, 2, axis=-1).T
    inv = f(1.0) / scale
    t_cos = np.stack([both(cos * scale), both(cos * inv)], 1).astype(f)
    t_sin = np.stack([both(sin * scale), both(sin * inv)], 1).astype(f)
    q, k = np.arange(S)[None, :], np.arange(S)[:, None]
    decay = np.where(q >= k, np.float64(0.96875) ** np.maximum(q - k, 0), 0.0).astype(f)
    decay = decay.reshape(T, P, S).transpose(1, 0, 2)
    causal = np.where(np.tril(np.ones((HEADS, HEADS), bool)), 0.0, NEG).astype(f)
    causal = np.broadcast_to(causal, (P, HEADS, HEADS))
    p = np.arange(P)
    split = -np.stack([p // HD % 2, p // (2 * HD) % 2, p % 2], 1).astype(f)
    sel = (p[:, None] % 32 // 2 == np.arange(NJ)[None, :]).astype(f)
    return {"t_split": split, "t_sel": sel, "t_cos": t_cos, "t_sin": t_sin, "t_decay": decay, "t_causal": causal}


def kernel(**inputs):
    import numpy as _np
    import concourse.bacc as _bacc
    from concourse import mybir as _mybir
    from concourse.bass_utils import run_bass_kernel_spmd as _run

    nc = _bacc.Bacc("TRN2", target_bir_lowering=False, num_devices=1)
    arrays, args = {}, {}
    data = {n: inputs[n] for n in _INS}
    data.update(tables())
    for name, val in data.items():
        arr = _np.ascontiguousarray(val)
        arrays[f"in_{name}"] = arr
        args[name] = nc.dram_tensor(f"in_{name}", arr.shape, _mybir.dt.from_np(arr.dtype), kind="ExternalInput").ap()
    out = nc.dram_tensor("out_0", (B, S, D), _mybir.dt.float32, kind="ExternalOutput").ap()
    build(nc, args, out)
    r = _run(nc, [arrays], core_ids=[0])
    return r.results[0]["out_0"]
```

```python
from contextlib import ExitStack

import numpy as np
import concourse.bass as bass
from concourse import mybir

F32 = mybir.dt.float32
F32R = mybir.dt.float32r
BF16 = mybir.dt.bfloat16
I32 = mybir.dt.int32
ALU = mybir.AluOpType
ACT = mybir.ActivationFunctionType
AX = mybir.AxisListType.X

B, S, D = 4, 256, 128
P = 128
T = S // P
NT = B * T
HEADS, HD = 16, 8
NJ, NI = 4, 4
E1, FF = 8, 512
CH = FF // P
E2 = 8
NA, KA = 32, 8
EPS = 1e-5
BIG = 1e30
NEG = -1e18

LANES = 32
W = S // LANES
G = 2
W1C = W + 1
LAGMAX = G * (LANES - 1)
HALF = 16
HS = HALF * G
SLOTS = -(-(S + LAGMAX) // (2 * HS)) * 2 * HS
ITERS = SLOTS // (2 * HS)
ROWS = LAGMAX + SLOTS
R = 8
STRIPS = S // R
FAR = 1e4


PIPE = [(L, n - (L - 5)) for n in range(B + 2) for L in (5, 6, 7) if 0 <= n - (L - 5) < B]
ORDER = ([(0, b) for b in range(B)] + [(L, b) for b in range(B) for L in (1, 2)]
         + [(L, b) for L in (3, 4) for b in range(B)] + PIPE)
ORDER_T = ([(0, 0)] + [o for b in range(B + 1) for o in ((0, b + 1), (1, b - 1), (2, b - 1)) if 0 <= o[1] < B]
           + [(3, b) for b in range(B)] + PIPE)


class Steps:

    def __init__(self, eng, sem):
        self.eng, self.sem, self.n = eng, sem, 0

    def __call__(self, ins):
        self.n += 1
        ins.then_inc(self.sem, 1)

    def settle(self, but=0):
        self.eng.wait_ge(self.sem, self.n - but)


def build(nc, a, out):
    with ExitStack() as ctx:
        def sb(name, shape, dt=F32):
            return ctx.enter_context(nc.sbuf_tensor(name, shape, dt))

        def sem(name):
            return ctx.enter_context(nc.semaphore(name))

        with ExitStack() as l0:
            def early(name, shape):
                return l0.enter_context(nc.sbuf_tensor(name, shape, F32R))

            qk = early("qk", [P, NJ, 2, S]); mT = early("mT", [P, 2, S]); sel = early("sel", [P, NJ, P])
        cd = sb("cd", [P, 6, HS // 2, W])
        Cw = sb("Cw", [P, SLOTS * W], BF16)
        Dw = sb("Dw", [P, 2, HS, W1C])
        junk = sb("junk", [P, 2, S])
        Gp = sb("Gp", [P, 2, S + 1], BF16)
        x = sb("x", [P, NT, D])
        cx = sb("cx", [P, NT, D])
        cxT = sb("cxT", [P, B, S])
        y = sb("y", [P, NT, D])
        yT = sb("yT", [P, B, S])
        st6 = sb("st6", [P, NT, 6])
        mv = sb("mv", [P, NT, 2])
        veps = sb("veps", [P, NT])
        rstd = sb("rstd", [P, NT])
        halfc = sb("halfc", [P, NT])
        gate = sb("gate", [P, 8])
        ident = sb("ident", [P, P])
        warm = sb("warm", [P, 2 * (B + 2)])
        identb = sb("identb", [P, P], BF16)
        ones = sb("ones", [P, P])
        wq = sb("wq", [P, D]); wk = sb("wk", [P, D]); wv = sb("wv", [P, D]); wo = sb("wo", [P, D])
        wqp = sb("wqp", [P, NJ, P]); wkp = sb("wkp", [P, NJ, P])
        spl = sb("spl", [P, 3]); selc = sb("selc", [P, NJ])
        rows = sb("rows", [1, 2, D])
        Z = sb("Z", [P, 4 * R * S])

        def part(at, *shape):
            n = int(np.prod(shape))
            names = "abcd"[:len(shape)]
            v = Z[:, at:at + n]
            if len(shape) == 1:
                return v
            return v.rearrange(f"p ({' '.join(names)}) -> p {' '.join(names)}", **dict(zip(names, shape)))

        qkh = part(0, NJ, 2, S).bitcast(F32R)
        mneg = part(2 * NJ * S, 2, T, P)
        mTh = part(2 * NJ * S + 2 * T * P, 2, S).bitcast(F32R)
        Ge = Z[0:B, 0:STRIPS * S // 2].bitcast(BF16).rearrange("p (n s) -> p n s", n=STRIPS)
        rq, ret = part(0, S), part(2 * S, T, S)
        rtmp = part(S, S)
        hg = part(6 * S, CH, S)
        xn, msk, Nc = (part(n * R * S, R, S) for n in (1, 2, 3))
        pen = Z[:, 0:R * S // 2].bitcast(BF16).rearrange("p (r s) -> p r s", r=R)
        hT = part(0, 2 * CH, S)
        uT = part(4 * NJ * S, NJ, S)
        vaug = part(5 * NJ * S, T, HEADS, 32)
        big = sb("big", [P, T * HEADS * S])
        pT = big[:].rearrange("p (t h s) -> p t h s", t=T, h=HEADS)
        w1 = big[:, 0:E1 * FF].rearrange("p (e f) -> p e f", e=E1)
        w2 = big[:, E1 * FF:2 * E1 * FF].rearrange("p (e c d) -> p e c d", e=E1, c=CH)
        rden = sb("rden", [P, T * HEADS])
        o = sb("o", [P, T, D])
        oT = sb("oT", [P, S])
        ads = sb("ads", [P, KA, D])
        adb = sb("adb", [KA, D])
        wB = sb("wB", [P, KA]); wc = sb("wc", [KA, 1]); wrow = sb("wrow", [KA, P])
        v3 = ads[:].rearrange("p (b t) d -> p b t d", t=T)
        kturn = [w[:].rearrange("p (b t) n -> p b (t n)", t=T) for w in (wqp, wkp)]
        rk = [kturn[b // 2][:, b % 2, :] for b in range(B)]
        weff = sb("weff", [P, D]); weffT = sb("weffT", [P, D])
        idsb = sb("idsb", [1, KA], I32)
        sq = sb("sq", [P, S])
        Y = sb("Y", [P, R * S])
        sqc = Y[:, 0:B * S].rearrange("p (b s) -> p b s", b=B)
        crem = Y[:, B * S:2 * B * S]
        dsum = Y[:].rearrange("p (c s) -> p c s", c=W)
        Ac = Y[:].rearrange("p (r s) -> p r s", r=R)
        aab = sb("aab", [P, S]); bbk = sb("bbk", [P, W])
        Dun = sb("Dun", [P, ROWS, W1C])
        Rw = sb("Rw", [P, 2, HS + 1, W1C])
        mb = sb("mb", [P, G, W1C])
        late = [Dun[:].rearrange("p r c -> p (r c)")[:, n * R * S // 2:(n + 1) * R * S // 2].bitcast(BF16)
                for n in range(3)]
        Cl = late[0].rearrange("p (s w) -> p s w", w=W)
        CT = late[1].rearrange("p (b t s) -> p b t s", t=T, b=B)
        Cs = late[2].rearrange("p (r s) -> p r s", r=R)
        Pi = late[0].rearrange("p (b t s) -> p b t s", t=T, b=B)
        Pm = late[1].rearrange("p (r s) -> p r s", r=R)
        prod2 = Dun[:].rearrange("p r c -> p (r c)")[:, R * S:R * S + 4 * HEADS * HD]
        iot = sb("iot", [P, S + 1]); ioti = sb("ioti", [P, S + 1], I32)
        iotr = sb("iotr", [P, R, S])
        Gx = sb("Gx", [P, S], BF16)
        ech = sb("ech", [B, STRIPS])
        el = sb("el", [P, R + 1]); al = sb("al", [P, R])
        Gb = sb("Gb", [P, S], BF16)
        c3 = sb("c3", [P, 3, NT * D], BF16)
        b1r = sb("b1r", [E1 * CH, P]); b1c = sb("b1c", [P, E1 * CH])
        b2r = sb("b2r", [E1, D])
        thr = sb("thr", [P, 17]); modt = sb("modt", [P, 9, 7]); modi = sb("modi", [P, 63], I32)
        thri = sb("thri", [P, 17], I32)
        ssum = sb("ssum", [P, 2, T]); cmp = sb("cmp", [P, 2 * T, 17]); cnt = sb("cnt", [P, 2, T])
        cnts = sb("cnts", [P, T]); hit = sb("hit", [P, T, 9, 7]); oh = sb("oh", [P, T, 9])
        wts = sb("wts", [P, 2, T, E1]); wtsT = sb("wtsT", [E1, S])
        acc = sb("acc", [P, 2, T, D])
        prod = sb("prod", [P, 4 * HEADS * HD])
        sc = sb("sc", [P, T, HEADS, HEADS]); sc2 = sb("sc2", [P, T, HEADS, HEADS])
        cmask = sb("cmask", [P, HEADS, HEADS])
        mx = sb("mx", [P, T * HEADS]); sm = sb("sm", [P, T * HEADS])
        wrT = sb("wrT", [P, E2]); wrr = sb("wrr", [E2, D]); brr = sb("brr", [1, E2])
        We = sb("We", [P, E2, D]); WeT = sb("WeT", [P, E2, D]); ber = sb("ber", [E2, D])
        lg = sb("lg", [P, T, E2]); lmx = sb("lmx", [P, T]); lsm = sb("lsm", [P, T])
        gm = sb("gm", [P, T, E2]); gmT = sb("gmT", [E2, S])
        w3 = sb("w3", [P, 3, D]); w3T = sb("w3T", [P, 5, D])
        xcos = sb("xcos", [P, 2, S]); xsin = sb("xsin", [P, 2, S]); decay = sb("decay", [P, T, S])
        f1 = sb("f1", [P, CH, D]); f2 = sb("f2", [P, FF]); fs = prod[:].rearrange("p (c d) -> p c d", c=CH); ft = sb("ft", [P, CH, D])
        fal = sb("fal", [P, CH + 1])
        neg = acc[:].rearrange("p a t d -> p (a t) d")
        f1T = sb("f1T", [P, CH, P]); f2T = sb("f2T", [P, CH, D])
        f1br = sb("f1br", [CH, P]); f1bc = sb("f1bc", [P, CH])
        PS = ctx.enter_context(nc.psum_tensor("PS", [P, 8, 512], F32))

        dD = nc.dram_tensor("dD", (P, ROWS * W1C), F32, kind="Internal").ap()
        dC = nc.dram_tensor("dC", (P, SLOTS * W), BF16, kind="Internal").ap()
        dCr = nc.dram_tensor("dCr", (B, S, S), BF16, kind="Internal").ap()
        dP = nc.dram_tensor("dP", (B, S, S), BF16, kind="Internal").ap()

        names = """ln_mv ln_rstd ln_y ln_T ln_yT ld_x ld_cx ld_w0 ld_gate ld_ids ld_ads ld_mix ld_moe ld_l2 ld_l3 ld_tab cst cst_v
            own_dve own_dp own_pool turns init_r lg_s gates padded padq
            cxT_p cxT_s q0_p q0_h q0_s v_p v_s s_p s_m mn_s qm_p qm_h qm_s st_p st_e pv_p uT_s un_p o_n oT_p oT_s at_p x0
            weff_s weffT_p weffT_s f0_p x1
            sq_s sqc_s aabb_p aabb_s dsq d_s d_w d_r0 d_r1 rows_g codes codes_w cl_r clT_p ct_s ct_w cs_r
            g_s g_r e_s e_r p_s p_w p_r ex_p x2 c3_s
            b1_s wt_s wtT_p wtT_s b2_p b2_s mm1_p mm1_s mm2_p mm2_s x3
            sc_s sc_e x4 weT_p weT_s lg_p lg_e gm_s gmT_p gmT_s eb_p e2_p e2_s x5
            w3T_p w3T_s kc_p kc_s rk_s k3_p k3_s v3_p v3_s rt_p rt_s ro_p x6
            fb_s fT_p fT_s h3_p h3_s f3_p x7 st_out""".split()
        s = {n: sem(n) for n in names}

        block = ctx.enter_context(nc.Block())

        def nth(L, b):
            return ORDER.index((L, b)) + 1

        def nth_T(L, b):
            return ORDER_T.index((L, b)) + 1

        def lnbank(L, b):
            return {0: 7, 1: 6, 2: 6, 3: 0, 5: 1, 6: 4, 7: 6}[L]

        def tiles(b):
            return slice(b * T, (b + 1) * T)

        def together(n):
            return slice(max(n - 2, 0) * T, min(n + 1, B) * T)

        @block.sync
        def _(sp):
            xin = a["x"].rearrange("b (t p) d -> p (b t) d", p=P)
            cin = a["ctx_1024"].rearrange("b (t p) d -> p (b t) d", p=P)
            sp.dma_start(x[:], xin).then_inc(s["ld_x"], 16)
            sp.dma_start(cx[:], cin).then_inc(s["ld_cx"], 16)
            for dst, nm in ((wq, "W_q"), (wk, "W_k"), (wv, "W_v"), (wo, "W_o")):
                sp.dma_start(dst[:], a["L0_xattn_" + nm]).then_inc(s["ld_w0"], 16)
            sp.dma_start(spl[:], a["t_split"]).then_inc(s["ld_w0"], 16)
            sp.dma_start(selc[:], a["t_sel"]).then_inc(s["ld_w0"], 16)
            sp.dma_start(rows[0:1, 0, :], a["L0_xattn_b_o"][None, :]).then_inc(s["ld_w0"], 16)
            for n, nm in enumerate(("g_xattn", "g_ffn")):
                sp.dma_start(gate[:, 4 * n:4 * n + 4],
                             a[nm][None, :].partition_broadcast(P)).then_inc(s["ld_gate"], 16)
            sp.dma_start(idsb[:], a["L0_ffn_ids"][None, :]).then_inc(s["ld_ids"], 16)
            sp.dma_start(wB[:], a["L0_ffn_weights"][None, :].partition_broadcast(P)).then_inc(s["ld_mix"], 16)
            sp.dma_start(wc[:], a["L0_ffn_weights"][:, None]).then_inc(s["ld_mix"], 16)
            sp.wait_ge(s["ld_ids"], 16)
            for k in range(KA):
                i = sp.value_load(idsb[0:1, k:k + 1], min_val=0, max_val=NA - 1)
                sp.dma_start(ads[:, k, :], a["L0_ffn_W"][bass.ds(i, 1), :, :].rearrange("a o d -> (a o) d")
                             ).then_inc(s["ld_ads"], 16)
                sp.dma_start(adb[k:k + 1, :], a["L0_ffn_b"][bass.ds(i, 1), :]).then_inc(s["ld_ads"], 16)
            sp.dma_start(b1r[:], a["L1_ffn_b1"].rearrange("e (c p) -> (e c) p", p=P)).then_inc(s["ld_moe"], 16)
            sp.dma_start(b2r[:], a["L1_ffn_b2"]).then_inc(s["ld_moe"], 16)
            sp.dma_start(wrr[:], a["L2_ffn_Wr"]).then_inc(s["ld_l2"], 16)
            sp.dma_start(brr[:], a["L2_ffn_br"][None, :]).then_inc(s["ld_l2"], 16)
            sp.dma_start(We[:], a["L2_ffn_We"].rearrange("e d c -> d e c")).then_inc(s["ld_l2"], 16)
            sp.dma_start(ber[:], a["L2_ffn_be"]).then_inc(s["ld_l2"], 16)
            for n, nm in enumerate(("Wq", "Wk", "Wv")):
                sp.dma_start(w3[:, n, :], a["L3_xattn_" + nm]).then_inc(s["ld_l3"], 16)
            sp.dma_start(f1[:], a["L3_ffn_w1"].rearrange("(c p) d -> p c d", p=P)).then_inc(s["ld_l3"], 16)
            sp.dma_start(f2[:], a["L3_ffn_w2"]).then_inc(s["ld_l3"], 16)
            sp.dma_start(f1br[:], a["L3_ffn_b1"].rearrange("(c p) -> c p", p=P)).then_inc(s["ld_l3"], 16)
            sp.dma_start(rows[0:1, 1, :], a["L3_ffn_b2"][None, :]).then_inc(s["ld_l3"], 16)
            sp.dma_start(xcos[:], a["t_cos"]).then_inc(s["ld_tab"], 16)
            sp.dma_start(xsin[:], a["t_sin"]).then_inc(s["ld_tab"], 16)
            sp.dma_start(decay[:], a["t_decay"]).then_inc(s["ld_tab"], 16)
            sp.dma_start(cmask[:], a["t_causal"]).then_inc(s["ld_tab"], 16)
            sp.wait_ge(s["pv_p"], 2 * B)
            sp.dma_start(w1, a["L1_ffn_W1"].rearrange("e d f -> d e f")).then_inc(s["ld_moe"], 16)
            sp.dma_start(w2, a["L1_ffn_W2"].rearrange("e (c p) d -> p e c d", p=P)).then_inc(s["ld_moe"], 16)
            sp.wait_ge(s["d_s"], W)
            sp.wait_ge(s["padded"], 3)
            sp.wait_ge(s["padq"], B)
            first = (LAGMAX + 2 * HS) * W1C
            table = Dun[:].rearrange("p r c -> p (r c)")
            sp.dma_start(dD[:, 0:first], table[:, 0:first]).then_inc(s["d_w"], 16)
            sp.wait_ge(s["d_w"], 16)

            skew = bass.AP(tensor=dD.tensor, offset=LAGMAX * W1C,
                           ap=[[LANES * ROWS * W1C, B], [ROWS * W1C - G * W1C, LANES], [1, SLOTS * W1C]])
            HW = HS * W1C
            for h in range(2):
                sp.dma_start(Dw[:, h].rearrange("p r c -> p (r c)"), skew[:, :, h * HW:(h + 1) * HW]
                             ).then_inc(s[f"d_r{h}"], 16)
            sp.dma_start(dD[:, first:], table[:, first:]).then_inc(s["d_w"], 16)
            sp.wait_ge(s["d_w"], 32)
            with sp.Fori(0, ITERS - 1) as it:
                for h in range(2):
                    sp.wait_ge(s["rows_g"], (2 * it + h) * 2 + 2)
                    sp.dma_start(Dw[:, h].rearrange("p r c -> p (r c)"),
                                 skew[:, :, bass.ds((2 * it + 2 + h) * HW, HW)]).then_inc(s[f"d_r{h}"], 16)
            sp.wait_ge(s["codes"], 4 * ITERS + 4)
            sp.dma_start(dC, Cw[:]).then_inc(s["codes_w"], 16)
            sp.wait_ge(s["codes_w"], 16)
            sp.dma_start(Cl.rearrange("p r c -> p (r c)"),
                         bass.AP(tensor=dC.tensor, offset=0,
                                 ap=[[LANES * SLOTS * W, B], [SLOTS * W + G * W, LANES], [1, S * W]])
                         ).then_inc(s["cl_r"], 16)
            sp.wait_ge(s["ct_s"], T)
            sp.dma_start(dCr.rearrange("b (t p) j -> p (b t) j", p=P), CT.rearrange("p b t s -> p (b t) s")).then_inc(s["ct_w"], 16)
            sp.wait_ge(s["ct_w"], 16)
            sp.dma_start(Cs.rearrange("p r j -> p (r j)"), dCr.rearrange("b (s r) j -> (b s) (r j)", r=R)
                         ).then_inc(s["cs_r"], 16)
            sp.wait_ge(s["g_s"], 1)
            sp.dma_start(Ge.rearrange("b s j -> b (s j)"), Gb[:]).then_inc(s["g_r"], 16)
            sp.wait_ge(s["e_s"], 1)
            sp.dma_start(el[:, R:R + 1], ech[:]).then_inc(s["e_r"], 16)
            sp.wait_ge(s["p_s"], 1)
            sp.dma_start(dP.rearrange("b (s r) j -> (b s) (r j)", r=R), Pm.rearrange("p r j -> p (r j)")
                         ).then_inc(s["p_w"], 16)
            sp.wait_ge(s["p_w"], 16)
            sp.dma_start(Pi.rearrange("p b t s -> p (b t) s"), dP.rearrange("b (t p) j -> p (b t) j", p=P)).then_inc(s["p_r"], 16)
            outv = out.rearrange("b (t p) d -> p (b t) d", p=P)
            for b in range(B):
                sp.wait_ge(s["x7"], b + 1)
                sp.dma_start(outv[:, tiles(b), :], x[:, tiles(b), :]).then_inc(s["st_out"], 16)
            sp.wait_ge(s["st_out"], 16 * B)

        @block.gpsimd
        def _(pool):
            own = Steps(pool, s["own_pool"])
            own(pool.memset(ident[:], 0.0))
            own(pool.memset(halfc[:], -0.5))
            pool.memset(ones[:], 1.0).then_inc(s["cst"], 1)
            own.settle()
            pool.affine_select(out=ident[:], in_=ident[:], compare_op=ALU.not_equal, fill=1.0, base=0,
                               pattern=[[-1, P]], channel_multiplier=1).then_inc(s["cst"], 1)
            pool.memset(mneg, 0.0).then_inc(s["cst"], 1)
            own(pool.memset(vaug, 0.0))
            own.settle()
            pool.memset(vaug[:, :, :, HD:HD + 1], 1.0).then_inc(s["cst"], 1)
            pool.iota(ioti[:], pattern=[[1, S + 1]], base=-1, channel_multiplier=0).then_inc(s["cst"], 1)
            pool.iota(thri[:], pattern=[[1, 17]], base=1, channel_multiplier=0).then_inc(s["cst"], 1)
            pool.iota(modi[:], pattern=[[1, 9], [8, 7]], base=-8, channel_multiplier=0).then_inc(s["cst"], 1)

            def inv_std(L, b):
                pool.wait_ge(s["ln_mv"], nth(L, b))
                pool.tensor_tensor(rstd[:, tiles(b)], veps[:, tiles(b)], halfc[:, tiles(b)], ALU.pow
                                   ).then_inc(s["ln_rstd"], 1)

            def rstds(L):
                for b in range(B):
                    inv_std(L, b)

            rstds(0)
            pool.memset(Dun[:, 0:LAGMAX, :], BIG).then_inc(s["padded"], 1)
            pool.memset(Dun[:, LAGMAX + S:ROWS, :], 0.0).then_inc(s["padded"], 1)
            own(pool.memset(Dun[:, LAGMAX:LAGMAX + S, 0:1], 0.0))
            own.settle()
            for b in range(B):
                pool.memset(Dun[b * LANES:b * LANES + 1, LAGMAX:LAGMAX + S, 0:1], BIG).then_inc(s["padq"], 1)
                pool.wait_ge(s["padq"], b + 1)
            own(pool.memset(Rw[:, 1, HS - 1:HS + 1, :], BIG))
            own.settle()
            for b in range(B):
                own(pool.memset(Rw[b * LANES:b * LANES + 1, 1, HS:HS + 1, 0:1], 0.0))
                own.settle()
            own.settle()
            pool.sem_inc(s["init_r"], 1)
            pool.memset(sc[:], 0.0).then_inc(s["padded"], 1)
            pool.wait_ge(s["ld_cx"], 16)
            cf = cx[:].rearrange("p t d -> p (t d)")
            own(pool.tensor_copy(c3[:, 0, :], cf))
            own.settle()
            own(pool.tensor_tensor(crem, cf, c3[:, 0, :], ALU.subtract))
            own.settle()
            own(pool.tensor_copy(c3[:, 1, :], crem))
            own.settle()
            own(pool.tensor_tensor(crem, crem, c3[:, 1, :], ALU.subtract))
            own.settle()
            pool.tensor_copy(c3[:, 2, :], crem).then_inc(s["c3_s"], 1)
            for b in range(B):
                inv_std(1, b)
                inv_std(2, b)
            pool.sem_inc(s["codes"], 4)
            n_code = 7
            with pool.Fori(0, ITERS) as it:
                for h in range(2):
                    for part_ in range(2):
                        k = [0]
                        nth_part = (2 * it + h) * 2 + part_

                        def step(ins):
                            k[0] += 1
                            ins.then_inc(s["own_pool"], 1)

                        def settle():
                            pool.wait_ge(s["own_pool"], own.n + nth_part * n_code + k[0])
                            pool.sem_inc(s["turns"], 1)

                        pool.wait_ge(s["rows_g"], nth_part + 1)
                        r0 = part_ * HS // 2
                        dg = Rw[:, h, r0:r0 + HS // 2, 0:W]
                        up = Rw[:, h, r0:r0 + HS // 2, 1:W + 1]
                        lf = Rw[:, h, r0 + 1:r0 + HS // 2 + 1, 0:W]
                        step(pool.tensor_tensor(cd[:, 0], dg, up, ALU.subtract))
                        step(pool.tensor_tensor(cd[:, 1], dg, lf, ALU.subtract))
                        step(pool.tensor_tensor(cd[:, 2], up, lf, ALU.subtract))
                        settle()
                        step(pool.tensor_scalar(cd[:, 3], cd[:, 0], 0.0, None, ALU.is_gt))
                        step(pool.tensor_scalar(cd[:, 4], cd[:, 1], 0.0, None, ALU.is_gt))
                        step(pool.tensor_scalar(cd[:, 5], cd[:, 2], 0.0, 0.5, ALU.is_gt, ALU.add))
                        settle()
                        step(pool.tensor_tensor(cd[:, 0], cd[:, 3], cd[:, 4], ALU.add))
                        settle()
                        assert k[0] == n_code
                        pool.tensor_tensor(Cw[:, bass.ds(nth_part * (HS // 2 * W), HS // 2 * W)],
                                           cd[:, 0].rearrange("p r c -> p (r c)"),
                                           cd[:, 5].rearrange("p r c -> p (r c)"), ALU.mult
                                           ).then_inc(s["codes"], 1)
                        pool.wait_ge(s["codes"], nth_part + 5)
            own.n += 4 * ITERS * n_code
            pool.wait_ge(s["ld_tab"], 64)
            kc = ft[:].rearrange("p (n c) d -> p n (c d)", n=2)
            for b in range(B):
                pool.wait_ge(s["kc_s"], b + 1)
                own(pool.tensor_tensor(rk[b], kc[:, 0, :], xcos[:, 1, :], ALU.mult))
                own(pool.tensor_tensor(kc[:, 1, :], kc[:, 1, :], xsin[:, 1, :], ALU.mult))
                own.settle()
                pool.tensor_tensor(rk[b], rk[b], kc[:, 1, :], ALU.add).then_inc(s["rk_s"], 1)
            for L in (3, 4):
                rstds(L)
            for n in range(B + 2):
                pool.wait_ge(s["ln_mv"], 5 * B + n + 1)
                pool.tensor_tensor(rstd[:, together(n)], veps[:, together(n)], halfc[:, together(n)], ALU.pow
                                   ).then_inc(s["ln_rstd"], 1)

        @block.tensor
        def _(pe):
            def ln_T(L, b):
                pe.wait_ge(s["ln_y"], nth(L, b))
                for t in range(T):
                    mm = pe.transpose(PS[:, lnbank(L, b), t * P:(t + 1) * P], y[:, b * T + t, :], ident[:])
                mm.then_inc(s["ln_T"], 1)

            pe.wait_ge(s["cst"], 2)
            pe.wait_ge(s["ld_cx"], 16)
            for n in range(NT):
                mm = pe.transpose(PS[:, 2 + n // 4, (n % 4) * P:(n % 4 + 1) * P], cx[:, n, :], ident[:])
                if n % 4 == 3:
                    mm.then_inc(s["cxT_p"], 1)
            ln_T(0, 0)
            pe.wait_ge(s["cst_v"], 1)
            pe.wait_ge(s["ld_w0"], 112)
            pe.wait_ge(s["cxT_s"], 2)

            def project(b):
                pe.wait_ge(s["ln_yT"], nth_T(0, b))
                for j in range(NJ):
                    pe.matmul(PS[:, j, 0:S], wqp[:, j, :], yT[:, b, :], start=True, stop=True)
                    pe.matmul(PS[:, j, S:2 * S], wkp[:, j, :], cxT[:, b, :], start=True, stop=True
                              ).then_inc(s["q0_p"], 1)
                for t in range(T):
                    mm = pe.matmul(PS[:, 7, t * P:(t + 1) * P], cxT[:, b, t * P:(t + 1) * P], wv[:],
                                   start=True, stop=True)
                mm.then_inc(s["v_p"], 1)

            def raw_scores(n):
                (jp, t), half = divmod(n // 2, T), n % 2
                for jj in range(2):
                    for i in range(2 * half, 2 * half + 2):
                        r = slice(32 * i, 32 * (i + 1))
                        j = 2 * jp + jj
                        mm = pe.matmul(PS[:, 2 * (n % 2) + i % 2, jj * S:(jj + 1) * S],
                                       qk[r, j, 0, t * P:(t + 1) * P], qk[r, j, 1, :], start=True, stop=True)
                mm.then_inc(s["s_p"], 1)

            def turn_maxima(b, jp, bank):
                pe.wait_ge(s["mn_s"], 2 * b + jp + 1)
                for t in range(T):
                    mm = pe.transpose(PS[:, bank, t * P:(t + 1) * P], mneg[:, jp, t, :], ident[:])
                mm.then_inc(s["qm_p"], 1)

            def shifted_scores(b, u):
                jp, t = divmod(u, T)
                at_ = 4 * (1 - u % 2)
                for jj in range(2):
                    if u == 0 and jj:
                        turn_maxima(b, 1, 0)
                    j = 2 * jp + jj
                    for i in range(NI):
                        r8 = slice(32 * i, 32 * i + 2 * NJ)
                        pe.matmul(PS[:, at_ + i, jj * S:(jj + 1) * S], sel[r8, j, :], mT[r8, jp, :],
                                  start=True, stop=False)
                    for i in range(NI):
                        r = slice(32 * i, 32 * (i + 1))
                        mm = pe.matmul(PS[:, at_ + i, jj * S:(jj + 1) * S], qk[r, j, 1, t * P:(t + 1) * P],
                                       qk[r, j, 0, :], start=False, stop=True)
                mm.then_inc(s["st_p"], 1)

            def weigh(b, jp):
                for jj in range(2):
                    for kt in range(T):
                        for i in range(NI):
                            h = (2 * jp + jj) * NI + i
                            mm = pe.matmul(PS[32 * i:32 * (i + 1), 4 + jp, jj * S:(jj + 1) * S], vaug[:, kt, h, :],
                                           pT[:, kt, h, :], start=(kt == 0), stop=(kt == T - 1))
                mm.then_inc(s["pv_p"], 1)

            def back(b):
                pe.wait_ge(s["uT_s"], 2 * (b + 1))
                for t in range(T):
                    for j in range(NJ):
                        mm = pe.transpose(PS[:, 4 + t, j * P:(j + 1) * P], uT[:, j, t * P:(t + 1) * P], ident[:])
                mm.then_inc(s["un_p"], 1)

            def turn(b):
                pe.wait_ge(s["o_n"], b + 1)
                for t in range(T):
                    mm = pe.transpose(PS[:, 5, t * P:(t + 1) * P], o[:, t, :], ident[:])
                mm.then_inc(s["oT_p"], 1)

            def finish(b):
                pe.wait_ge(s["oT_s"], b + 1)
                for t in range(T):
                    c = slice(t * P, (t + 1) * P)
                    pe.matmul(PS[:, 6, c], oT[:, c], wo[:], start=True, stop=False)
                    mm = pe.matmul(PS[:, 6, c], ones[0:1, :], rows[0:1, 0, :], start=False, stop=True)
                mm.then_inc(s["at_p"], 1)

            def adapt(b):
                pe.wait_ge(s["ln_yT"], nth_T(1, b))
                for t in range(T):
                    c = slice(S + t * D, S + (t + 1) * D)
                    pe.matmul(PS[:, 6, c], yT[:, b, t * P:(t + 1) * P], weffT[:], start=True, stop=False)
                    mm = pe.matmul(PS[:, 6, c], wrow[:], adb[:], start=False, stop=True)
                mm.then_inc(s["f0_p"], 1)

            def distances(b):
                pe.wait_ge(s["ln_yT"], nth_T(2, b))
                q = slice(b * LANES, (b + 1) * LANES)
                for c in range(W):
                    pe.matmul(PS[q, c // 2, (c % 2) * S:(c % 2 + 1) * S], yT[:, b, c:S:W], cxT[:, b, :],
                              start=True, stop=True)
                pe.matmul(PS[q, 7, 0:S], ones[:, 0:LANES], sqc[:, b, :], start=True, stop=True)
                pe.wait_ge(s["sq_s"], b + 1)
                for c in range(W):
                    mm = pe.matmul(PS[q, 7, S + c:S + c + 1], sq[:, c:S:W], ones[:, 0:1], start=True, stop=True)
                mm.then_inc(s["aabb_p"], 1)

            project(0)
            for b in range(B):
                pe.wait_ge(s["q0_s"], NJ * (b + 1))
                for n in range(8):
                    if b and n == 2:
                        back(b - 1)
                    if b and n == 3:
                        turn(b - 1)
                    if b and n == 4:
                        finish(b - 1)
                    if n == 5:
                        pe.wait_ge(s["v_s"], b + 1)
                        turn_maxima(b, 0, 7)
                    if n >= 2:
                        pe.wait_ge(s["s_m"], 8 * b + n - 1)
                    raw_scores(n)
                if b:
                    pe.wait_ge(s["x0"], b)
                for u in range(4):
                    if u < 2:
                        pe.wait_ge(s["qm_s"], 2 * b + u + 1)
                    else:
                        pe.wait_ge(s["st_e"], 4 * b + u - 1)
                    shifted_scores(b, u)
                pe.wait_ge(s["st_e"], 4 * b + 3)
                if b + 1 < B:
                    ln_T(0, b + 1)
                if b:
                    ln_T(1, b - 1)
                weigh(b, 0)
                if b:
                    adapt(b - 1)
                else:
                    pe.wait_ge(s["weff_s"], 1)
                    pe.transpose(PS[:, 6, 0:P], weff[:], ident[:]).then_inc(s["weffT_p"], 1)
                pe.wait_ge(s["st_e"], 4 * b + 4)
                if b + 1 < B:
                    project(b + 1)
                weigh(b, 1)
                if b:
                    pe.wait_ge(s["x1"], b)
                    ln_T(2, b - 1)
                else:
                    pe.wait_ge(s["weffT_s"], 1)
            back(B - 1)
            pe.wait_ge(s["sqc_s"], 1)
            distances(0)
            turn(B - 1)
            distances(1)
            pe.wait_ge(s["ln_yT"], nth_T(2, B - 2))
            finish(B - 1)
            distances(2)
            pe.wait_ge(s["x0"], B)
            ln_T(1, B - 1)
            adapt(B - 1)
            pe.wait_ge(s["x1"], B)
            ln_T(2, B - 1)
            distances(3)
            pe.wait_ge(s["ld_moe"], 64)
            pe.wait_ge(s["ld_l2"], 64)
            pe.wait_ge(s["aabb_s"], 1)
            pe.wait_ge(s["dsq"], W // 2)
            for e in range(E2):
                mm = pe.transpose(PS[:, 2 + e // 4, (e % 4) * D:(e % 4 + 1) * D], We[:, e, :], ident[:])
            pe.transpose(PS[:, 4, P:P + E1 * CH], b1r[:], ident[0:E1 * CH, 0:E1 * CH])
            pe.transpose(PS[:, 4, 0:E2], wrr[:], ident[0:E2, 0:E2]).then_inc(s["weT_p"], 1)
            pe.wait_ge(s["ld_l3"], 112)
            for n in range(3):
                pe.transpose(PS[:, 5, n * D:(n + 1) * D], w3[:, n, :], ident[:])
            pe.transpose(PS[:, 5, 3 * D:3 * D + CH], f1br[:], ident[0:CH, 0:CH]).then_inc(s["w3T_p"], 1)
            pe.wait_ge(s["fb_s"], 1)
            for c in range(CH):
                pe.transpose(PS[:, 6, c * P:(c + 1) * P], fs[:, c, :], ident[:])
            for c in range(CH):
                mm = pe.transpose(PS[:, 7, c * P:(c + 1) * P], ft[:, c, :], ident[:])
            mm.then_inc(s["fT_p"], 1)
            pe.wait_ge(s["weT_s"], 1)
            pe.wait_ge(s["cl_r"], 16)
            pe.wait_ge(s["cst_v"], 2)
            for t in range(T):
                bank = PS[:, 2 + t, :].bitcast(BF16)
                for c in range(W):
                    mm = pe.transpose(bank[:, c * P:(c + 1) * P], Cl[:, t * P:(t + 1) * P, c], identb[:])
                mm.then_inc(s["clT_p"], 1)
            pe.wait_ge(s["w3T_s"], 1)
            pe.wait_ge(s["fT_s"], 1)
            pe.wait_ge(s["b1_s"], 1)
            for b in range(B):
                if b >= 2:
                    pe.wait_ge(s["kc_s"], b - 1)
                pe.matmul(PS[:, 6 + b % 2, 0:S], w3T[:, 1, :], cxT[:, b, :], start=True, stop=True)
                pe.matmul(PS[:, 6 + b % 2, S:2 * S], w3T[:, 4, :], cxT[:, b, :], start=True, stop=True
                          ).then_inc(s["kc_p"], 1)
                for t in range(T):
                    c = (b % 2 * T + t) * D
                    mm = pe.matmul(PS[:, b // 2, c:c + D], cxT[:, b, t * P:(t + 1) * P], w3T[:, 2, :],
                                   start=True, stop=True)
                mm.then_inc(s["v3_p"], 1)
            pe.wait_ge(s["p_r"], 16)
            pe.wait_ge(s["c3_s"], 1)
            pe.wait_ge(s["w3T_s"], 1)
            pe.wait_ge(s["ct_s"], T)
            for b in range(B):
                for jt in range(T):
                    for n in range(3 * T):
                        t, part = divmod(n, 3)
                        mm = pe.matmul(PS[:, 2 + b, jt * P:(jt + 1) * P], Pi[:, b, t, jt * P:(jt + 1) * P],
                                       c3[:, part, (b * T + t) * D:(b * T + t + 1) * D],
                                       start=(n == 0), stop=(n == 3 * T - 1))
                mm.then_inc(s["ex_p"], 1)
            pe.wait_ge(s["x2"], B)
            pe.wait_ge(s["v3_s"], 2)
            pe.wait_ge(s["kc_s"], B)
            for b in range(B):
                if b:
                    pe.wait_ge(s["b2_s"], b)
                ln_T(3, b)
                pe.wait_ge(s["ln_yT"], nth_T(3, b))

                def up(e):
                    n = E1 * b + e
                    if n >= 2:
                        pe.wait_ge(s["mm1_s"], 2 * (n - 1))
                    for c in range(CH):
                        mm = pe.matmul(PS[:, 2 + 2 * (n % 2) + c // 2, (c % 2) * S:(c % 2 + 1) * S],
                                       w1[:, e, c * P:(c + 1) * P], yT[:, b, :], start=True, stop=True)
                        if c % 2:
                            mm.then_inc(s["mm1_p"], 1)

                def down(e):
                    n = E1 * b + e
                    pe.wait_ge(s["mm1_s"], 2 * (n + 1))
                    if n >= 2:
                        pe.wait_ge(s["mm2_s"], n - 1)
                    for t in range(T):
                        for c in range(CH):
                            mm = pe.matmul(PS[:, 6 + n % 2, t * D:(t + 1) * D], hT[:, CH * (n % 2) + c, t * P:(t + 1) * P],
                                           w2[:, e, c, :], start=(c == 0), stop=(c == CH - 1))
                    mm.then_inc(s["mm2_p"], 1)

                up(0)
                pe.wait_ge(s["wt_s"], b + 1)
                for t in range(T):
                    mm = pe.transpose(PS[0:E1, 1, t * P:(t + 1) * P], wts[:, b % 2, t, :], ident[:])
                mm.then_inc(s["wtT_p"], 1)
                for e in range(1, E1):
                    up(e)
                    if e == 1:
                        pe.wait_ge(s["wtT_s"], b + 1)
                        for t in range(T):
                            mm = pe.matmul(PS[:, 0, t * D:(t + 1) * D], wtsT[:, t * P:(t + 1) * P], b2r[:],
                                           start=True, stop=True)
                        mm.then_inc(s["b2_p"], 1)
                    down(e - 1)
                down(E1 - 1)
            pe.wait_ge(s["weT_s"], 1)
            pe.wait_ge(s["rk_s"], B)
            pe.wait_ge(s["v3_s"], 2)

            def expert(b, k, bank):
                h, t = divmod(k, 2)
                return pe.matmul(PS[:, bank, :], yT[:, b, t * P:(t + 1) * P],
                                 WeT[:, 4 * h:4 * h + 4, :].rearrange("p e d -> p (e d)"), start=True, stop=True)

            for n in range(B + 2):
                ba, br, bf = n, n - 1, n - 2
                do_a, do_r, do_f = ba < B, 0 <= br < B, 0 <= bf
                if do_a:
                    if ba:
                        pe.wait_ge(s["x5"], ba)
                    ln_T(5, ba)
                if do_r:
                    if br:
                        pe.wait_ge(s["x6"], br)
                    ln_T(6, br)
                if do_a:
                    pe.wait_ge(s["ln_yT"], nth_T(5, ba))
                    for t in range(T):
                        c = slice(t * E2, (t + 1) * E2)
                        pe.matmul(PS[:, 1, c], yT[:, ba, t * P:(t + 1) * P], wrT[:], start=True, stop=False)
                        mm = pe.matmul(PS[:, 1, c], ones[0:1, :], brr[:], start=False, stop=True)
                    mm.then_inc(s["lg_p"], 1)
                if do_r:
                    pe.wait_ge(s["ln_yT"], nth_T(6, br))
                    pe.matmul(PS[:, 4, 0:S], w3T[:, 0, :], yT[:, br, :], start=True, stop=True)
                    pe.matmul(PS[:, 4, S:2 * S], w3T[:, 3, :], yT[:, br, :], start=True, stop=True
                              ).then_inc(s["k3_p"], 1)
                if do_f:
                    if bf:
                        pe.wait_ge(s["x7"], bf)
                    ln_T(7, bf)
                if do_a:
                    expert(ba, 0, 0)
                    expert(ba, 1, 2)
                if do_a:
                    pe.wait_ge(s["gm_s"], ba + 1)
                    for t in range(T):
                        mm = pe.transpose(PS[0:E2, 1, t * P:(t + 1) * P], gm[:, t, :], ident[:])
                    mm.then_inc(s["gmT_p"], 1)
                    expert(ba, 2, 3).then_inc(s["e2_p"], 1)
                if do_a:
                    pe.wait_ge(s["gmT_s"], ba + 1)
                    for t in range(T):
                        mm = pe.matmul(PS[:, 1, t * D:(t + 1) * D], gmT[:, t * P:(t + 1) * P], ber[:],
                                       start=True, stop=True)
                    mm.then_inc(s["eb_p"], 1)
                if do_r:
                    pe.wait_ge(s["k3_s"], br + 1)
                    for t in range(T):
                        mm = pe.matmul(PS[:, 4, t * S:(t + 1) * S], rk[br][:, t * P:(t + 1) * P], rq,
                                       start=True, stop=True)
                    mm.then_inc(s["rt_p"], 1)
                if do_f:
                    pe.wait_ge(s["ln_yT"], nth_T(7, bf))
                    for c in range(CH):
                        mm = pe.matmul(PS[:, 6 + c // 2, (c % 2) * S:(c % 2 + 1) * S], f1T[:, c, :], yT[:, bf, :],
                                       start=True, stop=True)
                        if c % 2:
                            mm.then_inc(s["h3_p"], 1)
                if do_a:
                    pe.wait_ge(s["e2_s"], ba + 1)
                    expert(ba, 3, 0).then_inc(s["e2_p"], 1)
                if do_r:
                    pe.wait_ge(s["rt_s"], br + 1)
                    for t in range(T):
                        for kt in range(t + 1):
                            mm = pe.matmul(PS[:, 5, t * D:(t + 1) * D], ret[:, kt, t * P:(t + 1) * P],
                                           v3[:, br, kt, :], start=(kt == 0), stop=(kt == t))
                    mm.then_inc(s["ro_p"], 1)
                if do_f:
                    pe.wait_ge(s["h3_s"], 2 * (bf + 1))
                    for t in range(T):
                        c_ = slice(t * D, (t + 1) * D)
                        for c in range(CH):
                            pe.matmul(PS[:, 6, c_], hg[:, c, t * P:(t + 1) * P], f2T[:, c, :],
                                      start=(c == 0), stop=False)
                        mm = pe.matmul(PS[:, 6, c_], ones[0:1, :], rows[0:1, 1, :], start=False, stop=True)
                    mm.then_inc(s["f3_p"], 1)

        @block.scalar
        def _(act):
            def copy(out_, in_):
                return act.activation(out_, in_, ACT.Copy)

            def ln_yT(L, b):
                act.wait_ge(s["ln_T"], nth_T(L, b))
                copy(yT[:, b, :], PS[:, lnbank(L, b), 0:S]).then_inc(s["ln_yT"], 1)

            for n in range(2):
                act.wait_ge(s["cxT_p"], n + 1)
                copy(cxT[:, 2 * n:2 * n + 2, :].rearrange("p b s -> p (b s)"), PS[:, 2 + n, :]
                     ).then_inc(s["cxT_s"], 1)
            act.wait_ge(s["ld_gate"], 32)
            act.activation(gate[:], gate[:], ACT.Tanh).then_inc(s["gates"], 1)
            act.wait_ge(s["cst"], 4)

            def projected(b):
                for j in range(NJ):
                    act.wait_ge(s["q0_p"], NJ * b + j + 1)
                    if b:
                        act.wait_ge(s["q0_s"], NJ * (b - 1) + j + 1)
                    copy(qkh[:, j].rearrange("p n s -> p (n s)"), PS[:, j, :]).then_inc(s["q0_h"], 1)

            def values(b):
                act.wait_ge(s["v_p"], b + 1)
                if b:
                    act.wait_ge(s["pv_p"], 2 * b)
                copy(vaug[:, :, :, 0:HD].rearrange("p t h d -> p (t h) d"),
                     PS[:, 7, 0:S].rearrange("p (n d) -> p n d", d=HD)).then_inc(s["v_s"], 1)

            def turned(b, jp):
                act.wait_ge(s["pv_p"], 2 * b + jp + 1)
                if b:
                    act.wait_ge(s["un_p"], b)
                copy(uT[:, 2 * jp:2 * jp + 2, :].rearrange("p j s -> p (j s)"), PS[:, 4 + jp, :]
                     ).then_inc(s["uT_s"], 1)

            def o_T(b):
                act.wait_ge(s["oT_p"], b + 1)
                if b:
                    act.wait_ge(s["at_p"], b)
                copy(oT[:], PS[:, 5, 0:S]).then_inc(s["oT_s"], 1)

            ln_yT(0, 0)
            projected(0)
            values(0)
            for b in range(B):
                for jp in range(2):
                    act.wait_ge(s["qm_p"], 2 * b + jp + 1)
                    copy(mTh[:, jp, :], PS[:, (7, 0)[jp], 0:S]).then_inc(s["qm_h"], 1)
                for u in range(4):
                    jp, t = divmod(u, T)
                    at_ = 4 * (1 - u % 2)
                    act.wait_ge(s["st_p"], 4 * b + u + 1)
                    act.activation(pT[:, t, 2 * NI * jp:2 * NI * (jp + 1), :].rearrange("p (j i) q -> p i j q", j=2),
                                   PS[:, at_:at_ + 4, :].rearrange("p i (j q) -> p i j q", j=2),
                                   ACT.Exp, scale=HD ** -0.5).then_inc(s["st_e"], 1)
                if b + 1 < B:
                    ln_yT(0, b + 1)
                if b:
                    ln_yT(1, b - 1)
                else:
                    turned(b, 0)
                    act.wait_ge(s["weffT_p"], 1)
                    copy(weffT[:], PS[:, 6, 0:P]).then_inc(s["weffT_s"], 1)
                if b:
                    turned(b, 0)
                if b + 1 < B:
                    projected(b + 1)
                turned(b, 1)
                if b + 1 < B:
                    values(b + 1)
                if b:
                    ln_yT(2, b - 1)
                o_T(b)
            ln_yT(1, B - 1)
            ln_yT(2, B - 1)
            for c in range(W):
                act.wait_ge(s["dsq"], c // 2 + 1)
                act.activation(Dun[:, LAGMAX:LAGMAX + S, c + 1], dsum[:, c, :], ACT.Sqrt).then_inc(s["d_s"], 1)
            act.wait_ge(s["weT_p"], 1)
            copy(b1c[:], PS[:, 4, P:P + E1 * CH]).then_inc(s["b1_s"], 1)
            copy(WeT[:].rearrange("p e d -> p (e d)"), PS[:, 2:4, :].rearrange("p a n -> p (a n)"))
            copy(wrT[:], PS[:, 4, 0:E2]).then_inc(s["weT_s"], 1)
            act.wait_ge(s["w3T_p"], 1)
            copy(w3T[:, 0:3, :].rearrange("p a n -> p (a n)"), PS[:, 5, 0:3 * D])
            copy(f1bc[:], PS[:, 5, 3 * D:3 * D + CH])
            for n in range(2):
                pv = PS[:, 5, n * D:(n + 1) * D].rearrange("p (m two) -> p m two", two=2)
                wv_ = w3T[:, 3 + n, :].rearrange("p (m two) -> p m two", two=2)
                act.activation(wv_[:, :, 0], pv[:, :, 1], ACT.Copy, scale=-1.0)
                last = copy(wv_[:, :, 1], pv[:, :, 0])
            last.then_inc(s["w3T_s"], 1)
            act.wait_ge(s["fT_p"], 1)
            copy(f1T[:].rearrange("p c n -> p (c n)"), PS[:, 6, :])
            copy(f2T[:].rearrange("p c n -> p (c n)"), PS[:, 7, :]).then_inc(s["fT_s"], 1)
            for t in range(T):
                act.wait_ge(s["clT_p"], t + 1)
                copy(CT[:, :, t, :].rearrange("p b (k c) -> p b k c", c=W),
                     PS[:, 2 + t, :].bitcast(BF16).rearrange("p (c b k) -> p b k c", c=W, b=B)
                     ).then_inc(s["ct_s"], 1)
            for b in range(B):
                act.wait_ge(s["kc_p"], b + 1)
                if b:
                    act.wait_ge(s["rk_s"], b)
                copy(ft[:].rearrange("p c d -> p (c d)"), PS[:, 6 + b % 2, :]).then_inc(s["kc_s"], 1)
                if b % 2:
                    act.wait_ge(s["v3_p"], b + 1)
                    copy(v3[:, b - 1:b + 1].rearrange("p b t d -> p (b t d)"), PS[:, b // 2, :]
                         ).then_inc(s["v3_s"], 1)

            def head_exp(b):
                act.wait_ge(s["sc_s"], b + 1)
                act.activation(sc2[:], sc2[:], ACT.Exp).then_inc(s["sc_e"], 1)

            for b in range(B):
                ln_yT(3, b)
                for e in range(E1):
                    if e == 1:
                        act.wait_ge(s["wtT_p"], b + 1)
                        if b:
                            act.wait_ge(s["b2_p"], b)
                        copy(wtsT[:], PS[0:E1, 1, 0:S]).then_inc(s["wtT_s"], 1)
                    n = E1 * b + e
                    for c in range(CH):
                        act.wait_ge(s["mm1_p"], 2 * n + c // 2 + 1)
                        if n >= 2 and c == 0:
                            act.wait_ge(s["mm2_p"], n - 1)
                        last = act.activation(hT[:, CH * (n % 2) + c, :],
                                              PS[:, 2 + 2 * (n % 2) + c // 2, (c % 2) * S:(c % 2 + 1) * S],
                                              ACT.Relu, bias=b1c[:, e * CH + c:e * CH + c + 1])
                        if c % 2:
                            last.then_inc(s["mm1_s"], 1)
                    if b and e == 5:
                        head_exp(b - 1)
            for n in range(B + 2):
                ba, br, bf = n, n - 1, n - 2
                do_a, do_r, do_f = ba < B, 0 <= br < B, 0 <= bf
                if do_a:
                    ln_yT(5, ba)
                if do_r:
                    ln_yT(6, br)
                if do_a:
                    act.wait_ge(s["lg_s"], ba + 1)
                    act.activation(lg[:], lg[:], ACT.Exp).then_inc(s["lg_e"], 1)
                if do_f:
                    ln_yT(7, bf)
                if do_a:
                    act.wait_ge(s["gmT_p"], ba + 1)
                    copy(gmT[:], PS[0:E2, 1, 0:S]).then_inc(s["gmT_s"], 1)
                if do_f:
                    act.activation(warm[:, 2 * n:2 * n + 1], ones[:, 0:1], ACT.Gelu)
                if n == 1:
                    head_exp(B - 1)
                if do_f:
                    if bf:
                        act.wait_ge(s["f3_p"], bf)
                    for c in range(CH):
                        act.wait_ge(s["h3_p"], 2 * bf + c // 2 + 1)
                        last = act.activation(hg[:, c, :], PS[:, 6 + c // 2, (c % 2) * S:(c % 2 + 1) * S], ACT.Gelu,
                                              bias=f1bc[:, c:c + 1])
                        if c % 2:
                            last.then_inc(s["h3_s"], 1)
                    if n + 1 < B:
                        act.activation(warm[:, 2 * n + 1:2 * n + 2], ones[:, 0:1], ACT.Exp)

        @block.vector
        def _(v):
            own = Steps(v, s["own_dve"])

            def stats(L, b):
                if L:
                    v.wait_ge(s[f"x{L - 1}"], b + 1)
                for t in range(T):
                    own(v.bn_stats(st6[:, b * T + t, :], x[:, b * T + t, :]))
                own.settle()
                for t in range(T):
                    own(v.bn_aggr(mv[:, b * T + t, :], st6[:, b * T + t, :]))
                own.settle()
                v.tensor_scalar(veps[:, tiles(b)], mv[:, tiles(b), 1], EPS, None, ALU.add
                                ).then_inc(s["ln_mv"], 1)

            def norm(L, b):
                v.wait_ge(s["ln_rstd"], nth(L, b) if L < 5 else 5 * B + (b + L - 5) + 1)
                for t in range(T):
                    n = b * T + t
                    ins = v.tensor_scalar(y[:, n, :], x[:, n, :], mv[:, n, 0:1], rstd[:, n:n + 1],
                                          ALU.subtract, ALU.mult)
                ins.then_inc(s["ln_y"], 1)

            def add(L, b, src, g):
                v.scalar_tensor_tensor(out=x[:, tiles(b), :].rearrange("p t d -> p (t d)"), in0=src,
                                       scalar=gate[:, g:g + 1],
                                       in1=x[:, tiles(b), :].rearrange("p t d -> p (t d)"),
                                       op0=ALU.mult, op1=ALU.add).then_inc(s[f"x{L}"], 1)

            v.wait_ge(s["ld_x"], 16)
            stats(0, 0)
            norm(0, 0)
            v.wait_ge(s["ld_w0"], 112)
            for dst, src in ((wqp, wq), (wkp, wk)):
                for j in range(NJ):
                    own(v.tensor_copy(dst[:, j, :].rearrange("p (i n d) -> p i n d", i=NI, n=4),
                                      src[:, j * NI * HD:(j + 1) * NI * HD].rearrange("p (i d) -> p i d", i=NI)
                                      .unsqueeze(2).broadcast_to([P, NI, 4, HD])))
            own(v.tensor_copy(sel[:], selc[:].unsqueeze(2).broadcast_to([P, NJ, P])))
            own.settle()
            v.sem_inc(s["cst_v"], 1)

            def attended(b):
                v.wait_ge(s["un_p"], b + 1)
                pv = PS[:, 4:4 + T, :].rearrange("p t (n c) -> p (t n) c", c=32)
                own(v.reciprocal(rden[:], pv[:, :, HD]))
                own.settle()
                if b:
                    v.wait_ge(s["oT_p"], b)
                v.tensor_tensor(o[:].rearrange("p t (h d) -> p (t h) d", d=HD), pv[:, :, 0:HD],
                                rden[:].unsqueeze(2).broadcast_to([P, T * HEADS, HD]), ALU.mult
                                ).then_inc(s["o_n"], 1)

            def projected_out(b):
                v.wait_ge(s["at_p"], b + 1)
                v.wait_ge(s["gates"], 1)
                add(0, b, PS[:, 6, 0:S], 0)

            def maxima(b, n):
                (jp, t), half = divmod(n // 2, T), n % 2
                v.wait_ge(s["s_p"], 8 * b + n + 1)
                if b and n == 0:
                    v.wait_ge(s["qm_p"], 2 * b)
                at_ = 2 * (n % 2)
                v.tensor_reduce(mneg[:, jp, t, :].rearrange("p (i c) -> p i c", i=NI)[:, 2 * half:2 * half + 2,
                                                                                 4 * jp:4 * jp + 4:2],
                                PS[:, at_:at_ + 2, :].rearrange("p i (j k) -> p i j k", j=2), AX, ALU.max,
                                negate=True).then_inc(s["s_m"], 1)

            def split_maxima(b, jp):
                v.wait_ge(s["qm_h"], 2 * b + jp + 1)
                v.scalar_tensor_tensor(out=mT[:, jp, :], in0=mTh[:, jp, :].bitcast(F32), scalar=spl[:, 2:3],
                                       in1=PS[:, (7, 0)[jp], 0:S], op0=ALU.mult, op1=ALU.add
                                       ).then_inc(s["qm_s"], 1)

            def adapted(b):
                v.wait_ge(s["f0_p"], b + 1)
                add(1, b, PS[:, 6, S:2 * S], 4)
                stats(2, b)
                norm(2, b)

            def squares(b):
                v.wait_ge(s["ln_yT"], nth_T(2, b))
                if b:
                    v.wait_ge(s["aabb_p"], b)
                v.tensor_tensor(sq[:], yT[:, b, :], yT[:, b, :], ALU.mult).then_inc(s["sq_s"], 1)

            def binarised():
                v.wait_ge(s["ld_l3"], 112)
                own(v.tensor_reduce(fal[:, 0:CH], f1[:], AX, ALU.add, apply_absolute_value=True))
                own(v.tensor_reduce(fal[:, CH:CH + 1], f2[:], AX, ALU.add, apply_absolute_value=True))
                own.settle()
                own(v.tensor_scalar(fal[:, 0:CH], fal[:, 0:CH], 1.0 / D, None, ALU.mult))
                own(v.tensor_scalar(fal[:, CH:CH + 1], fal[:, CH:CH + 1], 1.0 / FF, None, ALU.mult))
                w2v = f2[:].rearrange("p (c n) -> p c n", c=CH)
                for dst, src in ((fs, f1[:]), (ft, w2v)):
                    own(v.tensor_scalar(dst[:], src, 0.0, None, ALU.is_gt))
                    own(v.tensor_scalar(neg, src, 0.0, None, ALU.is_lt))
                    own.settle()
                    own(v.tensor_tensor(dst[:], dst[:], neg, ALU.subtract))
                    own.settle()
                for c in range(CH):
                    own(v.scalar_tensor_tensor(out=fs[:, c, :], in0=fs[:, c, :], scalar=fal[:, c:c + 1], in1=f1[:, c, :],
                                               op0=ALU.mult, op1=ALU.subtract))
                own(v.scalar_tensor_tensor(out=ft[:].rearrange("p c n -> p (c n)"),
                                           in0=ft[:].rearrange("p c n -> p (c n)"), scalar=fal[:, CH:CH + 1],
                                           in1=f2[:], op0=ALU.mult, op1=ALU.subtract))
                own.settle()
                own(v.tensor_tensor(fs, fs, f1[:], ALU.add))
                own(v.tensor_tensor(ft[:], ft[:], w2v, ALU.add))
                own.settle()
                v.sem_inc(s["fb_s"], 1)

            for b in range(B):
                for j in range(NJ):
                    v.wait_ge(s["q0_h"], NJ * b + j + 1)
                    if b:
                        v.wait_ge(s["st_p"], 4 * b)
                    for n in range(2):
                        ins = v.scalar_tensor_tensor(out=qk[:, j, n, :], in0=qkh[:, j, n, :].bitcast(F32),
                                                     scalar=spl[:, n:n + 1], in1=PS[:, j, n * S:(n + 1) * S],
                                                     op0=ALU.mult, op1=ALU.add)
                    ins.then_inc(s["q0_s"], 1)
                for n in range(8):
                    if b and n == 1:
                        attended(b - 1)
                    if n == 6:
                        split_maxima(b, 0)
                        if b:
                            projected_out(b - 1)
                    maxima(b, n)
                    if n % 4 == 3:
                        v.wait_ge(s["s_m"], 8 * b + n + 1)
                        mp = mneg[:, n // 4].rearrange("p t (i c) -> p (t i) c", i=NI)
                        v.tensor_copy(mp[:, :, 1:2 * NJ:2], mp[:, :, 0:2 * NJ:2]).then_inc(s["mn_s"], 1)
                split_maxima(b, 1)
                if b:
                    stats(1, b - 1)
                    norm(1, b - 1)
                    if b == 2:
                        binarised()
                    adapted(b - 1)
                else:
                    for later in range(1, B):
                        stats(0, later)
                    for later in range(1, B):
                        norm(0, later)
                    v.wait_ge(s["ld_ads"], 32 * KA)
                    v.wait_ge(s["ld_mix"], 32)
                    own(v.tensor_scalar(weff[:], ads[:, 0, :], wB[:, 0:1], None, ALU.mult))
                    own(v.tensor_scalar(wrow[:], ones[0:KA, :], wc[:, 0:1], None, ALU.mult))
                    for k in range(1, KA):
                        own.settle()
                        own(v.scalar_tensor_tensor(out=weff[:], in0=ads[:, k, :], scalar=wB[:, k:k + 1],
                                                   in1=weff[:], op0=ALU.mult, op1=ALU.add))
                    own.settle()
                    v.sem_inc(s["weff_s"], 1)
                    v.wait_ge(s["cst"], 7)
                    v.tensor_copy(identb[:], ident[:]).then_inc(s["cst_v"], 1)
                    v.tensor_copy(iot[:], ioti[:]).then_inc(s["cst_v"], 1)
                    v.tensor_copy(thr[:], thri[:]).then_inc(s["cst_v"], 1)
                    v.tensor_copy(modt[:].rearrange("p a b -> p (a b)"), modi[:]).then_inc(s["cst_v"], 1)
                    v.wait_ge(s["cst_v"], 5)
                    own(v.tensor_copy(iotr[:], iot[:, 1:S + 1].unsqueeze(1).broadcast_to([P, R, S])))
            v.wait_ge(s["cxT_s"], 2)
            v.wait_ge(s["c3_s"], 1)
            cf = cxT[:].rearrange("p b s -> p (b s)")
            v.tensor_tensor(sqc.rearrange("p b s -> p (b s)"), cf, cf, ALU.mult).then_inc(s["sqc_s"], 1)
            squares(0)
            attended(B - 1)
            squares(1)
            projected_out(B - 1)
            stats(1, B - 1)
            norm(1, B - 1)
            squares(2)
            adapted(B - 1)
            squares(3)
            v.wait_ge(s["aabb_p"], B)
            own(v.tensor_copy(aab[:], PS[:, 7, 0:S]))
            own(v.tensor_copy(bbk[:], PS[:, 7, S:S + W]))
            own.settle()
            v.sem_inc(s["aabb_s"], 1)
            for c in range(W):
                own(v.tensor_scalar(dsum[:, c, :], aab[:], bbk[:, c:c + 1], None, ALU.add))
            own.settle()
            pairs = [dsum[:, c:c + 2, :].rearrange("p c s -> p (c s)") for c in range(0, W, 2)]
            for n in range(W // 2 + 1):
                if n < W // 2:
                    own(v.scalar_tensor_tensor(out=pairs[n], in0=PS[:, n, :], scalar=-2.0, in1=pairs[n],
                                               op0=ALU.mult, op1=ALU.add))
                if n:
                    own.settle(1 if n < W // 2 else 0)
                    v.tensor_scalar(pairs[n - 1], pairs[n - 1], 0.0, None, ALU.max).then_inc(s["dsq"], 1)
            v.wait_ge(s["init_r"], 1)
            n_dp = HALF * 3 * G - 1
            shift = [0] + list(range(LANES - 1))
            own(v.memset(mb[:, 0, 0:1], BIG))
            own.settle()
            with v.Fori(0, ITERS) as it:
                for h in range(2):
                    k = [0]

                    def step(ins):
                        k[0] += 1
                        ins.then_inc(s["own_dp"], 1)

                    def settle(but=0):
                        v.wait_ge(s["own_dp"], (2 * it + h) * n_dp + k[0] - but)

                    v.wait_ge(s[f"d_r{h}"], (it + 1) * 16)
                    v.wait_ge(s["codes"], (2 * it + h) * 2 + 2)
                    for st in range(HALF):
                        r0 = st * G
                        prev = Rw[:, 1 - h, HS, :] if st == 0 else Rw[:, h, r0, :]
                        for g in range(G):
                            if g:
                                prev = Rw[:, h, r0 + g, :]
                            step(v.tensor_tensor(mb[:, g, 1:W1C], prev[:, 0:W], prev[:, 1:W1C], ALU.min))
                            step(v.stream_shuffle(mb[:, 1 - g, 0:1], prev[:, W:W1C], shift))
                            settle(1)
                            ins = v.tensor_tensor_scan(Rw[:, h, r0 + g + 1, :], mb[:, g, :], Dw[:, h, r0 + g, :],
                                                       BIG, ALU.min, ALU.add)
                            if (st + 1) % (HALF // 2) == 0 and g == G - 1:
                                ins.then_inc(s["rows_g"], 1)
                                v.wait_ge(s["rows_g"], (2 * it + h) * 2 + (st + 1) // (HALF // 2))
                            else:
                                step(ins)
                                settle()
                        if st == 0:
                            step(v.tensor_copy(Rw[:, h, 0, :], Rw[:, 1 - h, HS, :]))
                    assert k[0] == n_dp, k[0]
            v.wait_ge(s["cs_r"], 16)
            own(v.tensor_scalar(msk, Cs, -FAR, 1.25 * FAR, ALU.mult, ALU.add))
            own(v.scalar_tensor_tensor(out=xn, in0=Cs, scalar=0.0,
                                       in1=iot[:, 0:S].unsqueeze(1).broadcast_to([P, R, S]),
                                       op0=ALU.is_gt, op1=ALU.add))
            own(v.tensor_scalar(pen, Cs, 0.5, 2 * FAR, ALU.min, ALU.mult))
            own.settle()
            own(v.tensor_tensor_scan(Nc.rearrange("p r j -> p (r j)"), msk.rearrange("p r j -> p (r j)"),
                                     xn.rearrange("p r j -> p (r j)"), 0.0, ALU.max, ALU.min))
            own(v.memset(Gp[:, :, 0:1], 0.0))
            own.settle()
            own(v.tensor_copy(Gp[:, 0, 1:S + 1], Nc[:, 0, :]))
            own.settle()
            for r in range(1, R):
                g0, g1 = (r - 1) % 2, r % 2
                own(v.tensor_tensor(Gx[:], Gp[:, g0, 0:S], pen[:, r, :], ALU.add))
                own.settle()
                own(v.tensor_tensor(Gx[:], Gx[:], Gp[:, g0, 1:S + 1], ALU.min))
                own.settle()
                to = Gb[:] if r == R - 1 else Gp[:, g1, 1:S + 1]
                ins = v.tensor_tensor_scan(to, msk[:, r, :], Gx[:], 0.0, ALU.max, ALU.min)
                if r == R - 1:
                    ins.then_inc(s["g_s"], 1)
                else:
                    own(ins)
                    own.settle()

            def lookup(lanes, at_, table, col, to, n=0):
                own(v.scalar_tensor_tensor(out=junk[0:lanes, n, :], in0=iot[0:lanes, 1:S + 1], scalar=at_[:, col],
                                           in1=table, op0=ALU.is_equal, op1=ALU.mult, accum_out=to))

            v.memset(ech[:, STRIPS - 1:STRIPS], float(S - 1)).then_inc(s["own_dve"], 1)
            own.n += 1
            own.settle()
            own(v.tensor_tensor_scan(Ac.rearrange("p r j -> p (r j)"), msk.rearrange("p r j -> p (r j)"),
                                     iotr[:].rearrange("p r j -> p (r j)"), 0.0, ALU.max, ALU.min))
            own.settle()
            v.wait_ge(s["g_r"], 16)
            for st in range(STRIPS - 1, 0, -1):
                lookup(B, ech, Ge[:, st, :], slice(st, st + 1), ech[:, st - 1:st])
                own.settle()
            v.sem_inc(s["e_s"], 1)
            v.wait_ge(s["e_r"], 16)
            for r in range(R - 1, -1, -1):
                lookup(P, el, Nc[:, r, :], slice(r + 1, r + 2), el[:, r:r + 1], 0)
                own.settle(1)
                lookup(P, el, Ac[:, r, :], slice(r + 1, r + 2), al[:, r:r + 1], 1)
                own(v.tensor_scalar(xn[:, r, :], iot[:, 1:S + 1], el[:, r + 1:r + 2], None, ALU.is_le))
                own.settle(2)
            own.settle()
            for r in range(R):
                own(v.scalar_tensor_tensor(out=Pm[:, r, :], in0=iot[:, 1:S + 1], scalar=al[:, r:r + 1],
                                           in1=xn[:, r, :], op0=ALU.is_ge, op1=ALU.mult))
            own.settle()
            v.sem_inc(s["p_s"], 1)
            for b in range(B):
                v.wait_ge(s["ex_p"], b + 1)
                add(2, b, PS[:, 2 + b, 0:S], 1)
            stats(3, 0)
            norm(3, 0)
            def routes(b):
                v.wait_ge(s["ln_y"], nth(3, b))
                own(v.tensor_tensor(ssum[:, 0, :], y[:, tiles(b), 0], y[:, tiles(b), 1], ALU.add))
                own.settle()
                own(v.tensor_scalar(ssum[:, 1, :], ssum[:, 0, :], -1.0, None, ALU.mult))
                own.settle()
                thb = thr[:].unsqueeze(1).broadcast_to([P, T, 17])
                own(v.tensor_tensor(cmp[:, 0:T, :], thb, ssum[:, 0, :].unsqueeze(2).broadcast_to([P, T, 17]),
                                    ALU.is_le))
                own(v.tensor_tensor(cmp[:, T:2 * T, :], thb, ssum[:, 1, :].unsqueeze(2).broadcast_to([P, T, 17]),
                                    ALU.is_gt))
                own.settle()
                own(v.tensor_reduce(cnt[:].rearrange("p a t -> p (a t)"), cmp[:], AX, ALU.add))
                own.settle()
                own(v.tensor_tensor(cnts[:], cnt[:, 0, :], cnt[:, 1, :], ALU.add))
                own.settle()
                for t in range(T):
                    own(v.tensor_scalar(hit[:, t], modt[:], cnts[:, t:t + 1], None, ALU.is_equal))
                own.settle()
                own(v.tensor_reduce(oh[:].rearrange("p t e -> p (t e)"),
                                    hit[:].rearrange("p t e m -> p (t e) m"), AX, ALU.add))
                own.settle()
                wb = wts[:, b % 2]
                own(v.tensor_tensor(wb, oh[:, :, 0:E1], oh[:, :, 1:E1 + 1], ALU.add))
                own.settle()
                v.tensor_scalar(wb, wb, 0.5, None, ALU.mult).then_inc(s["wt_s"], 1)

            def head_scores(b, qb):
                kk = 4 * (qb + 1)
                prs = [p_[:, 0:4 * kk * HD].rearrange("p (q k d) -> p q k d", q=4, d=HD) for p_ in (prod, prod2)]
                for t in range(T):
                    q4 = y[:, b * T + t, 32 * qb:32 * (qb + 1)].rearrange("p (q d) -> p q d", d=HD)
                    kv = cx[:, b * T + t, 0:kk * HD].rearrange("p (k d) -> p k d", d=HD)
                    own.settle(1)
                    own(v.tensor_tensor(prs[t], q4.unsqueeze(2).broadcast_to([P, 4, kk, HD]),
                                        kv.unsqueeze(1).broadcast_to([P, 4, kk, HD]), ALU.mult))
                for t in range(T):
                    own.settle(1)
                    own(v.tensor_reduce(sc[:, t, 4 * qb:4 * qb + 4, 0:kk], prs[t], AX, ALU.add))

            s2f = sc2[:].rearrange("p t q k -> p (t q) k")
            bc = [P, T * HEADS, HEADS]

            def head_shift(b):
                own.settle()
                for t in range(T):
                    own(v.scalar_tensor_tensor(out=sc2[:, t].rearrange("p q k -> p (q k)"),
                                               in0=sc[:, t].rearrange("p q k -> p (q k)"), scalar=HD ** -0.5,
                                               in1=cmask[:].rearrange("p q k -> p (q k)"),
                                               op0=ALU.mult, op1=ALU.add))
                own.settle()
                own(v.tensor_reduce(mx[:], s2f, AX, ALU.max))
                own.settle()
                v.tensor_tensor(s2f, s2f, mx[:].unsqueeze(2).broadcast_to(bc), ALU.subtract
                                ).then_inc(s["sc_s"], 1)

            def head_weights(b):
                v.wait_ge(s["sc_e"], b + 1)
                own(v.tensor_reduce(sm[:], s2f, AX, ALU.add))
                own.settle()
                own(v.reciprocal(sm[:], sm[:]))
                own.settle()
                own(v.tensor_tensor(s2f, s2f, sm[:].unsqueeze(2).broadcast_to(bc), ALU.mult))
                own.settle()

            def head_values(b, qb):
                kk = 4 * (qb + 1)
                prs = [p_[:, 0:4 * kk * HD].rearrange("p (q d k) -> p q d k", q=4, d=HD) for p_ in (prod, prod2)]
                for t in range(T):
                    kv = cx[:, b * T + t, 0:kk * HD].rearrange("p (k d) -> p d k", d=HD)
                    own.settle(1)
                    own(v.tensor_tensor(prs[t], sc2[:, t, 4 * qb:4 * qb + 4, 0:kk].unsqueeze(2)
                                        .broadcast_to([P, 4, HD, kk]),
                                        kv.unsqueeze(1).broadcast_to([P, 4, HD, kk]), ALU.mult))
                for t in range(T):
                    own.settle(1)
                    own(v.tensor_reduce(acc[:, b % 2, t, 32 * qb:32 * (qb + 1)]
                                        .rearrange("p (q d) -> p q d", d=HD), prs[t], AX, ALU.add))

            def head_add(b):
                own.settle()
                add(4, b, acc[:, b % 2].rearrange("p t d -> p (t d)"), 2)

            v.wait_ge(s["padded"], 3)
            v.wait_ge(s["ld_tab"], 64)
            routes(0)
            v.wait_ge(s["wt_s"], 1)
            for b in range(B):
                v.wait_ge(s["b2_p"], b + 1)
                ab = acc[:, b % 2]
                v.tensor_copy(ab.rearrange("p t d -> p (t d)"), PS[:, 0, 0:S]).then_inc(s["b2_s"], 1)
                if b:
                    norm(4, b - 1)
                    v.wait_ge(s["ln_y"], nth(4, b - 1))
                v.wait_ge(s["b2_s"], b + 1)
                for e in range(E1):
                    if b:
                        for qb in ((0, 1), (2,), (3,))[e] if e < 3 else ():
                            head_scores(b - 1, qb)
                        if e == 3:
                            head_shift(b - 1)
                        if e == 5:
                            head_weights(b - 1)
                        for qb in ((0, 1), (2,), (3,))[e - 5] if e >= 5 else ():
                            head_values(b - 1, qb)
                    if b == 0 and 1 <= e < B:
                        stats(3, e)
                        norm(3, e)
                    if b + 1 < B and e == 4:
                        routes(b + 1)
                    n = E1 * b + e
                    v.wait_ge(s["mm2_p"], n + 1)
                    if n:
                        v.wait_ge(s["mm2_s"], n)
                    for t in range(T):
                        ins = v.scalar_tensor_tensor(out=ab[:, t, :], in0=PS[:, 6 + n % 2, t * D:(t + 1) * D],
                                                     scalar=wts[:, b % 2, t, e:e + 1], in1=ab[:, t, :],
                                                     op0=ALU.mult, op1=ALU.add)
                    ins.then_inc(s["mm2_s"], 1)
                if b:
                    head_add(b - 1)
                v.wait_ge(s["mm2_s"], E1 * (b + 1))
                add(3, b, ab.rearrange("p t d -> p (t d)"), 5)
                stats(4, b)
                if b:
                    v.wait_ge(s["x4"], b)
            norm(4, B - 1)
            v.wait_ge(s["ln_y"], nth(4, B - 1))
            def gate_shift(b):
                v.wait_ge(s["lg_p"], b + 1)
                lp = PS[:, 1, 0:T * E2].rearrange("p (t e) -> p t e", e=E2)
                own(v.tensor_reduce(lmx[:], lp, AX, ALU.max))
                own.settle()
                v.tensor_tensor(lg[:], lp, lmx[:].unsqueeze(2).broadcast_to([P, T, E2]), ALU.subtract
                                ).then_inc(s["lg_s"], 1)

            def gates_open(b):
                v.wait_ge(s["lg_e"], b + 1)
                own(v.tensor_reduce(lsm[:], lg[:], AX, ALU.add))
                own.settle()
                own(v.reciprocal(lsm[:], lsm[:]))
                own.settle()
                own(v.tensor_tensor(lg[:], lg[:], lsm[:].unsqueeze(2).broadcast_to([P, T, E2]), ALU.mult))
                own.settle()
                v.tensor_scalar(gm[:], lg[:], 0.5, None, ALU.is_gt).then_inc(s["gm_s"], 1)

            def mix(b, h):
                ab = acc[:, b % 2]
                if h == 0:
                    v.wait_ge(s["gm_s"], b + 1)
                    v.wait_ge(s["eb_p"], b + 1)
                    own(v.tensor_copy(ab.rearrange("p t d -> p (t d)"), PS[:, 1, 0:S]))
                    own.settle()
                v.wait_ge(s["e2_p"], 2 * b + h + 1)
                for e in range(4):
                    for t in range(T):
                        own.settle(1)
                        own(v.scalar_tensor_tensor(out=ab[:, t, :],
                                                   in0=PS[:, ((0, 2), (3, 0))[h][t], e * D:(e + 1) * D],
                                                   scalar=gm[:, t, 4 * h + e:4 * h + e + 1], in1=ab[:, t, :],
                                                   op0=ALU.mult, op1=ALU.add))
                own.settle()
                if h == 0:
                    v.sem_inc(s["e2_s"], 1)
                else:
                    add(5, b, ab.rearrange("p t d -> p (t d)"), 6)

            def rotate(b):
                v.wait_ge(s["k3_p"], b + 1)
                own(v.tensor_tensor(rq, PS[:, 4, 0:S], xcos[:, 0, :], ALU.mult))
                own(v.tensor_tensor(rtmp, PS[:, 4, S:2 * S], xsin[:, 0, :], ALU.mult))
                own.settle()
                v.tensor_tensor(rq, rq, rtmp, ALU.add).then_inc(s["k3_s"], 1)

            def decayed(b):
                v.wait_ge(s["rt_p"], b + 1)
                for t in range(T):
                    ins = v.tensor_tensor(ret[:, t, :], PS[:, 4, t * S:(t + 1) * S], decay[:, t, :], ALU.mult)
                ins.then_inc(s["rt_s"], 1)

            for n in range(B + 2):
                ba, br, bf = n, n - 1, n - 2
                do_a, do_r, do_f = ba < B, 0 <= br < B, 0 <= bf
                now = [(L, b) for L, b in PIPE if b + L - 5 == n]
                for L, b in now:
                    v.wait_ge(s[f"x{L - 1}"], b + 1)
                    for t in range(T):
                        own(v.bn_stats(st6[:, b * T + t, :], x[:, b * T + t, :]))
                own.settle()
                for L, b in now:
                    for t in range(T):
                        own(v.bn_aggr(mv[:, b * T + t, :], st6[:, b * T + t, :]))
                own.settle()
                v.tensor_scalar(veps[:, together(n)], mv[:, together(n), 1], EPS, None, ALU.add
                                ).then_inc(s["ln_mv"], 1)
                if n < 2:
                    head_scores(B - 1, 2 * n)
                for L, b in now:
                    norm(L, b)
                if n < 2:
                    head_scores(B - 1, 2 * n + 1)
                elif n == 2:
                    head_values(B - 1, 0)
                if do_a:
                    gate_shift(ba)
                if n == 1:
                    head_shift(B - 1)
                if do_a:
                    gates_open(ba)
                if n == 2:
                    head_values(B - 1, 1)
                if do_r:
                    rotate(br)
                if do_a:
                    mix(ba, 0)
                if do_r:
                    decayed(br)
                if n == 2:
                    head_values(B - 1, 2)
                if do_a:
                    mix(ba, 1)
                if n == 1:
                    head_weights(B - 1)
                if n == 2:
                    head_values(B - 1, 3)
                    head_add(B - 1)
                if do_r:
                    v.wait_ge(s["ro_p"], br + 1)
                    add(6, br, PS[:, 5, 0:S], 3)
                if do_f:
                    v.wait_ge(s["f3_p"], bf + 1)
                    add(7, bf, PS[:, 6, 0:S], 7)


_INS = ["x", "ctx_1024", "g_xattn", "g_ffn", "L0_xattn_W_q", "L0_xattn_W_k", "L0_xattn_W_v", "L0_xattn_W_o",
        "L0_xattn_b_o", "L0_ffn_W", "L0_ffn_b", "L0_ffn_ids", "L0_ffn_weights", "L1_ffn_W1", "L1_ffn_b1",
        "L1_ffn_W2", "L1_ffn_b2", "L2_ffn_Wr", "L2_ffn_br", "L2_ffn_We", "L2_ffn_be", "L3_xattn_Wq",
        "L3_xattn_Wk", "L3_xattn_Wv", "L3_ffn_w1", "L3_ffn_b1", "L3_ffn_w2", "L3_ffn_b2"]


def tables():
    f = np.float32
    base = (np.arange(0, D, 2, dtype=f) + f(0.4 * D)) / f(1.4 * D)
    pos = np.arange(0, S, dtype=f)
    scale = (base[None, :] ** (pos[:, None] / f(512.0))).astype(f)
    freqs = (f(1.0) / f(10000.0) ** (np.arange(D // 2, dtype=f) / f(D // 2))).astype(f)
    arg = (pos[:, None] * freqs[None, :]).astype(f)
    sin, cos = np.sin(arg), np.cos(arg)
    both = lambda m: np.repeat(m, 2, axis=-1).T
    inv = f(1.0) / scale
    t_cos = np.stack([both(cos * scale), both(cos * inv)], 1).astype(f)
    t_sin = np.stack([both(sin * scale), both(sin * inv)], 1).astype(f)
    q, k = np.arange(S)[None, :], np.arange(S)[:, None]
    decay = np.where(q >= k, np.float64(0.96875) ** np.maximum(q - k, 0), 0.0).astype(f)
    decay = decay.reshape(T, P, S).transpose(1, 0, 2)
    causal = np.where(np.tril(np.ones((HEADS, HEADS), bool)), 0.0, NEG).astype(f)
    causal = np.broadcast_to(causal, (P, HEADS, HEADS))
    p = np.arange(P)
    split = -np.stack([p // HD % 2, p // (2 * HD) % 2, p % 2], 1).astype(f)
    sel = (p[:, None] % 32 // 2 == np.arange(NJ)[None, :]).astype(f)
    return {"t_split": split, "t_sel": sel, "t_cos": t_cos, "t_sin": t_sin, "t_decay": decay, "t_causal": causal}


def kernel(**inputs):
    import numpy as _np
    import concourse.bacc as _bacc
    from concourse import mybir as _mybir
    from concourse.bass_utils import run_bass_kernel_spmd as _run

    nc = _bacc.Bacc("TRN2", target_bir_lowering=False, num_devices=1)
    arrays, args = {}, {}
    data = {n: inputs[n] for n in _INS}
    data.update(tables())
    for name, val in data.items():
        arr = _np.ascontiguousarray(val)
        arrays[f"in_{name}"] = arr
        args[name] = nc.dram_tensor(f"in_{name}", arr.shape, _mybir.dt.from_np(arr.dtype), kind="ExternalInput").ap()
    out = nc.dram_tensor("out_0", (B, S, D), _mybir.dt.float32, kind="ExternalOutput").ap()
    build(nc, args, out)
    r = _run(nc, [arrays], core_ids=[0])
    return r.results[0]["out_0"]
```
